# Optimizing a Trainium2 kernel written in Bass

```python
import numpy as np
import jax
import jax.numpy as jnp

def _softmax(x, axis=-1):
    return jax.nn.softmax(x, axis=axis)

def _gelu(x):
    return jax.nn.gelu(x, approximate=True)

def _silu(x):
    return jax.nn.silu(x)

def _sigmoid(x):
    return jax.nn.sigmoid(x)

def _layernorm(x, axis=-1, eps=1e-05):
    m = jnp.mean(x, axis=axis, keepdims=True)
    v = jnp.var(x, axis=axis, keepdims=True)
    return (x - m) / jnp.sqrt(v + eps)

def _scatter_add(tgt, idx, src, axis=0):
    return tgt.at[idx].add(src)

def _segment_sum(src, seg, n):
    return jax.ops.segment_sum(src, seg, n)
kernel_name = 'mk_hybrid_d1_jaxref_r4_e8342e'

def setup_inputs(seed: int=0):
    np.random.seed(seed)
    _w = jnp.asarray

    def _L0_attn_a_setup():
        import jax, jax.numpy as jnp
        import numpy as np
        EMBED_DIM = 512
        NUM_HEADS = 16
        HEAD_DIM = EMBED_DIM // NUM_HEADS
        WINDOW = 128

        def _sliding_window_attn(q, k, v, window):
            B, H, S, d = q.shape
            C = window
            nc = S // C
            qc = q.reshape(B, H, nc, C, d)

            def two_chunks(t):
                tc = t.reshape(B, H, nc, C, d)
                prev = jnp.pad(tc[:, :, :-1], ((0, 0), (0, 0), (1, 0), (0, 0), (0, 0)))
                return jnp.concatenate([prev, tc], axis=3)
            kc = two_chunks(k)
            vc = two_chunks(v)
            scale = 1.0 / np.sqrt(d).astype(np.float32)
            scores = jnp.einsum('bhnid,bhnjd->bhnij', qc, kc) * scale
            i = jnp.arange(C)[:, None]
            j = jnp.arange(2 * C)[None, :]
            band = (j >= i) & (j <= i + C)
            kv_global = (jnp.arange(nc)[:, None, None] - 1) * C + j[None]
            mask = band[None] & (kv_global >= 0)
            scores = jnp.where(mask[None, None], scores, jnp.finfo(scores.dtype).min)
            probs = jax.nn.softmax(scores, axis=-1)
            out = jnp.einsum('bhnij,bhnjd->bhnid', probs, vc)
            return out.reshape(B, H, S, d)
        key = jax.random.key(seed)
        k1, k2, k3 = jax.random.split(key, 3)
        B, S = (2, 1024)
        x = jax.random.normal(k1, (B, S, EMBED_DIM), dtype=jnp.float32)
        w_qkv = jax.random.normal(k2, (3 * EMBED_DIM, EMBED_DIM), dtype=jnp.float32) * 0.02
        w_out = jax.random.normal(k3, (EMBED_DIM, EMBED_DIM), dtype=jnp.float32) * 0.02
        return {'x': x, 'w_qkv': w_qkv, 'w_out': w_out}
    _L0_attn_a_in = _L0_attn_a_setup()

    def _L0_attn_b_setup():
        import jax, jax.numpy as jnp
        import numpy as np
        D_MODEL = 512
        D_STATE = 128
        D_CONV = 4
        EXPAND = 2
        HEADDIM = 64
        NGROUPS = 1
        D_INNER = EXPAND * D_MODEL
        NHEADS = D_INNER // HEADDIM
        D_XBC = D_INNER + 2 * NGROUPS * D_STATE
        D_IN_PROJ = 2 * D_INNER + 2 * NGROUPS * D_STATE + NHEADS
        BLOCK_LEN = 64

        def _segsum(x):
            T = x.shape[-1]
            xc = jnp.cumsum(x, axis=-1)
            seg = xc[..., :, None] - xc[..., None, :]
            mask = jnp.tril(jnp.ones((T, T), dtype=bool))
            return jnp.where(mask, seg, -jnp.inf)

        def _ssd_scan(X, A, B, C, block_len):
            b, L, h, p = X.shape
            c = L // block_len
            X = X.reshape(b, c, block_len, h, p)
            A = A.reshape(b, c, block_len, h).transpose(0, 3, 1, 2)
            B = B.reshape(b, c, block_len, h, -1)
            C = C.reshape(b, c, block_len, h, -1)
            A_cumsum = jnp.cumsum(A, axis=-1)
            Lmat = jnp.exp(_segsum(A))
            Y_diag = jnp.einsum('bclhn,bcshn,bhcls,bcshp->bclhp', C, B, Lmat, X)
            decay_states = jnp.exp(A_cumsum[:, :, :, -1:] - A_cumsum)
            states = jnp.einsum('bclhn,bhcl,bclhp->bchpn', B, decay_states, X)
            init = jnp.zeros_like(states[:, :1])
            states = jnp.concatenate([init, states], axis=1)
            A_last = jnp.pad(A_cumsum[:, :, :, -1], ((0, 0), (0, 0), (1, 0)))
            decay_chunk = jnp.exp(_segsum(A_last))
            new_states = jnp.einsum('bhzc,bchpn->bzhpn', decay_chunk, states)
            states = new_states[:, 1:]
            state_decay_out = jnp.exp(A_cumsum)
            Y_off = jnp.einsum('bclhn,bchpn,bhcl->bclhp', C, states, state_decay_out)
            return (Y_diag + Y_off).reshape(b, L, h, p)

        def _forward(x, in_proj_w, conv_w, conv_b, A_log, D, dt_bias, norm_w, out_proj_w):
            Bsz, L, _ = x.shape
            proj = x @ in_proj_w.T
            z = proj[:, :, :D_INNER]
            xBC = proj[:, :, D_INNER:D_INNER + D_XBC]
            dt_raw = proj[:, :, D_INNER + D_XBC:]
            xBC_t = xBC.transpose(0, 2, 1)
            conv = jax.lax.conv_general_dilated(xBC_t, conv_w, window_strides=(1,), padding=[(D_CONV - 1, 0)], feature_group_count=D_XBC, dimension_numbers=('NCH', 'OIH', 'NCH'))
            conv = conv + conv_b[None, :, None]
            xBC = jax.nn.silu(conv).transpose(0, 2, 1)
            x_ssm = xBC[:, :, :D_INNER]
            B_param = xBC[:, :, D_INNER:D_INNER + NGROUPS * D_STATE]
            C_param = xBC[:, :, D_INNER + NGROUPS * D_STATE:]
            dt = jax.nn.softplus(dt_raw + dt_bias)
            A = -jnp.exp(A_log)
            x_heads = x_ssm.reshape(Bsz, L, NHEADS, HEADDIM)
            hpg = NHEADS // NGROUPS
            X = x_heads * dt[..., None]
            A_disc = dt * A[None, None, :]
            B_heads = jnp.repeat(B_param.reshape(Bsz, L, NGROUPS, D_STATE), hpg, axis=2)
            C_heads = jnp.repeat(C_param.reshape(Bsz, L, NGROUPS, D_STATE), hpg, axis=2)
            pad_len = (BLOCK_LEN - L % BLOCK_LEN) % BLOCK_LEN
            if pad_len > 0:
                X = jnp.pad(X, ((0, 0), (0, pad_len), (0, 0), (0, 0)))
                A_disc = jnp.pad(A_disc, ((0, 0), (0, pad_len), (0, 0)))
                B_heads = jnp.pad(B_heads, ((0, 0), (0, pad_len), (0, 0), (0, 0)))
                C_heads = jnp.pad(C_heads, ((0, 0), (0, pad_len), (0, 0), (0, 0)))
            Y = _ssd_scan(X, A_disc, B_heads, C_heads, BLOCK_LEN)[:, :L]
            Y = Y + x_heads * D[None, None, :, None]
            y = Y.reshape(Bsz, L, D_INNER)
            y = y * jax.nn.silu(z)
            rms = jnp.sqrt(jnp.mean(y * y, axis=-1, keepdims=True) + 1e-05)
            y = y / rms * norm_w
            return y @ out_proj_w.T
        key = jax.random.key(seed)
        ks = jax.random.split(key, 8)
        x = jax.random.normal(ks[0], (2, 512, D_MODEL), dtype=jnp.float32)
        in_proj_w = jax.random.normal(ks[1], (D_IN_PROJ, D_MODEL), dtype=jnp.float32) * 0.02
        conv_w = jax.random.normal(ks[2], (D_XBC, 1, D_CONV), dtype=jnp.float32) * 0.2
        conv_b = jnp.zeros((D_XBC,), dtype=jnp.float32)
        A_log = jnp.log(jnp.arange(1, NHEADS + 1, dtype=jnp.float32))
        D = jnp.ones((NHEADS,), dtype=jnp.float32)
        dt_bias = jax.random.normal(ks[3], (NHEADS,), dtype=jnp.float32) * 0.1
        norm_w = jnp.ones((D_INNER,), dtype=jnp.float32)
        out_proj_w = jax.random.normal(ks[4], (D_MODEL, D_INNER), dtype=jnp.float32) * 0.02
        return {'x': x, 'in_proj_w': in_proj_w, 'conv_w': conv_w, 'conv_b': conv_b, 'A_log': A_log, 'D': D, 'dt_bias': dt_bias, 'norm_w': norm_w, 'out_proj_w': out_proj_w}
    _L0_attn_b_in = _L0_attn_b_setup()

    def _L0_ffn_setup():
        import jax, jax.numpy as jnp
        import numpy as np
        TOP_K = 2
        key = jax.random.key(seed)
        k1, k2, k3, k4 = jax.random.split(key, 4)
        B, S, H, I, E = (2, 256, 512, 352, 8)
        hidden_states = jax.random.normal(k1, (B, S, H), dtype=jnp.float32)
        gate_w = jax.random.normal(k2, (E, H), dtype=jnp.float32) * (1.0 / np.sqrt(H))
        w1 = jax.random.normal(k3, (E, 2 * I, H), dtype=jnp.float32) * (1.0 / np.sqrt(H))
        w2 = jax.random.normal(k4, (E, H, I), dtype=jnp.float32) * (1.0 / np.sqrt(I))
        return {'hidden_states': hidden_states, 'gate_w': gate_w, 'w1': w1, 'w2': w2}
    _L0_ffn_in = _L0_ffn_setup()
    _d = {'L0_attn_a_x': _L0_attn_a_in['x'], 'L0_attn_a_w_qkv': _L0_attn_a_in['w_qkv'], 'L0_attn_a_w_out': _L0_attn_a_in['w_out'], 'L0_attn_b_in_proj_w': _L0_attn_b_in['in_proj_w'], 'L0_attn_b_conv_w': _L0_attn_b_in['conv_w'], 'L0_attn_b_conv_b': _L0_attn_b_in['conv_b'], 'L0_attn_b_A_log': _L0_attn_b_in['A_log'], 'L0_attn_b_D': _L0_attn_b_in['D'], 'L0_attn_b_dt_bias': _L0_attn_b_in['dt_bias'], 'L0_attn_b_norm_w': _L0_attn_b_in['norm_w'], 'L0_attn_b_out_proj_w': _L0_attn_b_in['out_proj_w'], 'L0_ffn_gate_w': _L0_ffn_in['gate_w'], 'L0_ffn_w1': _L0_ffn_in['w1'], 'L0_ffn_w2': _L0_ffn_in['w2']}
    _x0 = _d['L0_attn_a_x']
    _d['L0_attn_a_x'] = jax.random.normal(jax.random.fold_in(jax.random.key(seed), 1), (2, 1024, 512), dtype=_x0.dtype)
    del _x0
    return _d

def reference(L0_attn_a_x, L0_attn_a_w_qkv, L0_attn_a_w_out, L0_attn_b_in_proj_w, L0_attn_b_conv_w, L0_attn_b_conv_b, L0_attn_b_A_log, L0_attn_b_D, L0_attn_b_dt_bias, L0_attn_b_norm_w, L0_attn_b_out_proj_w, L0_ffn_gate_w, L0_ffn_w1, L0_ffn_w2):

    def _L0_attn_a_ref(x, w_qkv, w_out):
        import jax, jax.numpy as jnp
        import numpy as np
        EMBED_DIM = 512
        NUM_HEADS = 16
        HEAD_DIM = EMBED_DIM // NUM_HEADS
        WINDOW = 128

        def _sliding_window_attn(q, k, v, window):
            B, H, S, d = q.shape
            C = window
            nc = S // C
            qc = q.reshape(B, H, nc, C, d)

            def two_chunks(t):
                tc = t.reshape(B, H, nc, C, d)
                prev = jnp.pad(tc[:, :, :-1], ((0, 0), (0, 0), (1, 0), (0, 0), (0, 0)))
                return jnp.concatenate([prev, tc], axis=3)
            kc = two_chunks(k)
            vc = two_chunks(v)
            scale = 1.0 / np.sqrt(d).astype(np.float32)
            scores = jnp.einsum('bhnid,bhnjd->bhnij', qc, kc) * scale
            i = jnp.arange(C)[:, None]
            j = jnp.arange(2 * C)[None, :]
            band = (j >= i) & (j <= i + C)
            kv_global = (jnp.arange(nc)[:, None, None] - 1) * C + j[None]
            mask = band[None] & (kv_global >= 0)
            scores = jnp.where(mask[None, None], scores, jnp.finfo(scores.dtype).min)
            probs = jax.nn.softmax(scores, axis=-1)
            out = jnp.einsum('bhnij,bhnjd->bhnid', probs, vc)
            return out.reshape(B, H, S, d)
        B, S, E = x.shape
        qkv = jnp.einsum('bse,fe->bsf', x, w_qkv)
        qkv = qkv.reshape(B, S, 3, NUM_HEADS, HEAD_DIM)
        qkv = jnp.transpose(qkv, (2, 0, 3, 1, 4))
        q, k, v = (qkv[0], qkv[1], qkv[2])
        attn = _sliding_window_attn(q, k, v, WINDOW)
        attn = jnp.transpose(attn, (0, 2, 1, 3)).reshape(B, S, E)
        return jnp.einsum('bse,fe->bsf', attn, w_out)

    def _L0_attn_b_ref(x, in_proj_w, conv_w, conv_b, A_log, D, dt_bias, norm_w, out_proj_w):
        import jax, jax.numpy as jnp
        import numpy as np
        D_MODEL = 512
        D_STATE = 128
        D_CONV = 4
        EXPAND = 2
        HEADDIM = 64
        NGROUPS = 1
        D_INNER = EXPAND * D_MODEL
        NHEADS = D_INNER // HEADDIM
        D_XBC = D_INNER + 2 * NGROUPS * D_STATE
        D_IN_PROJ = 2 * D_INNER + 2 * NGROUPS * D_STATE + NHEADS
        BLOCK_LEN = 64

        def _segsum(x):
            T = x.shape[-1]
            xc = jnp.cumsum(x, axis=-1)
            seg = xc[..., :, None] - xc[..., None, :]
            mask = jnp.tril(jnp.ones((T, T), dtype=bool))
            return jnp.where(mask, seg, -jnp.inf)

        def _ssd_scan(X, A, B, C, block_len):
            b, L, h, p = X.shape
            c = L // block_len
            X = X.reshape(b, c, block_len, h, p)
            A = A.reshape(b, c, block_len, h).transpose(0, 3, 1, 2)
            B = B.reshape(b, c, block_len, h, -1)
            C = C.reshape(b, c, block_len, h, -1)
            A_cumsum = jnp.cumsum(A, axis=-1)
            Lmat = jnp.exp(_segsum(A))
            Y_diag = jnp.einsum('bclhn,bcshn,bhcls,bcshp->bclhp', C, B, Lmat, X)
            decay_states = jnp.exp(A_cumsum[:, :, :, -1:] - A_cumsum)
            states = jnp.einsum('bclhn,bhcl,bclhp->bchpn', B, decay_states, X)
            init = jnp.zeros_like(states[:, :1])
            states = jnp.concatenate([init, states], axis=1)
            A_last = jnp.pad(A_cumsum[:, :, :, -1], ((0, 0), (0, 0), (1, 0)))
            decay_chunk = jnp.exp(_segsum(A_last))
            new_states = jnp.einsum('bhzc,bchpn->bzhpn', decay_chunk, states)
            states = new_states[:, 1:]
            state_decay_out = jnp.exp(A_cumsum)
            Y_off = jnp.einsum('bclhn,bchpn,bhcl->bclhp', C, states, state_decay_out)
            return (Y_diag + Y_off).reshape(b, L, h, p)

        def _forward(x, in_proj_w, conv_w, conv_b, A_log, D, dt_bias, norm_w, out_proj_w):
            Bsz, L, _ = x.shape
            proj = x @ in_proj_w.T
            z = proj[:, :, :D_INNER]
            xBC = proj[:, :, D_INNER:D_INNER + D_XBC]
            dt_raw = proj[:, :, D_INNER + D_XBC:]
            xBC_t = xBC.transpose(0, 2, 1)
            conv = jax.lax.conv_general_dilated(xBC_t, conv_w, window_strides=(1,), padding=[(D_CONV - 1, 0)], feature_group_count=D_XBC, dimension_numbers=('NCH', 'OIH', 'NCH'))
            conv = conv + conv_b[None, :, None]
            xBC = jax.nn.silu(conv).transpose(0, 2, 1)
            x_ssm = xBC[:, :, :D_INNER]
            B_param = xBC[:, :, D_INNER:D_INNER + NGROUPS * D_STATE]
            C_param = xBC[:, :, D_INNER + NGROUPS * D_STATE:]
            dt = jax.nn.softplus(dt_raw + dt_bias)
            A = -jnp.exp(A_log)
            x_heads = x_ssm.reshape(Bsz, L, NHEADS, HEADDIM)
            hpg = NHEADS // NGROUPS
            X = x_heads * dt[..., None]
            A_disc = dt * A[None, None, :]
            B_heads = jnp.repeat(B_param.reshape(Bsz, L, NGROUPS, D_STATE), hpg, axis=2)
            C_heads = jnp.repeat(C_param.reshape(Bsz, L, NGROUPS, D_STATE), hpg, axis=2)
            pad_len = (BLOCK_LEN - L % BLOCK_LEN) % BLOCK_LEN
            if pad_len > 0:
                X = jnp.pad(X, ((0, 0), (0, pad_len), (0, 0), (0, 0)))
                A_disc = jnp.pad(A_disc, ((0, 0), (0, pad_len), (0, 0)))
                B_heads = jnp.pad(B_heads, ((0, 0), (0, pad_len), (0, 0), (0, 0)))
                C_heads = jnp.pad(C_heads, ((0, 0), (0, pad_len), (0, 0), (0, 0)))
            Y = _ssd_scan(X, A_disc, B_heads, C_heads, BLOCK_LEN)[:, :L]
            Y = Y + x_heads * D[None, None, :, None]
            y = Y.reshape(Bsz, L, D_INNER)
            y = y * jax.nn.silu(z)
            rms = jnp.sqrt(jnp.mean(y * y, axis=-1, keepdims=True) + 1e-05)
            y = y / rms * norm_w
            return y @ out_proj_w.T
        return _forward(x, in_proj_w, conv_w, conv_b, A_log, D, dt_bias, norm_w, out_proj_w)

    def _L0_ffn_ref(hidden_states, gate_w, w1, w2):
        import jax, jax.numpy as jnp
        import numpy as np
        TOP_K = 2
        B, S, H = hidden_states.shape
        E = gate_w.shape[0]
        T = B * S
        x = hidden_states.reshape(T, H)
        logits = jnp.einsum('th,eh->te', x, gate_w)
        probs = jax.nn.softmax(logits, axis=-1)
        topw, sel = jax.lax.top_k(probs, TOP_K)
        topw = topw / jnp.sum(topw, axis=-1, keepdims=True)
        combine = jnp.zeros((T, E), dtype=x.dtype).at[jnp.arange(T)[:, None], sel].add(topw)
        gate_up = jnp.einsum('th,eoh->eto', x, w1)
        g, u = jnp.split(gate_up, 2, axis=-1)
        act = jax.nn.silu(g) * u
        expert_out = jnp.einsum('eti,ehi->eth', act, w2)
        out = jnp.einsum('eth,te->th', expert_out, combine)
        return out.reshape(B, S, H)
    x = L0_attn_a_x
    x = x + _L0_attn_a_ref(_layernorm(x, axis=-1), L0_attn_a_w_qkv, L0_attn_a_w_out)
    x = x + _L0_ffn_ref(_layernorm(x, axis=-1), L0_ffn_gate_w, L0_ffn_w1, L0_ffn_w2)
    x = x + _L0_attn_b_ref(_layernorm(x, axis=-1), L0_attn_b_in_proj_w, L0_attn_b_conv_w, L0_attn_b_conv_b, L0_attn_b_A_log, L0_attn_b_D, L0_attn_b_dt_bias, L0_attn_b_norm_w, L0_attn_b_out_proj_w)
    x = x + _L0_ffn_ref(_layernorm(x, axis=-1), L0_ffn_gate_w, L0_ffn_w1, L0_ffn_w2)
    return x

_drawn_inputs = setup_inputs


def setup_inputs(seed=0):
    import zlib

    import numpy as np

    out = dict(_drawn_inputs(seed))
    spreads = {'L0_attn_b_conv_b': (0.0, 0.1), 'L0_attn_b_D': (1.0, 0.2), 'L0_attn_b_norm_w': (1.0, 0.2)}
    factors = {'L0_attn_b_dt_bias': 4.359}
    for name, (base, spread) in spreads.items():
        noise = np.random.default_rng([zlib.crc32(name.encode()), seed]).standard_normal(out[name].shape)
        drawn = base * np.exp(spread * noise) if base else spread * noise
        out[name] = jnp.asarray(drawn.astype(out[name].dtype))
    for name, factor in factors.items():
        out[name] = (out[name] * factor).astype(out[name].dtype)
    return out
```

```python
from contextlib import contextmanager
from contextlib import ExitStack

import concourse.bass as bass
from concourse import mybir

F32 = mybir.dt.float32
BF16 = mybir.dt.bfloat16
I32 = mybir.dt.int32
U32 = mybir.dt.uint32
ALU = mybir.AluOpType
ACT = mybir.ActivationFunctionType
AX = mybir.AxisListType

P = 128
BATCH, SEQ, D = 2, 1024, 512
ROWS = BATCH * SEQ
TILES = ROWS // P
TURNS = TILES // 2
TURNS_PER_BATCH = TURNS // BATCH
KD = D // P
EPS = 1e-5
NEG = -1e30

HEADS, HD = 16, 32
HG = P // HD
WIN = P

EXPERTS, TOPK, INTER = 8, 2, 352
KI = -(-INTER // P)
LAST_I = INTER - (KI - 1) * P
SLOTS = -(-(TOPK * ROWS + EXPERTS * (P - 1)) // (2 * P)) * 2
SPARE = P
W1E = KD * 2 * INTER
W2E = KI * D

INNER, STATE, MHEADS, MHD, TAPS = 1024, 128, 16, 64, 4
XBC = INNER + 2 * STATE
CB = XBC // P
KY = INNER // P
WIN_COLS = 2 * INNER + 2 * STATE + MHEADS


class Chain:

    def __init__(self, eng, sem, turn=0, per_turn=0):
        self.eng, self.sem, self.turn, self.per_turn, self.n = eng, sem, turn, per_turn, 0

    def __call__(self, ins):
        self.n += 1
        ins.then_inc(self.sem, 1)
        self.eng.wait_ge(self.sem, self.turn * self.per_turn + self.n)

    def end(self):
        assert self.n == self.per_turn, self.n


def cut(arena, at, *shape):
    n = 1
    for s in shape:
        n *= s
    v = arena[:, at:at + n]
    if len(shape) == 2:
        v = v.rearrange("p (a b) -> p a b", b=shape[1])
    if len(shape) == 3:
        v = v.rearrange("p (a b c) -> p a b c", b=shape[1], c=shape[2])
    return v, at + n


def spread(ap, axis, n):
    v = ap.unsqueeze(axis)
    shape = list(v.shape)
    shape[axis] = n
    return v.broadcast_to(shape)


@contextmanager
def stage_semaphores(nc, tag):
    taken = []

    def sem(name):
        taken.append(nc.alloc_semaphore(name=f"{tag}_{name}"))
        return taken[-1]

    yield sem
    nc.clear_and_free_semaphores(taken)
    nc.all_engine_barrier()


class Core:

    def __init__(self, nc, ctx):
        self.nc, self.ctx = nc, ctx
        self.bank = [ctx.enter_context(nc.psum_tensor(f"bank{i}", [P, 512], F32)) for i in range(8)]

        def sb(name, shape, dt=F32):
            return ctx.enter_context(nc.sbuf_tensor(name, shape, dt))

        self.pool_dma = {tag: [ctx.enter_context(nc.semaphore(f"{tag}_{name}"))
                               for name in ("gathered0", "gathered1", "added")] for tag in ("moe_a", "moe_b")}
        self.ident = sb("ident", [P, P])
        self.identb = sb("identb", [P, P], BF16)
        self.zero = sb("zero", [P, 512])
        self.att_mask = sb("att_mask", [P, 3, 2 * P], BF16)
        self.ssd_mask = sb("ssd_mask", [P, 4, P], BF16)
        self.upto = sb("upto", [P, P])
        self.before = sb("before", [P, P], BF16)
        self.ones = sb("ones", [P, P])
        self.onesb = sb("onesb", [P, P], BF16)
        self.count = sb("count", [P, P])
        self.rowid = sb("rowid", [P, TILES])
        self.spareid = sb("spareid", [P, 1])
        self.mhalf = sb("mhalf", [P, 1])
        self.keep = sb("keep", [P, TURNS_PER_BATCH])
        left = (nc.sbuf_bytes_remaining - 64) // 4 // 8 * 8
        self.arena = sb("arena", [P, left])
        self.left = left
        self.w1_at, self.w2_at = 0, EXPERTS * W1E
        self.work_at = self.w2_at + EXPERTS * W2E
        self.kept_experts = 6
        self.other_at = self.kept_experts * W1E
        self.w1 = self.arena[:, 0:EXPERTS * W1E]
        self.w2 = self.arena[:, self.w2_at:self.work_at]


def make_constants(core, spare_rows):
    nc = core.nc
    with stage_semaphores(nc, "const") as sem, ExitStack() as ctx:
        made, base_made, zeroed = sem("made"), sem("base_made"), sem("spare_zeroed")
        block = ctx.enter_context(nc.Block())

        @block.vector
        def _(dve):
            for ap, value in ((core.zero, 0.0), (core.ident, 0.0), (core.identb, 0.0), (core.ones, 1.0),
                              (core.onesb, 1.0), (core.att_mask, 0.0), (core.ssd_mask, 0.0),
                              (core.mhalf, -0.5), (core.keep, 1.0)):
                last = nc.vector.memset(ap[:], value)
            last.then_inc(base_made, 1)

        @block.gpsimd
        def _(pool):
            g = Chain(pool, made)
            pool.wait_ge(base_made, 1)
            for m in (core.ident, core.identb):
                g(nc.gpsimd.affine_select(out=m[:], in_=m[:], compare_op=ALU.not_equal, fill=1.0, base=0,
                                          pattern=[[-1, P]], channel_multiplier=1))
            g(nc.gpsimd.affine_select(out=core.upto[:], in_=core.ones[:], compare_op=ALU.is_ge, fill=0.0,
                                      base=0, pattern=[[1, P]], channel_multiplier=-1))
            g(nc.gpsimd.affine_select(out=core.before[:], in_=core.onesb[:], compare_op=ALU.is_gt, fill=0.0,
                                      base=0, pattern=[[1, P]], channel_multiplier=-1))
            m = core.ssd_mask
            g(nc.gpsimd.affine_select(out=m[:], in_=m[:], compare_op=ALU.is_ge, fill=NEG, base=0,
                                      pattern=[[0, 4], [1, P]], channel_multiplier=-1))
            for which, own, prev in ((0, 0, None), (1, 0, 1), (2, 1, 0)):
                m = core.att_mask[:, which, own * P:own * P + P]
                g(nc.gpsimd.affine_select(out=m, in_=m, compare_op=ALU.is_ge, fill=NEG, base=0,
                                          pattern=[[-1, P]], channel_multiplier=1))
                if prev is not None:
                    m = core.att_mask[:, which, prev * P:prev * P + P]
                    g(nc.gpsimd.affine_select(out=m, in_=m, compare_op=ALU.is_ge, fill=NEG, base=0,
                                              pattern=[[1, P]], channel_multiplier=-1))
            g(nc.gpsimd.memset(core.att_mask[:, 0, P:2 * P], NEG))
            g(nc.gpsimd.memset(core.keep[:, 0:1], 0.0))
            g(nc.gpsimd.iota(core.count[:], [[1, P]], 0, 0, allow_small_or_imprecise_dtypes=True))
            g(nc.gpsimd.iota(core.rowid[:], [[P, TILES]], 0, 1, allow_small_or_imprecise_dtypes=True))
            g(nc.gpsimd.iota(core.spareid[:], [[0, 1]], ROWS, 1, allow_small_or_imprecise_dtypes=True))

        @block.sync
        def _(sp):
            sp.wait_ge(base_made, 1)
            for rows in spare_rows:
                sp.dma_start(rows, core.zero[:]).then_inc(zeroed, 16)
            sp.wait_ge(zeroed, 16 * len(spare_rows))


def attention(core, x_in, x_out, w_qkv, w_out, w1_dram):
    nc, bank = core.nc, core.bank
    arena, at = core.arena, core.other_at
    wqkv, at = cut(arena, at, KD, 3 * D)
    wo, at = cut(arena, at, KD, D)
    x, at = cut(arena, at, 2, D)
    xn, at = cut(arena, at, D)
    xnT, at = cut(arena, at, KD, P)
    qz, at = cut(arena, at, HG, KD, P)
    kT, at = cut(arena, at, KD, 2, P)
    v, at = cut(arena, at, 2, D)
    probs, at = cut(arena, at, 2, HG, 2 * P)
    probsT, at = cut(arena, at, 2, 4, P)
    o, at = cut(arena, at, D)
    oT, at = cut(arena, at, KD, P)
    xo, at = cut(arena, at, D)
    st, at = cut(arena, at, 6)
    mv, at = cut(arena, at, 2)
    var_eps, at = cut(arena, at, 1)
    rstd, at = cut(arena, at, 1)
    nmax, at = cut(arena, at, HEADS)
    psum_p, at = cut(arena, at, HEADS)
    rinv, at = cut(arena, at, HEADS)
    assert at <= core.left
    score_banks = ((bank[2], bank[3]), (bank[4], bank[5]))
    with stage_semaphores(nc, "att") as sem, ExitStack() as ctx:
        weights_in = [sem(f"w{k}_in") for k in range(2)]
        x_loaded = [sem("x_loaded0"), sem("x_loaded1")]
        experts_in = sem("experts_in")
        chain = sem("dve_chain")
        cleared = sem("cleared")
        var_ready, rstd_ready, xn_ready = sem("var_ready"), sem("rstd_ready"), sem("xn_ready")
        x_turned, xnT_ready = sem("x_turned"), sem("xnT_ready")
        q_made, k_made, v_made = sem("q_made"), sem("k_made"), sem("v_made")
        q_ready, k_ready, v_ready = sem("q_ready"), sem("k_ready"), sem("v_ready")
        scores_made, max_ready, probs_ready = sem("scores_made"), sem("max_ready"), sem("probs_ready")
        probs_turned, probsT_ready, pv_made = sem("probs_turned"), sem("probsT_ready"), sem("pv_made")
        o_ready, o_turned, oT_ready = sem("o_ready"), sem("o_turned"), sem("oT_ready")
        out_made, added, stored = sem("out_made"), sem("added"), sem("stored")
        block = ctx.enter_context(nc.Block())

        @block.sync
        def _(sp):
            for par in range(2):
                sp.dma_start(x[:, par], x_in[par]).then_inc(x_loaded[par], 16)
            sp.dma_start(wqkv, w_qkv).then_inc(weights_in[0], 16)
            sp.dma_start(wo, w_out).then_inc(weights_in[1], 16)
            for e in range(core.kept_experts):
                sp.dma_start(core.w1[:, e * W1E:(e + 1) * W1E], w1_dram[:, e]).then_inc(experts_in, 16)
            with sp.Fori(0, TURNS - 1) as i:
                for par in range(2):
                    sp.wait_ge(added, 2 * i + par + 1)
                    sp.dma_start(x_out[bass.ds(2 * i + par, 1)].rearrange("a p d -> p a d"),
                                 xo.unsqueeze(1)).then_inc(stored, 16)
                    sp.dma_start(x[:, par:par + 1], x_in[bass.ds(2 * i + 2 + par, 1)]
                                 .rearrange("a p d -> p a d")).then_inc(x_loaded[par], 16)
            for par in range(2):
                t = TILES - 2 + par
                sp.wait_ge(added, t + 1)
                sp.dma_start(x_out[t], xo).then_inc(stored, 16)
            sp.wait_ge(stored, 16 * TILES)
            sp.wait_ge(experts_in, 16 * core.kept_experts)

        @block.gpsimd
        def _(pool):
            nc.gpsimd.memset(qz, 0.0).then_inc(cleared, 1)
            nc.gpsimd.memset(kT, 0.0).then_inc(cleared, 1)
            nc.gpsimd.memset(v, 0.0).then_inc(cleared, 1)
            with pool.Fori(0, TURNS) as i:
                for par in range(2):
                    pool.wait_ge(var_ready, 2 * i + par + 1)
                    nc.gpsimd.tensor_tensor(rstd, var_eps, core.mhalf[:], ALU.pow).then_inc(rstd_ready, 1)

        @block.vector
        def _(dve):
            dve.wait_ge(cleared, 3)
            with dve.Fori(0, TURNS) as i:
                link = Chain(dve, chain, i, 6)
                for par in range(2):
                    t = 2 * i + par
                    dve.wait_ge(x_loaded[par], 16 * i + 16)
                    link(nc.vector.bn_stats(st, x[:, par]))
                    nc.vector.nop(nofuse=True)
                    link(nc.vector.bn_aggr(mv, st))
                    nc.vector.tensor_scalar(var_eps, mv[:, 1:2], EPS, None, ALU.add).then_inc(var_ready, 1)
                    dve.wait_ge(rstd_ready, t + 1)
                    dve.wait_ge(x_turned, t)
                    nc.vector.tensor_scalar(xn, x[:, par], mv[:, 0:1], rstd, ALU.subtract, ALU.mult)\
                        .then_inc(xn_ready, 1)
                    dve.wait_ge(k_made, t + 1)
                    dve.wait_ge(scores_made, 4 * t)
                    nc.vector.tensor_copy(kT[:, :, par], bank[0][:].rearrange("p (a b) -> p a b", b=P))\
                        .then_inc(k_ready, 1)

                    def row_max(g):
                        dve.wait_ge(scores_made, 4 * t + g + 1)
                        if g == 0:
                            dve.wait_ge(probs_ready, 4 * t)
                        for pair in range(2):
                            last = nc.vector.tensor_reduce(
                                nmax[:, HG * g + 2 * pair:HG * g + 2 * pair + 2],
                                score_banks[g % 2][pair][:].rearrange("p (h j) -> p h j", h=2),
                                AX.X, ALU.max, negate=True)
                        last.then_inc(max_ready, 1)

                    def probs_out(g):
                        for half, b in ((0, 6), (1, 1)):
                            dve.wait_ge(probs_turned, 8 * t + 2 * g + half + 1)
                            dve.wait_ge(pv_made, 4 * t + g)
                            nc.vector.tensor_copy(probsT[:, half], bank[b][:].rearrange("p (a b) -> p a b", b=P))\
                                .then_inc(probsT_ready, 1)

                    row_max(0)
                    row_max(1)
                    probs_out(0)
                    row_max(2)
                    probs_out(1)
                    row_max(3)
                    probs_out(2)
                    probs_out(3)
                    link(nc.vector.reciprocal(rinv, psum_p))
                    dve.wait_ge(pv_made, 4 * t + 4)
                    dve.wait_ge(o_turned, t)
                    nc.vector.tensor_tensor(o.rearrange("p (h d) -> p h d", d=HD),
                                            bank[7][:].rearrange("p (h d) -> p h d", d=HD),
                                            spread(rinv, 2, HD), ALU.mult).then_inc(o_ready, 1)
                    dve.wait_ge(out_made, t + 1)
                    dve.wait_ge(stored, 32 * i + 16 * par)
                    nc.vector.tensor_tensor(xo, bank[1][:], x[:, par], ALU.add).then_inc(added, 1)
                link.end()

        @block.scalar
        def _(act):
            act.wait_ge(cleared, 3)
            with act.Fori(0, TURNS) as i:
                for par in range(2):
                    t = 2 * i + par
                    act.wait_ge(x_turned, t + 1)
                    act.wait_ge(v_made, t)
                    nc.scalar.activation(xnT, bank[0][:].rearrange("p (a b) -> p a b", b=P), ACT.Copy)\
                        .then_inc(xnT_ready, 1)
                    act.wait_ge(q_made, t + 1)
                    act.wait_ge(scores_made, 4 * t)
                    for r in range(HG):
                        rows = slice(HD * r, HD * r + HD)
                        last = nc.scalar.activation(qz[rows, r], bank[1][rows, :].rearrange("p (a b) -> p a b", b=P),
                                                    ACT.Copy, scale=float(HD) ** -0.5)
                    last.then_inc(q_ready, 1)
                    act.wait_ge(v_made, t + 1)
                    act.wait_ge(pv_made, 4 * t)
                    nc.scalar.activation(v[:, par], bank[6][:], ACT.Copy).then_inc(v_ready, 1)
                    for g in range(4):
                        act.wait_ge(max_ready, 4 * t + g + 1)
                        if g == 0:
                            act.wait_ge(o_ready, t)
                        act.wait_ge(probs_turned, 8 * t + (2 * (g - 1) if g >= 2 else 0))
                        for r in range(HG):
                            h = HG * g + r
                            last = nc.scalar.activation(
                                probs[:, g % 2, r], score_banks[g % 2][r // 2][:, (r % 2) * 2 * P:(r % 2 + 1) * 2 * P],
                                ACT.Exp, bias=nmax[:, h:h + 1], accum_out=psum_p[:, h:h + 1])
                        last.then_inc(probs_ready, 1)
                    act.wait_ge(o_turned, t + 1)
                    act.wait_ge(out_made, t)
                    nc.scalar.activation(oT, bank[0][:].rearrange("p (a b) -> p a b", b=P), ACT.Copy)\
                        .then_inc(oT_ready, 1)

        @block.tensor
        def _(pe):
            pe.wait_ge(weights_in[0], 16)
            pe.wait_ge(weights_in[1], 16)
            with pe.Fori(0, TURNS) as i:
                for par in range(2):
                    t = 2 * i + par
                    pe.wait_ge(xn_ready, t + 1)
                    for k in range(KD):
                        last = nc.tensor.transpose(bank[0][:, k * P:k * P + P], xn[:, k * P:k * P + P], core.ident[:])
                    last.then_inc(x_turned, 1)
                    pe.wait_ge(xnT_ready, t + 1)
                    pe.wait_ge(added, t)
                    for b, first, done in ((1, 0, q_made), (0, D, k_made)):
                        for c in range(KD):
                            for k in range(KD):
                                last = nc.tensor.matmul(bank[b][:, c * P:c * P + P],
                                                        wqkv[:, k, first + c * P:first + c * P + P], xnT[:, k],
                                                        start=(k == 0), stop=(k == KD - 1))
                        last.then_inc(done, 1)
                    for k in range(KD):
                        last = nc.tensor.matmul(bank[6][:], xnT[:, k], wqkv[:, k, 2 * D:3 * D],
                                                start=(k == 0), stop=(k == KD - 1))
                    last.then_inc(v_made, 1)
                    pe.wait_ge(q_ready, t + 1)
                    pe.wait_ge(k_ready, t + 1)

                    first_chunk = i % TURNS_PER_BATCH

                    def scores(g):
                        if g >= 2:
                            pe.wait_ge(probs_ready, 4 * t + g - 1)
                        for r in range(HG):
                            out = score_banks[g % 2][r // 2][:, (r % 2) * 2 * P:(r % 2 + 1) * 2 * P]
                            if par == 0:
                                mask = core.att_mask[:, bass.ds(1 - (TURNS_PER_BATCH - first_chunk) // TURNS_PER_BATCH, 1)]\
                                    .rearrange("p a j -> p (a j)")
                            else:
                                mask = core.att_mask[:, 2]
                            nc.tensor.matmul(out, core.identb[:], mask, start=True, stop=False)
                            last = nc.tensor.matmul(out, qz[:, r, g], kT[:, g].rearrange("p a j -> p (a j)"),
                                                    start=False, stop=True)
                        last.then_inc(scores_made, 1)

                    def values(g):
                        pe.wait_ge(probs_ready, 4 * t + g + 1)
                        for half, b in ((0, 6), (1, 1)):
                            if g == 0 and half == 0:
                                pe.wait_ge(v_ready, t + 1)
                            for j in range(4):
                                last = nc.tensor.transpose(bank[b][:, j * P:j * P + P],
                                                           probs[:, g % 2, 2 * half + j // 2, (j % 2) * P:(j % 2 + 1) * P],
                                                           core.ident[:])
                            last.then_inc(probs_turned, 1)
                        if g == 0:
                            pe.wait_ge(o_ready, t)
                        for half in range(2):
                            pe.wait_ge(probsT_ready, 8 * t + 2 * g + half + 1)
                            for r in range(2):
                                h = HG * g + 2 * half + r
                                for s in range(2):
                                    last = nc.tensor.matmul(bank[7][:, h * HD:h * HD + HD], probsT[:, half, 2 * r + s],
                                                            v[:, s, h * HD:h * HD + HD], start=(s == 0), stop=(s == 1))
                        last.then_inc(pv_made, 1)

                    scores(0)
                    scores(1)
                    values(0)
                    scores(2)
                    values(1)
                    scores(3)
                    values(2)
                    values(3)
                    pe.wait_ge(o_ready, t + 1)
                    for k in range(KD):
                        last = nc.tensor.transpose(bank[0][:, k * P:k * P + P], o[:, k * P:k * P + P], core.ident[:])
                    last.then_inc(o_turned, 1)
                    pe.wait_ge(oT_ready, t + 1)
                    for k in range(KD):
                        last = nc.tensor.matmul(bank[1][:], oT[:, k], wo[:, k], start=(k == 0), stop=(k == KD - 1))
                    last.then_inc(out_made, 1)


def experts(core, tag, x_rows, xn_rows, gate, w1_dram, w2_dram, w2_tail):
    nc, bank, arena = core.nc, core.bank, core.arena
    gate_sb, at = cut(arena, core.work_at, KD, EXPERTS)
    index, at = cut(arena, at, SLOTS)
    weight, at = cut(arena, at, SLOTS)
    owner, at = cut(arena, at, SLOTS)
    index, owner = index.bitcast(U32), owner.bitcast(I32)
    stage_at = at
    with stage_semaphores(nc, tag) as sem:
        gate_in, rest_in, tail_in = sem("gate_in"), sem("rest_in"), sem("w2_in")
        score_rows(core, sem, x_rows, xn_rows, gate_sb, gate, w1_dram, w2_dram, w2_tail, gate_in, rest_in, tail_in,
                   stage_at)
        sort_rows(core, sem, index, weight, owner, stage_at)
        run_slots(core, tag, sem, x_rows, xn_rows, index, weight, owner, rest_in, tail_in, stage_at)


def score_rows(core, sem, x_rows, xn_rows, gate_sb, gate, w1_dram, w2_dram, w2_tail, gate_in, rest_in, tail_in, at):
    nc, bank, arena = core.nc, core.bank, core.arena
    x_in = x_rows.rearrange("(t p) d -> t p d", p=P)
    xn_out = xn_rows.rearrange("(t p) d -> t p d", p=P)
    x, at = cut(arena, at, 2, D)
    xn, at = cut(arena, at, 2, D)
    xnT, at = cut(arena, at, KD, P)
    st, at = cut(arena, at, 6)
    mv, at = cut(arena, at, 2)
    var_eps, at = cut(arena, at, 1)
    rstd, at = cut(arena, at, 1)
    assert at <= core.left
    x_loaded = [sem("x_loaded0"), sem("x_loaded1")]
    xn_stored = [sem("xn_stored0"), sem("xn_stored1")]
    chain = sem("norm_chain")
    var_ready, rstd_ready, xn_ready = sem("var_ready"), sem("rstd_ready"), sem("xn_ready")
    x_turned, xnT_ready, logits_made = sem("x_turned"), sem("xnT_ready"), sem("logits_made")
    with nc.Block() as block:
        @block.sync
        def _(sp):
            for par in range(2):
                sp.dma_start(x[:, par], x_in[par]).then_inc(x_loaded[par], 16)
            sp.dma_start(gate_sb, gate).then_inc(gate_in, 16)
            with sp.Fori(0, TURNS) as i:
                for par in range(2):
                    sp.wait_ge(xn_ready, 2 * i + par + 1)
                    sp.dma_start(xn_out[bass.ds(2 * i + par, 1)].rearrange("a p d -> p a d"),
                                 xn[:, par:par + 1]).then_inc(xn_stored[par], 16)
                    sp.dma_start(x[:, par:par + 1], x_in[bass.ds((2 * i + 2 + par) % (TILES + 1), 1)]
                                 .rearrange("a p d -> p a d")).then_inc(x_loaded[par], 16)
            for par in range(2):
                sp.wait_ge(xn_stored[par], 16 * TURNS)
                sp.wait_ge(x_loaded[par], 16 * (TURNS + 1))

        @block.gpsimd
        def _(pool):
            with pool.Fori(0, TURNS) as i:
                for par in range(2):
                    pool.wait_ge(var_ready, 2 * i + par + 1)
                    nc.gpsimd.tensor_tensor(rstd, var_eps, core.mhalf[:], ALU.pow).then_inc(rstd_ready, 1)

        @block.vector
        def _(dve):
            with dve.Fori(0, TURNS) as i:
                link = Chain(dve, chain, i, 4)
                for par in range(2):
                    t = 2 * i + par
                    dve.wait_ge(x_loaded[par], 16 * i + 16)
                    link(nc.vector.bn_stats(st, x[:, par]))
                    nc.vector.nop(nofuse=True)
                    link(nc.vector.bn_aggr(mv, st))
                    nc.vector.tensor_scalar(var_eps, mv[:, 1:2], EPS, None, ALU.add).then_inc(var_ready, 1)
                    dve.wait_ge(rstd_ready, t + 1)
                    dve.wait_ge(x_turned, t)
                    dve.wait_ge(xn_stored[par], 16 * i)
                    nc.vector.tensor_scalar(xn[:, par], x[:, par], mv[:, 0:1], rstd, ALU.subtract, ALU.mult)\
                        .then_inc(xn_ready, 1)
                link.end()

        @block.scalar
        def _(act):
            for e in range(core.kept_experts, EXPERTS):
                act.dma_start(core.w1[:, e * W1E:(e + 1) * W1E], w1_dram[:, e]).then_inc(rest_in, 16)
            w2 = core.w2.rearrange("p (e k d) -> p e k d", e=EXPERTS, k=KI)
            act.dma_start(w2[:, :, 0:KI - 1], w2_dram).then_inc(tail_in, 16)
            act.dma_start(w2[0:LAST_I, :, KI - 1], w2_tail).then_inc(tail_in, 16)
            with act.Fori(0, TURNS) as i:
                for par in range(2):
                    t = 2 * i + par
                    act.wait_ge(x_turned, t + 1)
                    act.wait_ge(logits_made, t)
                    nc.scalar.activation(xnT, bank[par][:].rearrange("p (a b) -> p a b", b=P), ACT.Copy)\
                        .then_inc(xnT_ready, 1)

        @block.tensor
        def _(pe):
            pe.wait_ge(gate_in, 16)
            with pe.Fori(0, TURNS) as i:
                for par in range(2):
                    t = 2 * i + par
                    pe.wait_ge(xn_ready, t + 1)
                    pe.wait_ge(xnT_ready, t)
                    for k in range(KD):
                        last = nc.tensor.transpose(bank[par][:, k * P:k * P + P], xn[:, par, k * P:k * P + P],
                                                   core.ident[:])
                    last.then_inc(x_turned, 1)
                    pe.wait_ge(xnT_ready, t + 1)
                    for k in range(KD):
                        last = nc.tensor.matmul(bank[7][:, bass.ds(EXPERTS * t, EXPERTS)], xnT[:, k], gate_sb[:, k],
                                                start=(k == 0), stop=(k == KD - 1))
                    last.then_inc(logits_made, 1)


def sort_rows(core, sem, index, weight, owner, at):
    nc, bank, arena = core.nc, core.bank, core.arena
    E, T, K = EXPERTS, TILES, TOPK
    logits, at = cut(arena, at, T, E)
    best, at = cut(arena, at, T, 8)
    which, at = cut(arena, at, T, 8)
    which_f, at = cut(arena, at, T, K)
    chosen, at = cut(arena, at, K, T * E)
    both, at = cut(arena, at, (T + 1) * E)
    both = both.bitcast(BF16)[:, 0:(T + 1) * E].rearrange("p (t e) -> p t e", e=E)
    gap, at = cut(arena, at, T)
    gap_exp, at = cut(arena, at, T)
    den, at = cut(arena, at, T)
    w, at = cut(arena, at, K, T)
    need, at = cut(arena, at, E)
    need_i, at = cut(arena, at, E)
    slots_i, at = cut(arena, at, E)
    slots, at = cut(arena, at, E)
    end, at = cut(arena, at, E)
    start, at = cut(arena, at, E)
    place, at = cut(arena, at, T * E)
    picked, at = cut(arena, at, K, T * E)
    entry, at = cut(arena, at, K * T)
    entry_i, at = cut(arena, at, K * T)
    slot_i, at = cut(arena, at, K * T)
    spot_i, at = cut(arena, at, K * T)
    slot, at = cut(arena, at, K * T)
    spot, at = cut(arena, at, K * T)
    at_spot, at = cut(arena, at, K * T, P)
    by_slot, at = cut(arena, at, 3, K * T, SLOTS)
    empty, at = cut(arena, at, SLOTS)
    index_f, at = cut(arena, at, SLOTS)
    past, at = cut(arena, at, SLOTS, E)
    owner_f, at = cut(arena, at, SLOTS)
    assert at <= core.left
    chain = sem("sort_chain")
    both_ready, ranks_made, gap_ready, exp_ready = sem("both"), sem("ranks"), sem("gap"), sem("exp")
    tables_ready, lists_made, done = sem("tables"), sem("lists"), sem("sorted")
    with nc.Block() as block:
        @block.vector
        def _(dve):
            link = Chain(dve, chain)
            link(nc.vector.tensor_copy(logits.rearrange("p t e -> p (t e)"), bank[7][:, 0:T * E]))
            for t in range(T):
                last = nc.vector.max(best[:, t], logits[:, t])
            link(last)
            for t in range(T):
                last = nc.vector.max_index(which.bitcast(U32)[:, t], best[:, t], logits[:, t])
            link(last)
            nc.vector.tensor_tensor(gap, best[:, :, 1], best[:, :, 0], ALU.subtract).then_inc(gap_ready, 1)
            link(nc.vector.tensor_copy(which_f, which.bitcast(U32)[:, :, 0:K]))
            for k in range(K):
                last = nc.vector.tensor_tensor(chosen[:, k].rearrange("p (t e) -> p t e", e=E),
                                               spread(core.count[:, 0:E], 1, T), spread(which_f[:, :, k], 2, E),
                                               ALU.is_equal)
            link(last)
            link(nc.vector.memset(both[:, T], 0.0))
            nc.vector.tensor_tensor(both[:, 0:T].rearrange("p t e -> p (t e)"), chosen[:, 0], chosen[:, 1], ALU.add)\
                .then_inc(both_ready, 1)
            dve.wait_ge(exp_ready, 1)
            link(nc.vector.tensor_scalar(den, gap_exp, 1.0, None, ALU.add))
            link(nc.vector.reciprocal(w[:, 0], den))
            link(nc.vector.tensor_tensor(w[:, 1], gap_exp, w[:, 0], ALU.mult))
            dve.wait_ge(ranks_made, 1)
            link(nc.vector.tensor_scalar(need, bank[0][:, T * E:(T + 1) * E], float(P - 1), None, ALU.add))
            link(nc.vector.tensor_copy(need_i.bitcast(I32), need))
            link(nc.vector.tensor_scalar(slots_i.bitcast(I32), need_i.bitcast(I32), 7, None, ALU.logical_shift_right))
            link(nc.vector.tensor_copy(slots, slots_i.bitcast(I32)))
            link(nc.vector.tensor_tensor_scan(end, slots, core.zero[:, 0:E], 0.0, ALU.add, ALU.add))
            link(nc.vector.tensor_tensor(start, end, slots, ALU.subtract))
            link(nc.vector.tensor_scalar(start, start, float(P), None, ALU.mult))
            link(nc.vector.tensor_tensor(place.rearrange("p (t e) -> p t e", e=E),
                                         bank[0][:, 0:T * E].rearrange("p (t e) -> p t e", e=E),
                                         spread(start, 1, T), ALU.add))
            link(nc.vector.tensor_tensor(picked, chosen, spread(place, 1, K), ALU.mult))
            link(nc.vector.tensor_reduce(entry, picked.rearrange("p k (t e) -> p (k t) e", e=E), AX.X, ALU.add))
            link(nc.vector.tensor_copy(entry_i.bitcast(I32), entry))
            link(nc.vector.tensor_scalar(slot_i.bitcast(I32), entry_i.bitcast(I32), 7, None, ALU.logical_shift_right))
            link(nc.vector.tensor_scalar(spot_i.bitcast(I32), entry_i.bitcast(I32), P - 1, None, ALU.bitwise_and))
            link(nc.vector.tensor_copy(slot, slot_i.bitcast(I32)))
            link(nc.vector.tensor_copy(spot, spot_i.bitcast(I32)))
            link(nc.vector.tensor_tensor(at_spot, spread(core.count[:], 1, K * T), spread(spot, 2, P), ALU.is_equal))
            link(nc.vector.tensor_tensor(by_slot[:, 2], spread(core.count[:, 0:SLOTS], 1, K * T),
                                         spread(slot, 2, SLOTS), ALU.is_equal))
            for k in range(K):
                part = slice(k * T, (k + 1) * T)
                link(nc.vector.tensor_tensor(by_slot[:, 0, part], by_slot[:, 2, part],
                                             spread(core.rowid[:], 2, SLOTS), ALU.mult))
            for k in range(K):
                part = slice(k * T, (k + 1) * T)
                last = nc.vector.tensor_tensor(by_slot[:, 1, part], by_slot[:, 2, part],
                                               spread(w[:, k], 2, SLOTS), ALU.mult)
            last.then_inc(tables_ready, 1)
            link(nc.vector.tensor_tensor(past, spread(core.count[:, 0:SLOTS], 2, E), spread(end, 1, SLOTS), ALU.is_ge))
            link(nc.vector.tensor_reduce(owner_f, past, AX.X, ALU.add))
            link(nc.vector.tensor_scalar(owner_f, owner_f, float(E - 1), None, ALU.min))
            link(nc.vector.tensor_copy(owner, owner_f))
            dve.wait_ge(lists_made, 1)
            link(nc.vector.tensor_scalar(empty, bank[1][:, 2 * SLOTS:3 * SLOTS], -1.0, 1.0, ALU.mult, ALU.add))
            link(nc.vector.scalar_tensor_tensor(out=index_f, in0=empty, scalar=core.spareid[:], in1=bank[1][:, 0:SLOTS],
                                                op0=ALU.mult, op1=ALU.add))
            link(nc.vector.tensor_copy(index, index_f))
            link(nc.vector.tensor_copy(weight, bank[1][:, SLOTS:2 * SLOTS]))

        @block.scalar
        def _(act):
            act.wait_ge(gap_ready, 1)
            nc.scalar.activation(gap_exp, gap, ACT.Exp).then_inc(exp_ready, 1)

        @block.tensor
        def _(pe):
            pe.wait_ge(both_ready, 1)
            nc.tensor.matmul(bank[0][:, 0:(T + 1) * E], core.before[:], both.rearrange("p t e -> p (t e)"),
                             start=True, stop=False)
            for t in range(T):
                last = nc.tensor.matmul(bank[0][:, (t + 1) * E:(T + 1) * E].rearrange("p (t e) -> p t e", e=E),
                                        core.onesb[:], spread(both[:, t], 1, T - t), start=False, stop=(t == T - 1))
            last.then_inc(ranks_made, 1)
            pe.wait_ge(tables_ready, 1)
            for j in range(K * T):
                last = nc.tensor.matmul(bank[1][:, 0:3 * SLOTS].rearrange("p (c s) -> p c s", c=3), at_spot[:, j],
                                        by_slot[:, :, j], start=(j == 0), stop=(j == K * T - 1))
            last.then_inc(lists_made, 1)


def run_slots(core, tag, sem, x_rows, xn_rows, index, weight, owner, rest_in, tail_in, at):
    nc, bank, arena = core.nc, core.bank, core.arena
    rows, at = cut(arena, at, 2, D)
    rowsT, at = cut(arena, at, 2, KD * P)
    silu, at = cut(arena, at, 2, INTER)
    act_sb, at = cut(arena, at, INTER)
    actT, at = cut(arena, at, KI, P)
    y, at = cut(arena, at, 2, D)
    from_rows, at = cut(arena, at, 2)
    to_rows, at = cut(arena, at, 1)
    from_rows, to_rows = from_rows.bitcast(U32), to_rows.bitcast(U32)
    assert at <= core.left
    w1 = core.w1.rearrange("p (e n) -> p e n", e=EXPERTS)
    w2 = core.w2.rearrange("p (e n) -> p e n", e=EXPERTS)
    picked, placed = sem("index_read"), sem("index_to")
    *gathered, added = core.pool_dma[tag]
    rows_turned, rowsT_ready, up_made, silu_ready = sem("rows_turned"), sem("rowsT_ready"), sem("up"), sem("silu")
    act_ready, act_turned, actT_ready = sem("act_ready"), sem("act_turned"), sem("actT_ready")
    y_made, y_ready = sem("y_made"), sem("y_ready")
    turns = SLOTS // 2
    with nc.Block() as block:
        @block.gpsimd
        def _(pool):
            def gather(s, par, turn):
                if turn is not None:
                    pool.wait_ge(rows_turned, s - 1)
                    nc.gpsimd.nop(nofuse=True)
                nc.gpsimd.tensor_copy(from_rows[:, par:par + 1], index[:, bass.ds(s, 1)]).then_inc(picked, 1)
                pool.wait_ge(picked, s + 1)
                nc.gpsimd.nop(nofuse=True)
                nc.gpsimd.indirect_dma_start(
                    out=rows[:, par], out_offset=None, in_=xn_rows,
                    in_offset=bass.IndirectOffsetOnAxis(ap=from_rows[:, par:par + 1], axis=0))\
                    .then_inc(gathered[par], 16)

            def add(s, par):
                pool.wait_ge(added, 16 * s)
                nc.gpsimd.nop(nofuse=True)
                nc.gpsimd.tensor_copy(to_rows, index[:, bass.ds(s, 1)]).then_inc(placed, 1)
                pool.wait_ge(placed, s + 1)
                pool.wait_ge(y_ready, s + 1)
                nc.gpsimd.nop(nofuse=True)
                nc.gpsimd.indirect_dma_start(
                    out=x_rows, out_offset=bass.IndirectOffsetOnAxis(ap=to_rows, axis=0),
                    in_=y[:, par], in_offset=None, compute_op=ALU.add).then_inc(added, 16)

            for par in range(2):
                gather(par, par, None)
            with pool.Fori(0, turns - 1) as i:
                for par in range(2):
                    gather(2 * i + 2 + par, par, i + 1)
                    add(2 * i + par, par)
            for par in range(2):
                add(SLOTS - 2 + par, par)
            pool.wait_ge(added, 16 * SLOTS)

        def turned(act, s, par):
            act.wait_ge(rows_turned, s + 1)
            if not isinstance(s, int) or s >= 2:
                act.wait_ge(up_made, s - 1)
            nc.scalar.activation(rowsT[:, par], bank[0][:], ACT.Copy).then_inc(rowsT_ready, 1)

        def gated(act, s, par):
            act.wait_ge(up_made, s + 1)
            act.wait_ge(act_ready, s)
            nc.scalar.activation(silu[:, par], bank[1 + 2 * par][:, 0:INTER], ACT.Silu).then_inc(silu_ready, 1)

        def result(act, s, par):
            act.wait_ge(y_made, s + 1)
            act.wait_ge(added, 16 * s)
            nc.scalar.activation(y[:, par], bank[6][:], ACT.Copy).then_inc(y_ready, 1)

        @block.scalar
        def _(act):
            turned(act, 0, 0)
            turned(act, 1, 1)
            gated(act, 0, 0)
            with act.Fori(0, turns - 1) as i:
                for par in range(2):
                    s = 2 * i + par
                    gated(act, s + 1, 1 - par)
                    turned(act, s + 2, par)
                    result(act, s, par)
            gated(act, SLOTS - 1, 1)
            result(act, SLOTS - 2, 0)
            result(act, SLOTS - 1, 1)

        def product(dve, s, par):
            dve.wait_ge(silu_ready, s + 1)
            dve.wait_ge(act_turned, s)
            nc.vector.scalar_tensor_tensor(out=act_sb, in0=silu[:, par], scalar=weight[:, bass.ds(s, 1)],
                                           in1=bank[2 + 2 * par][:, 0:INTER], op0=ALU.mult, op1=ALU.mult)\
                .then_inc(act_ready, 1)

        def act_out(dve, s):
            dve.wait_ge(act_turned, s + 1)
            dve.wait_ge(y_made, s)
            nc.vector.tensor_copy(actT[:, 0:KI - 1], bank[5][:, 0:(KI - 1) * P].rearrange("p (a b) -> p a b", b=P))
            nc.vector.tensor_copy(actT[0:LAST_I, KI - 1], bank[5][0:LAST_I, (KI - 1) * P:KI * P])\
                .then_inc(actT_ready, 1)

        @block.vector
        def _(dve):
            product(dve, 0, 0)
            with dve.Fori(0, turns - 1) as i:
                for par in range(2):
                    s = 2 * i + par
                    act_out(dve, s)
                    product(dve, s + 1, 1 - par)
            act_out(dve, SLOTS - 2)
            product(dve, SLOTS - 1, 1)
            act_out(dve, SLOTS - 1)

        @block.tensor
        def _(pe):
            def turn(s, par, i):
                pe.wait_ge(gathered[par], 16 * i + 16)
                pe.wait_ge(rowsT_ready, s)
                for k in range(KD):
                    last = nc.tensor.transpose(bank[0][:, k * P:k * P + P], rows[:, par, k * P:k * P + P],
                                               core.ident[:])
                last.then_inc(rows_turned, 1)

            def up(s, par):
                e = pe.value_load(owner[0:1, bass.ds(s, 1)], min_val=0, max_val=EXPERTS - 1)
                pe.wait_ge(rowsT_ready, s + 1)
                if not isinstance(s, int) or s >= 1:
                    pe.wait_ge(act_ready, s - 1)
                for part in range(2):
                    for k in range(KD):
                        at = (2 * k + part) * INTER
                        last = nc.tensor.matmul(bank[1 + 2 * par + part][:, 0:INTER], rowsT[:, par, k * P:k * P + P],
                                                w1[:, bass.ds(e, 1), at:at + INTER].rearrange("p a n -> p (a n)"),
                                                start=(k == 0), stop=(k == KD - 1))
                last.then_inc(up_made, 1)

            def turn_act(s):
                pe.wait_ge(act_ready, s + 1)
                pe.wait_ge(actT_ready, s)
                for k in range(KI):
                    n = P if k < KI - 1 else LAST_I
                    last = nc.tensor.transpose(bank[5][0:n, k * P:k * P + P], act_sb[:, k * P:k * P + n], core.ident[:])
                last.then_inc(act_turned, 1)

            def down(s):
                e = pe.value_load(owner[0:1, bass.ds(s, 1)], min_val=0, max_val=EXPERTS - 1)
                pe.wait_ge(actT_ready, s + 1)
                pe.wait_ge(y_ready, s)
                for k in range(KI):
                    n = P if k < KI - 1 else LAST_I
                    last = nc.tensor.matmul(bank[6][:], actT[0:n, k],
                                            w2[0:n, bass.ds(e, 1), k * D:k * D + D].rearrange("p a n -> p (a n)"),
                                            start=(k == 0), stop=(k == KI - 1))
                last.then_inc(y_made, 1)

            turn(0, 0, 0)
            pe.wait_ge(rest_in, 16 * (EXPERTS - core.kept_experts))
            pe.wait_ge(tail_in, 32)
            up(0, 0)
            turn(1, 1, 0)
            with pe.Fori(0, turns - 1) as i:
                for par in range(2):
                    s = 2 * i + par
                    up(s + 1, 1 - par)
                    turn_act(s)
                    turn(s + 2, par, i + 1)
                    down(s)
            up(SLOTS - 1, 1)
            turn_act(SLOTS - 2)
            down(SLOTS - 2)
            turn_act(SLOTS - 1)
            down(SLOTS - 1)


def mamba(core, x_in, x_out, in_w, out_w, conv_w, conv_b, a_log, d_skip, dt_bias, norm_w):
    nc, bank, arena = core.nc, core.bank, core.arena
    H = MHEADS
    at = core.other_at
    w_in, at = cut(arena, at, KD, WIN_COLS)
    w_out, at = cut(arena, at, KY, D)
    taps, at = cut(arena, at, CB, TAPS)
    tap_bias, at = cut(arena, at, CB)
    norm, at = cut(arena, at, KY)
    a_row, at = cut(arena, at, H)
    d_row, at = cut(arena, at, H)
    dtb_row, at = cut(arena, at, H)
    x, at = cut(arena, at, 2, D)
    xn, at = cut(arena, at, D)
    xnT, at = cut(arena, at, KD, P)
    halo = TAPS - 1
    cin = []
    for par in range(2):
        c, at = cut(arena, at, CB, halo + P)
        cin.append(c)
    conv, at = cut(arena, at, CB, P)
    xc, at = cut(arena, at, 2, CB, P)
    zs, at = cut(arena, at, 2, INNER)
    decays, at = cut(arena, at, 2, 4, P)
    xs, at = cut(arena, at, INNER)
    xskip, at = cut(arena, at, INNER)
    xdt, at = cut(arena, at, INNER)
    xlast, at = cut(arena, at, INNER)
    state, at = cut(arena, at, INNER)
    ysum, at = cut(arena, at, INNER)
    y, at = cut(arena, at, INNER)
    yT, at = cut(arena, at, KY, P)
    xo, at = cut(arena, at, D)
    b_rows, at = cut(arena, at, STATE)
    st, at = cut(arena, at, 6)
    mv, at = cut(arena, at, 2)
    var_eps, at = cut(arena, at, 1)
    rstd, at = cut(arena, at, 1)
    u, at = cut(arena, at, H)
    mag, at = cut(arena, at, H)
    e_mag, at = cut(arena, at, H)
    ratio, at = cut(arena, at, H)
    ratio2, at = cut(arena, at, H)
    series, at = cut(arena, at, H)
    dt, at = cut(arena, at, 2, H)
    da, at = cut(arena, at, 2, H)
    sums, at = cut(arena, at, 2 * H)
    ncs, at = cut(arena, at, H)
    gap, at = cut(arena, at, H)
    to_end, at = cut(arena, at, H)
    from_start, at = cut(arena, at, 2 * H)
    carried, at = cut(arena, at, 2 * H)
    squares, at = cut(arena, at, 1)
    mean_eps, at = cut(arena, at, 1)
    rinv, at = cut(arena, at, 1)
    assert at <= core.left, at - core.left
    small = bank[2]
    CS, SUM, BC, BROWS, DT = 0, H, P, 2 * P, 3 * P
    with stage_semaphores(nc, "mam") as sem, ExitStack() as ctx:
        w_in_here, w_out_here, rows_here = sem("w_in"), sem("w_out"), sem("rows_here")
        x_loaded = [sem("x_loaded0"), sem("x_loaded1")]
        chains = [sem("chain_first"), sem("chain_loop"), sem("chain_last")]
        cleared, a_exp, a_ready = sem("cleared"), sem("a_exp"), sem("a_ready")
        var_ready, rstd_ready, xn_ready = sem("var_ready"), sem("rstd_ready"), sem("xn_ready")
        x_turned, xnT_ready = sem("x_turned"), sem("xnT_ready")
        front_made, cin_ready, conv_ready, xc_ready, z_ready = (
            sem("front_made"), sem("cin_ready"), sem("conv_ready"), sem("xc_ready"), sem("z_ready"))
        dt_made, mag_ready, e_mag_ready, da_ready = sem("dt_made"), sem("mag"), sem("e_mag"), sem("da_ready")
        xs_turned, xs_ready, small_made, b_ready = sem("xs_turned"), sem("xs_ready"), sem("small"), sem("b_ready")
        sums_ready = sem("sums_ready")
        gap_ready, exps_ready, to_end_ready, carried_ready = sem("gap"), sem("exps"), sem("to_end"), sem("carried")
        xdt_ready, xskip_ready, xlast_ready = sem("xdt"), sem("xskip"), sem("xlast")
        sums_made, decays_ready, mixed_ready, yd_made = sem("sums"), sem("decays"), sem("mixed"), sem("yd_made")
        yo_made, yo_read, ysum_ready, y_ready = sem("yo_made"), sem("yo_read"), sem("ysum"), sem("y_ready")
        st_made, decayed, state_ready = sem("st_made"), sem("decayed"), sem("state_ready")
        y_turned, yT_ready, squares_ready = sem("y_turned"), sem("yT_ready"), sem("squares")
        mean_ready, rinv_ready = sem("mean"), sem("rinv")
        out_made, added, stored = sem("out_made"), sem("added"), sem("stored")
        block = ctx.enter_context(nc.Block())

        @block.sync
        def _(sp):
            for par in range(2):
                sp.dma_start(x[:, par], x_in[par]).then_inc(x_loaded[par], 16)
            for k in range(KD):
                sp.dma_start(w_in[:, k], in_w[:, k]).then_inc(w_in_here, 16)
            for dst, src in ((taps, conv_w), (tap_bias, conv_b), (norm, norm_w)):
                sp.dma_start(dst, src).then_inc(rows_here, 16)
            for dst, src in ((a_row, a_log), (d_row, d_skip), (dtb_row, dt_bias)):
                sp.dma_start(dst, src.partition_broadcast(P)).then_inc(rows_here, 16)
            sp.dma_start(w_out, out_w).then_inc(w_out_here, 16)
            with sp.Fori(0, TURNS - 1) as i:
                for par in range(2):
                    sp.wait_ge(added, 2 * i + par + 1)
                    sp.dma_start(x_out[bass.ds(2 * i + par, 1)].rearrange("a p d -> p a d"),
                                 xo.unsqueeze(1)).then_inc(stored, 16)
                    sp.dma_start(x[:, par:par + 1], x_in[bass.ds(2 * i + 2 + par, 1)]
                                 .rearrange("a p d -> p a d")).then_inc(x_loaded[par], 16)
            for par in range(2):
                t = TILES - 2 + par
                sp.wait_ge(added, t + 1)
                sp.dma_start(x_out[t], xo).then_inc(stored, 16)
            sp.wait_ge(stored, 16 * TILES)

        @block.gpsimd
        def _(pool):
            nc.gpsimd.memset(state, 0.0).then_inc(cleared, 1)
            for c in cin:
                nc.gpsimd.memset(c, 0.0).then_inc(cleared, 1)
            pool.wait_ge(rows_here, 96)
            pool.wait_ge(cleared, 3)

            def norm_power(n):
                pool.wait_ge(var_ready, n + 1)
                nc.gpsimd.tensor_tensor(rstd, var_eps, core.mhalf[:], ALU.pow).then_inc(rstd_ready, 1)

            def by_head(v):
                return v.rearrange("p (h d) -> p h d", h=H)

            def step(t):
                pool.wait_ge(xs_ready, 2 * t + 2)
                pool.wait_ge(squares_ready, t)
                nc.gpsimd.tensor_tensor(by_head(xskip), by_head(xs), spread(d_row, 2, MHD), ALU.mult)\
                    .then_inc(xskip_ready, 1)
                pool.wait_ge(to_end_ready, t + 1)
                pool.wait_ge(xdt_ready, t + 1)
                pool.wait_ge(st_made, 2 * t)
                nc.gpsimd.tensor_tensor(by_head(xlast), by_head(xdt), spread(to_end, 2, MHD), ALU.mult)\
                    .then_inc(xlast_ready, 1)
                pool.wait_ge(carried_ready, t + 1)
                pool.wait_ge(yo_made, 2 * t + 2)
                pool.wait_ge(state_ready, t)
                nc.gpsimd.tensor_tensor(by_head(state), by_head(state), spread(carried[:, H:2 * H], 2, MHD), ALU.mult)\
                    .then_inc(decayed, 1)
                pool.wait_ge(mean_ready, t + 1)
                nc.gpsimd.tensor_tensor(rinv, mean_eps, core.mhalf[:], ALU.pow).then_inc(rinv_ready, 1)

            norm_power(0)
            norm_power(1)
            with pool.Fori(0, TILES - 2) as t:
                step(t)
                norm_power(t + 2)
            step(TILES - 2)
            step(TILES - 1)

        @block.vector
        def _(dve):
            def layer_norm(link, n, par, turn):
                dve.wait_ge(x_loaded[par], 16 * turn + 16)
                link(nc.vector.bn_stats(st, x[:, par]))
                nc.vector.nop(nofuse=True)
                link(nc.vector.bn_aggr(mv, st))
                nc.vector.tensor_scalar(var_eps, mv[:, 1:2], EPS, None, ALU.add).then_inc(var_ready, 1)
                dve.wait_ge(rstd_ready, n + 1)
                dve.wait_ge(x_turned, n)
                nc.vector.tensor_scalar(xn, x[:, par], mv[:, 0:1], rstd, ALU.subtract, ALU.mult).then_inc(xn_ready, 1)

            def time_steps(link, n, par):
                dve.wait_ge(dt_made, n + 1)
                link(nc.vector.tensor_tensor(u, small[:, DT:DT + H], dtb_row, ALU.add))
                nc.vector.scalar_tensor_tensor(out=mag, in0=u, scalar=-1.0, in1=u, op0=ALU.mult, op1=ALU.max)\
                    .then_inc(mag_ready, 1)
                dve.wait_ge(e_mag_ready, n + 1)
                link(nc.vector.tensor_scalar(ratio, e_mag, 2.0, None, ALU.add))
                link(nc.vector.reciprocal(ratio, ratio))
                link(nc.vector.tensor_tensor(ratio, e_mag, ratio, ALU.mult))
                link(nc.vector.tensor_tensor(ratio2, ratio, ratio, ALU.mult))
                link(nc.vector.tensor_scalar(series, ratio2, 1.0 / 15, None, ALU.mult))
                for odd in (13, 11, 9, 7, 5, 3):
                    link(nc.vector.scalar_tensor_tensor(out=series, in0=series, scalar=1.0 / odd, in1=ratio2,
                                                        op0=ALU.add, op1=ALU.mult))
                link(nc.vector.scalar_tensor_tensor(out=series, in0=series, scalar=1.0, in1=ratio,
                                                    op0=ALU.add, op1=ALU.mult))
                link(nc.vector.tensor_scalar(u, u, 0.0, None, ALU.max))
                link(nc.vector.scalar_tensor_tensor(out=dt[:, par], in0=series, scalar=2.0, in1=u,
                                                    op0=ALU.mult, op1=ALU.add))
                nc.vector.tensor_tensor(da[:, par], dt[:, par], a_row, ALU.mult).then_inc(da_ready, 1)

            def convolve(link, n, par, keep):
                dve.wait_ge(cin_ready, 3 * n + 3)
                link(nc.vector.tensor_scalar(cin[par][:, :, 0:halo], cin[1 - par][:, :, P:P + halo], keep, None,
                                             ALU.mult))
                dve.wait_ge(xc_ready, n)
                for k in range(TAPS):
                    for c in range(CB):
                        src = cin[par][:, c, k:k + P]
                        if k == 0:
                            last = nc.vector.tensor_scalar(conv[:, c], src, taps[:, c, k:k + 1], None, ALU.mult)
                        else:
                            last = nc.vector.scalar_tensor_tensor(out=conv[:, c], in0=src, scalar=taps[:, c, k:k + 1],
                                                                  in1=conv[:, c], op0=ALU.mult, op1=ALU.add)
                    if k < TAPS - 1:
                        link(last)
                last.then_inc(conv_ready, 1)

            def by_head(v):
                return v.rearrange("p (h d) -> p h d", h=v.shape[1] // MHD)

            def step(link, t, turn, par, front):
                keep = core.keep[:, bass.ds(turn % TURNS_PER_BATCH, 1)] if par == 0 else core.ones[:, 0:1]
                dve.wait_ge(sums_ready, t + 1)
                dve.wait_ge(decays_ready, 4 * t)
                link(nc.vector.tensor_scalar(ncs, sums[:, 0:H], -1.0, None, ALU.mult))
                dve.wait_ge(to_end_ready, t)
                nc.vector.tensor_tensor(gap, sums[:, H:2 * H], ncs, ALU.add).then_inc(gap_ready, 1)
                dve.wait_ge(xs_ready, 2 * t + 2)
                dve.wait_ge(yd_made, 4 * t)
                dve.wait_ge(xlast_ready, t)
                nc.vector.tensor_tensor(by_head(xdt), by_head(xs), spread(dt[:, par], 2, MHD), ALU.mult)\
                    .then_inc(xdt_ready, 1)
                dve.wait_ge(exps_ready, t + 1)
                dve.wait_ge(decayed, t)
                nc.vector.tensor_scalar(carried, from_start, keep, None, ALU.mult).then_inc(carried_ready, 1)
                for g in range(4):
                    dve.wait_ge(decays_ready, 4 * t + g + 1)
                    nc.vector.tensor_tensor(decays[:, g % 2], decays[:, g % 2], spread(small[:, BC:BC + P], 1, 4),
                                            ALU.mult).then_inc(mixed_ready, 1)
                dve.wait_ge(carried_ready, t + 1)
                for half, b in ((0, 7), (1, 3)):
                    part = slice(half * 512, half * 512 + 512)
                    dve.wait_ge(yo_made, 2 * t + half + 1)
                    nc.vector.tensor_tensor(by_head(ysum[:, part]), by_head(bank[b][:]),
                                            spread(carried[:, 8 * half:8 * half + 8], 2, MHD), ALU.mult)\
                        .then_inc(yo_read, 1)
                dve.wait_ge(yd_made, 4 * t + 4)
                dve.wait_ge(yo_read, 2 * t + 2)
                for half in range(2):
                    part = slice(half * 512, half * 512 + 512)
                    last = nc.vector.tensor_tensor(ysum[:, part], ysum[:, part], bank[5 + half][:], ALU.add)
                last.then_inc(ysum_ready, 1)
                dve.wait_ge(ysum_ready, t + 1)
                dve.wait_ge(xskip_ready, t + 1)
                link(nc.vector.tensor_tensor(ysum, ysum, xskip, ALU.add))
                dve.wait_ge(z_ready, 2 * t + 2)
                dve.wait_ge(y_turned, t)
                dve.wait_ge(squares_ready, t)
                nc.vector.tensor_tensor(y, ysum, zs[:, par], ALU.mult).then_inc(y_ready, 1)
                dve.wait_ge(decayed, t + 1)
                for half, b in ((0, 4), (1, 7)):
                    part = slice(half * 512, half * 512 + 512)
                    dve.wait_ge(st_made, 2 * t + half + 1)
                    last = nc.vector.tensor_tensor(state[:, part], state[:, part], bank[b][:], ALU.add)
                last.then_inc(state_ready, 1)
                dve.wait_ge(y_turned, t + 1)
                dve.wait_ge(out_made, t)
                for half in range(2):
                    part = slice(4 * half, 4 * half + 4)
                    last = nc.vector.tensor_tensor(yT[:, part], bank[3 + half][:].rearrange("p (a b) -> p a b", b=P),
                                                   spread(norm[:, part], 2, P), ALU.mult)
                last.then_inc(yT_ready, 1)
                dve.wait_ge(squares_ready, t + 1)
                nc.vector.tensor_scalar(mean_eps, squares, 1.0 / INNER, EPS, ALU.mult, ALU.add).then_inc(mean_ready, 1)
                if front:
                    after = core.keep[:, bass.ds((turn + 1) % TURNS_PER_BATCH, 1)] if par else core.ones[:, 0:1]
                    convolve(link, t + 1, 1 - par, after)
                    time_steps(link, t + 1, 1 - par)
                dve.wait_ge(out_made, t + 1)
                dve.wait_ge(rinv_ready, t + 1)
                dve.wait_ge(stored, 16 * t)
                nc.vector.scalar_tensor_tensor(out=xo, in0=bank[7][:], scalar=rinv, in1=x[:, par],
                                               op0=ALU.mult, op1=ALU.add).then_inc(added, 1)

            dve.wait_ge(cleared, 3)
            dve.wait_ge(rows_here, 96)
            dve.wait_ge(a_exp, 1)
            nc.vector.tensor_scalar(a_row, a_row, -1.0, None, ALU.mult).then_inc(a_ready, 1)
            dve.wait_ge(a_ready, 1)
            link = Chain(dve, chains[0])
            layer_norm(link, 0, 0, 0)
            convolve(link, 0, 0, core.keep[:, 0:1])
            time_steps(link, 0, 0)
            layer_norm(link, 1, 1, 0)
            with dve.Fori(0, TURNS - 1) as i:
                link = Chain(dve, chains[1], i, 46)
                for par in range(2):
                    step(link, 2 * i + par, i, par, True)
                    layer_norm(link, 2 * i + par + 2, par, i + 1)
                link.end()
            link = Chain(dve, chains[2])
            step(link, TILES - 2, TURNS - 1, 0, True)
            step(link, TILES - 1, TURNS - 1, 1, False)

        @block.scalar
        def _(act):
            def by_chunk(v):
                return v.rearrange("p (a b) -> p a b", b=P)

            def rows_out(n):
                act.wait_ge(x_turned, n + 1)
                act.wait_ge(dt_made, n)
                nc.scalar.activation(xnT, by_chunk(bank[0][:]), ACT.Copy).then_inc(xnT_ready, 1)

            def conv_in(n, par, part):
                act.wait_ge(front_made, 5 * n + part + 1)
                act.wait_ge(conv_ready, n)
                c = slice(4 * part, min(4 * part + 4, CB))
                nc.scalar.activation(cin[par][:, c, halo:halo + P],
                                     by_chunk(bank[(1, 0, 1)[part]][:, 0:(c.stop - c.start) * P]), ACT.Copy)\
                    .then_inc(cin_ready, 1)

            def gate(n, par):
                for half in range(2):
                    act.wait_ge(front_made, 5 * n + 4 + half)
                    if not isinstance(n, int) or n >= 2:
                        act.wait_ge(y_ready, n - 1)
                    nc.scalar.activation(zs[:, par, half * 512:half * 512 + 512], bank[half][:], ACT.Silu)\
                        .then_inc(z_ready, 1)

            def conv_out(n, par):
                act.wait_ge(conv_ready, n + 1)
                if not isinstance(n, int) or n >= 2:
                    act.wait_ge(out_made, n - 1)
                for c in range(CB):
                    last = nc.scalar.activation(xc[:, par, c], conv[:, c], ACT.Silu, bias=tap_bias[:, c:c + 1])
                last.then_inc(xc_ready, 1)

            def e_mags(n):
                act.wait_ge(mag_ready, n + 1)
                act.wait_ge(da_ready, n)
                nc.scalar.activation(e_mag, mag, ACT.Exp, scale=-1.0).then_inc(e_mag_ready, 1)

            def decay(t, g):
                act.wait_ge(sums_made, 4 * t + g + 1)
                act.wait_ge(yd_made, 4 * t + (g - 1 if g >= 2 else 0))
                for r in range(4):
                    h = 4 * g + r
                    last = nc.scalar.activation(decays[:, g % 2, r], bank[3 + g % 2][:, r * P:r * P + P], ACT.Exp,
                                                bias=ncs[:, h:h + 1])
                last.then_inc(decays_ready, 1)

            def step(t, par, front):
                act.wait_ge(xs_turned, t + 1)
                act.wait_ge(xdt_ready, t)
                act.wait_ge(xskip_ready, t)
                for half in range(2):
                    nc.scalar.activation(xs[:, half * 512:half * 512 + 512], bank[3 + half][:], ACT.Copy)\
                        .then_inc(xs_ready, 1)
                act.wait_ge(small_made, t + 1)
                act.wait_ge(gap_ready, t)
                nc.scalar.activation(sums, small[:, CS:CS + 2 * H], ACT.Copy).then_inc(sums_ready, 1)
                act.wait_ge(st_made, 2 * t)
                nc.scalar.activation(b_rows, small[:, BROWS:BROWS + P], ACT.Copy).then_inc(b_ready, 1)
                act.wait_ge(carried_ready, t)
                nc.scalar.activation(from_start, small[:, CS:CS + 2 * H], ACT.Exp).then_inc(exps_ready, 1)
                act.wait_ge(gap_ready, t + 1)
                act.wait_ge(xlast_ready, t)
                nc.scalar.activation(to_end, gap, ACT.Exp).then_inc(to_end_ready, 1)
                if front:
                    rows_out(t + 1)
                decay(t, 0)
                if front:
                    conv_in(t + 1, 1 - par, 0)
                decay(t, 1)
                decay(t, 2)
                if front:
                    conv_in(t + 1, 1 - par, 1)
                decay(t, 3)
                if front:
                    conv_in(t + 1, 1 - par, 2)
                    gate(t + 1, 1 - par)
                act.wait_ge(y_ready, t + 1)
                act.wait_ge(mean_ready, t)
                nc.scalar.activation(xskip, y, ACT.Square, accum_out=squares).then_inc(squares_ready, 1)
                if front:
                    conv_out(t + 1, 1 - par)
                    e_mags(t + 1)

            act.wait_ge(rows_here, 96)
            act.wait_ge(cleared, 3)
            nc.scalar.activation(a_row, a_row, ACT.Exp).then_inc(a_exp, 1)
            rows_out(0)
            for part in range(3):
                conv_in(0, 0, part)
            gate(0, 0)
            conv_out(0, 0)
            e_mags(0)
            with act.Fori(0, TURNS - 1) as i:
                for par in range(2):
                    step(2 * i + par, par, True)
            step(TILES - 2, 0, True)
            step(TILES - 1, 1, False)

        @block.tensor
        def _(pe):
            def turn_rows(n):
                pe.wait_ge(xn_ready, n + 1)
                pe.wait_ge(z_ready, 2 * n)
                for k in range(KD):
                    last = nc.tensor.transpose(bank[0][:, k * P:k * P + P], xn[:, k * P:k * P + P], core.ident[:])
                last.then_inc(x_turned, 1)

            def channels(n, part):
                if part == 0:
                    pe.wait_ge(xnT_ready, n + 1)
                if part == 2:
                    pe.wait_ge(cin_ready, 3 * n + 1)
                for c in range(4 * part, min(4 * part + 4, CB)):
                    at = INNER + c * P
                    for k in range(KD):
                        last = nc.tensor.matmul(bank[(1, 0, 1)[part]][:, (c % 4) * P:(c % 4) * P + P],
                                                w_in[:, k, at:at + P], xnT[:, k], start=(k == 0), stop=(k == KD - 1))
                last.then_inc(front_made, 1)

            def gate_rows(n, half):
                pe.wait_ge(cin_ready, 3 * n + 2 + half)
                for k in range(KD):
                    last = nc.tensor.matmul(bank[half][:], xnT[:, k], w_in[:, k, half * 512:half * 512 + 512],
                                            start=(k == 0), stop=(k == KD - 1))
                last.then_inc(front_made, 1)

            def dt_rows(n):
                pe.wait_ge(mixed_ready, 4 * n)
                pe.wait_ge(exps_ready, n)
                pe.wait_ge(b_ready, n)
                for k in range(KD):
                    last = nc.tensor.matmul(small[:, DT:DT + H], xnT[:, k], w_in[:, k, INNER + XBC:WIN_COLS],
                                            start=(k == 0), stop=(k == KD - 1))
                last.then_inc(dt_made, 1)

            def running_sums(t, par, g):
                if g >= 2:
                    pe.wait_ge(decays_ready, 4 * t + g - 1)
                b = bank[3 + g % 2]
                nc.tensor.matmul(b[:], core.identb[:], core.ssd_mask[:].rearrange("p a b -> p (a b)"),
                                 start=True, stop=False)
                for r in range(4):
                    h = 4 * g + r
                    last = nc.tensor.matmul(b[:, r * P:r * P + P], da[:, par, h:h + 1].broadcast_to([P, P]),
                                            core.upto[:], start=False, stop=(r == 3))
                last.then_inc(sums_made, 1)

            def own_rows(t, g):
                pe.wait_ge(mixed_ready, 4 * t + g + 1)
                if g == 0:
                    pe.wait_ge(xdt_ready, t + 1)
                    pe.wait_ge(ysum_ready, t)
                for r in range(4):
                    h = 4 * g + r
                    last = nc.tensor.matmul(bank[5 + g // 2][:, (h % 8) * MHD:(h % 8 + 1) * MHD], decays[:, g % 2, r],
                                            xdt[:, h * MHD:h * MHD + MHD], start=True, stop=True)
                last.then_inc(yd_made, 1)

            def step(t, par, front):
                B, C = xc[:, par, KY], xc[:, par, KY + 1]
                if front:
                    turn_rows(t + 1)
                pe.wait_ge(xc_ready, t + 1)
                pe.wait_ge(yT_ready, t)
                for k in range(KY):
                    last = nc.tensor.transpose(bank[3 + k // 4][:, (k % 4) * P:(k % 4 + 1) * P], xc[:, par, k],
                                               core.ident[:])
                last.then_inc(xs_turned, 1)
                pe.wait_ge(da_ready, t + 1)
                nc.tensor.transpose(small[:, BROWS:BROWS + P], B, core.ident[:])
                nc.tensor.matmul(small[:, CS:CS + H], core.upto[:], da[:, par], start=True, stop=True)
                nc.tensor.matmul(small[:, SUM:SUM + H], core.ones[:], da[:, par], start=True, stop=True)
                nc.tensor.matmul(small[:, BC:BC + P], B, C, start=True, stop=True).then_inc(small_made, 1)
                pe.wait_ge(xs_ready, 2 * t + 2)
                running_sums(t, par, 0)
                running_sums(t, par, 1)
                if front:
                    channels(t + 1, 0)
                own_rows(t, 0)
                running_sums(t, par, 2)
                if front:
                    channels(t + 1, 1)
                own_rows(t, 1)
                running_sums(t, par, 3)
                if front:
                    channels(t + 1, 2)
                pe.wait_ge(state_ready, t)
                pe.wait_ge(added, t)
                nc.tensor.matmul(bank[7][:], C, state[:, 0:512], start=True, stop=True).then_inc(yo_made, 1)
                pe.wait_ge(decays_ready, 4 * t + 3)
                nc.tensor.matmul(bank[3][:], C, state[:, 512:1024], start=True, stop=True).then_inc(yo_made, 1)
                own_rows(t, 2)
                own_rows(t, 3)
                if front:
                    gate_rows(t + 1, 0)
                pe.wait_ge(xlast_ready, t + 1)
                pe.wait_ge(b_ready, t + 1)
                pe.wait_ge(decays_ready, 4 * t + 4)
                nc.tensor.matmul(bank[4][:], b_rows, xlast[:, 0:512], start=True, stop=True).then_inc(st_made, 1)
                pe.wait_ge(yo_read, 2 * t + 1)
                nc.tensor.matmul(bank[7][:], b_rows, xlast[:, 512:1024], start=True, stop=True).then_inc(st_made, 1)
                if front:
                    gate_rows(t + 1, 1)
                    dt_rows(t + 1)
                pe.wait_ge(y_ready, t + 1)
                pe.wait_ge(state_ready, t + 1)
                for k in range(KY):
                    last = nc.tensor.transpose(bank[3 + k // 4][:, (k % 4) * P:(k % 4 + 1) * P],
                                               y[:, k * P:k * P + P], core.ident[:])
                last.then_inc(y_turned, 1)
                pe.wait_ge(yT_ready, t + 1)
                for k in range(KY):
                    last = nc.tensor.matmul(bank[7][:], yT[:, k], w_out[:, k], start=(k == 0), stop=(k == KY - 1))
                last.then_inc(out_made, 1)

            pe.wait_ge(w_in_here, 16 * KD)
            turn_rows(0)
            for part in range(3):
                channels(0, part)
            gate_rows(0, 0)
            gate_rows(0, 1)
            dt_rows(0)
            pe.wait_ge(w_out_here, 16)
            pe.wait_ge(cleared, 3)
            with pe.Fori(0, TURNS - 1) as i:
                for par in range(2):
                    step(2 * i + par, par, True)
            step(TILES - 2, 0, True)
            step(TILES - 1, 1, False)


def hybrid_block(nc, x, w_qkv, w_out, in_w, conv_w, conv_b, a_log, d_skip, dt_bias, norm_w, out_w, gate, w1, w2, w2_tail, out):
    def tiles(rows):
        return rows[0:ROWS].rearrange("(t p) d -> t p d", p=P)

    with ExitStack() as ctx:
        core = Core(nc, ctx)
        mid = nc.dram_tensor("mid_rows", (ROWS + SPARE, D), F32).ap()
        xn_rows = nc.dram_tensor("normalised_rows", (ROWS + SPARE, D), F32).ap()
        make_constants(core, [rows[ROWS:ROWS + SPARE] for rows in (mid, xn_rows, out)])
        attention(core, tiles(x), tiles(mid), w_qkv, w_out, w1)
        experts(core, "moe_a", mid, xn_rows, gate, w1, w2, w2_tail)
        mamba(core, tiles(mid), tiles(out), in_w, out_w, conv_w, conv_b, a_log, d_skip, dt_bias, norm_w)
        experts(core, "moe_b", out, xn_rows, gate, w1, w2, w2_tail)


def _by_partition(w):
    import numpy as _np
    return _np.ascontiguousarray(w.T.reshape(-1, 128, w.shape[0]).transpose(1, 0, 2))


def kernel(**inputs):
    import numpy as _np
    import concourse.bacc as _bacc
    from concourse import mybir as _mybir
    from concourse.bass_utils import run_bass_kernel_spmd as _run

    a = {name: _np.asarray(v) for name, v in inputs.items()}
    w1, w2 = a["L0_ffn_w1"], a["L0_ffn_w2"]
    n_e, two_i, d = w1.shape
    inner = w2.shape[2]
    whole = inner // 128 * 128
    w1 = w1.transpose(2, 0, 1).reshape(d // 128, 128, n_e, two_i).transpose(1, 2, 0, 3).reshape(128, n_e, -1)
    w2 = w2.transpose(2, 0, 1)
    taps = a["L0_attn_b_conv_w"].shape[2]
    laid = {
        "x": a["L0_attn_a_x"].reshape(-1, d),
        "w_qkv": _by_partition(a["L0_attn_a_w_qkv"]),
        "w_out": _by_partition(a["L0_attn_a_w_out"]),
        "in_w": _by_partition(a["L0_attn_b_in_proj_w"]),
        "conv_w": a["L0_attn_b_conv_w"].reshape(-1, 128, taps).transpose(1, 0, 2),
        "conv_b": a["L0_attn_b_conv_b"].reshape(-1, 128).T,
        "a_log": a["L0_attn_b_A_log"],
        "d_skip": a["L0_attn_b_D"],
        "dt_bias": a["L0_attn_b_dt_bias"],
        "norm_w": a["L0_attn_b_norm_w"].reshape(-1, 128).T,
        "out_w": _by_partition(a["L0_attn_b_out_proj_w"]),
        "gate": _by_partition(a["L0_ffn_gate_w"]),
        "w1": w1,
        "w2": w2[:whole].reshape(whole // 128, 128, n_e, d).transpose(1, 2, 0, 3),
        "w2_tail": w2[whole:],
    }
    nc = _bacc.Bacc("TRN2", target_bir_lowering=False, num_devices=1)
    arrays, args = {}, []
    for name, v in laid.items():
        v = _np.ascontiguousarray(v)
        arrays[f"in_{name}_dram"] = v
        args.append(nc.dram_tensor(f"in_{name}_dram", v.shape, _mybir.dt.from_np(v.dtype), kind="ExternalInput").ap())
    rows = laid["x"].shape[0]
    args.append(nc.dram_tensor("out_dram", (rows + 128, d), _mybir.dt.float32, kind="ExternalOutput").ap())
    hybrid_block(nc, *args)
    r = _run(nc, [arrays], core_ids=[0])
    return r.results[0]["out_dram"][:rows].reshape(a["L0_attn_a_x"].shape)
```

```python
from contextlib import contextmanager
from contextlib import ExitStack

import concourse.bass as bass
from concourse import mybir

F32 = mybir.dt.float32
BF16 = mybir.dt.bfloat16
F32R = mybir.dt.float32r
I32 = mybir.dt.int32
U32 = mybir.dt.uint32
ALU = mybir.AluOpType
ACT = mybir.ActivationFunctionType
AX = mybir.AxisListType

P = 128
BATCH, SEQ, D = 2, 1024, 512
ROWS = BATCH * SEQ
TILES = ROWS // P
TURNS = TILES // 2
TURNS_PER_BATCH = TURNS // BATCH
KD = D // P
EPS = 1e-5
NEG = -1e30

HEADS, HD = 16, 32
HG = P // HD
WIN = P

EXPERTS, TOPK, INTER = 8, 2, 352
KI = -(-INTER // P)
LAST_I = INTER - (KI - 1) * P
SLOTS = -(-(TOPK * ROWS + EXPERTS * (P - 1)) // (2 * P)) * 2
SPARE = P
W1E = KD * 2 * INTER
W2E = KI * D

INNER, STATE, MHEADS, MHD, TAPS = 1024, 128, 16, 64, 4
BLK = 64
XBC = INNER + 2 * STATE
CB = XBC // P
KY = INNER // P
WIN_COLS = 2 * INNER + 2 * STATE + MHEADS


class Chain:

    def __init__(self, eng, sem, turn=0, per_turn=0):
        self.eng, self.sem, self.turn, self.per_turn, self.n = eng, sem, turn, per_turn, 0

    def __call__(self, ins):
        self.n += 1
        ins.then_inc(self.sem, 1)
        self.eng.wait_ge(self.sem, self.turn * self.per_turn + self.n)

    def end(self):
        assert self.n == self.per_turn, self.n


def after(eng, sem, n):
    if not isinstance(n, int) or n > 0:
        eng.wait_ge(sem, n)


def cut(arena, at, *shape):
    n = 1
    for s in shape:
        n *= s
    v = arena[:, at:at + n]
    if len(shape) == 2:
        v = v.rearrange("p (a b) -> p a b", b=shape[1])
    if len(shape) == 3:
        v = v.rearrange("p (a b c) -> p a b c", b=shape[1], c=shape[2])
    return v, at + n


def spread(ap, axis, n):
    v = ap.unsqueeze(axis)
    shape = list(v.shape)
    shape[axis] = n
    return v.broadcast_to(shape)


@contextmanager
def stage_semaphores(nc, tag):
    taken = []

    def sem(name):
        taken.append(nc.alloc_semaphore(name=f"{tag}_{name}"))
        return taken[-1]

    yield sem
    nc.clear_and_free_semaphores(taken)
    nc.all_engine_barrier()


class Core:

    def __init__(self, nc, ctx):
        self.nc, self.ctx = nc, ctx
        self.bank = [ctx.enter_context(nc.psum_tensor(f"bank{i}", [P, 512], F32)) for i in range(8)]

        def sb(name, shape, dt=F32):
            return ctx.enter_context(nc.sbuf_tensor(name, shape, dt))

        self.pool_dma = {tag: [ctx.enter_context(nc.semaphore(f"{tag}_{name}"))
                               for name in ("gathered0", "gathered1", "added")] for tag in ("moe_a", "moe_b")}
        self.ident = sb("ident", [P, P])
        self.identb = sb("identb", [P, P], BF16)
        self.zero = sb("zero", [P, 8])
        self.att_mask = sb("att_mask", [P, 3, 2 * P], BF16)
        self.ssd_mask = sb("ssd_mask", [P, MHEADS // 2, BLK], BF16)
        self.upto = sb("upto", [P, BLK])
        self.upto_own = sb("upto_own", [P, P])
        self.own = sb("own", [P, P])
        self.own_r = sb("own_r", [P, P], F32R)
        self.halves = sb("halves", [P, 2, INNER], F32R)
        self.in_block = sb("in_block", [P, 2, P])
        self.before = sb("before", [P, P], BF16)
        self.ones = sb("ones", [P, P])
        self.onesb = sb("onesb", [P, P], BF16)
        self.count = sb("count", [P, P])
        self.rowid = sb("rowid", [P, TILES])
        self.spareid = sb("spareid", [P, 1])
        self.mhalf = sb("mhalf", [P, 1])
        self.keep = sb("keep", [P, TURNS_PER_BATCH])
        left = (nc.sbuf_bytes_remaining - 64) // 4 // 8 * 8
        self.arena = sb("arena", [P, left])
        self.left = left
        self.w1_at, self.w2_at = 0, EXPERTS * W1E
        self.work_at = self.w2_at + EXPERTS * W2E
        self.kept_experts = 4
        self.other_at = self.kept_experts * W1E
        self.w1 = self.arena[:, 0:EXPERTS * W1E]
        self.w2 = self.arena[:, self.w2_at:self.work_at]


def make_constants(core, spare_rows):
    nc = core.nc
    with stage_semaphores(nc, "const") as sem, ExitStack() as ctx:
        made, base_made, zeroed = sem("made"), sem("base_made"), sem("spare_zeroed")
        zero_rows = core.arena[:, core.other_at:core.other_at + D]
        block = ctx.enter_context(nc.Block())

        @block.vector
        def _(dve):
            for ap, value in ((core.zero, 0.0), (core.ident, 0.0), (core.identb, 0.0), (core.ones, 1.0),
                              (core.onesb, 1.0), (core.att_mask, 0.0), (core.ssd_mask, 0.0), (core.in_block, 1.0),
                              (core.mhalf, -0.5), (core.keep, 1.0)):
                nc.vector.memset(ap[:], value)
            nc.vector.memset(zero_rows, 0.0).then_inc(base_made, 1)

        @block.gpsimd
        def _(pool):
            g = Chain(pool, made)
            pool.wait_ge(base_made, 1)
            for m in (core.ident, core.identb):
                g(nc.gpsimd.affine_select(out=m[:], in_=m[:], compare_op=ALU.not_equal, fill=1.0, base=0,
                                          pattern=[[-1, P]], channel_multiplier=1))
            g(nc.gpsimd.affine_select(out=core.before[:], in_=core.onesb[:], compare_op=ALU.is_gt, fill=0.0,
                                      base=0, pattern=[[1, P]], channel_multiplier=-1))
            for b in range(2):
                rows = slice(b * BLK, (b + 1) * BLK)
                m = core.ssd_mask[rows]
                g(nc.gpsimd.affine_select(out=m, in_=m, compare_op=ALU.is_ge, fill=NEG, base=0,
                                          pattern=[[0, MHEADS // 2], [1, BLK]], channel_multiplier=-1))
                g(nc.gpsimd.affine_select(out=core.upto[rows], in_=core.ones[rows, 0:BLK], compare_op=ALU.is_ge,
                                          fill=0.0, base=0, pattern=[[1, BLK]], channel_multiplier=-1))
                m = core.in_block[:, b]
                g(nc.gpsimd.affine_select(out=m, in_=m, compare_op=ALU.is_ge, fill=0.0, base=-b * BLK,
                                          pattern=[[0, P]], channel_multiplier=1))
                g(nc.gpsimd.affine_select(out=m, in_=m, compare_op=ALU.is_ge, fill=0.0, base=b * BLK + BLK - 1,
                                          pattern=[[0, P]], channel_multiplier=-1))
                g(nc.gpsimd.tensor_copy(core.own[:, b * BLK:(b + 1) * BLK], m[:, 0:BLK]))
                g(nc.gpsimd.tensor_copy(core.own_r[:, b * BLK:(b + 1) * BLK], m[:, 0:BLK]))
            g(nc.gpsimd.affine_select(out=core.upto_own[:], in_=core.own[:], compare_op=ALU.is_ge, fill=0.0,
                                      base=0, pattern=[[1, P]], channel_multiplier=-1))
            for which, own, prev in ((0, 0, None), (1, 0, 1), (2, 1, 0)):
                m = core.att_mask[:, which, own * P:own * P + P]
                g(nc.gpsimd.affine_select(out=m, in_=m, compare_op=ALU.is_ge, fill=NEG, base=0,
                                          pattern=[[-1, P]], channel_multiplier=1))
                if prev is not None:
                    m = core.att_mask[:, which, prev * P:prev * P + P]
                    g(nc.gpsimd.affine_select(out=m, in_=m, compare_op=ALU.is_ge, fill=NEG, base=0,
                                              pattern=[[1, P]], channel_multiplier=-1))
            g(nc.gpsimd.memset(core.att_mask[:, 0, P:2 * P], NEG))
            g(nc.gpsimd.memset(core.keep[:, 0:1], 0.0))
            g(nc.gpsimd.iota(core.count[:], [[1, P]], 0, 0, allow_small_or_imprecise_dtypes=True))
            g(nc.gpsimd.iota(core.rowid[:], [[P, TILES]], 0, 1, allow_small_or_imprecise_dtypes=True))
            g(nc.gpsimd.iota(core.spareid[:], [[0, 1]], ROWS, 1, allow_small_or_imprecise_dtypes=True))

        @block.sync
        def _(sp):
            sp.wait_ge(base_made, 1)
            for rows in spare_rows:
                sp.dma_start(rows, zero_rows).then_inc(zeroed, 16)
            sp.wait_ge(zeroed, 16 * len(spare_rows))


def attention(core, x_in, x_out, w_qkv, w_out, w1_dram):
    nc, bank = core.nc, core.bank
    arena, at = core.arena, core.other_at
    wqkv, at = cut(arena, at, KD, 3 * D)
    wo, at = cut(arena, at, KD, D)
    x, at = cut(arena, at, 2, D)
    xn, at = cut(arena, at, D)
    xnT, at = cut(arena, at, KD, P)
    qz = []
    for par in range(2):
        q, at = cut(arena, at, HG, KD, P)
        qz.append(q)
    kT, at = cut(arena, at, KD, 2, P)
    v, at = cut(arena, at, 2, D)
    probs, at = cut(arena, at, 2, HG, 2 * P)
    probsT, at = cut(arena, at, 2, 4, P)
    o, at = cut(arena, at, D)
    oT, at = cut(arena, at, KD, P)
    xo, at = cut(arena, at, D)
    xres, at = cut(arena, at, 2, D)
    st, at = cut(arena, at, 6)
    mv, at = cut(arena, at, 2)
    var_eps, at = cut(arena, at, 1)
    rstd, at = cut(arena, at, 1)
    nmax, at = cut(arena, at, HEADS)
    psum_p, at = cut(arena, at, HEADS)
    rinv, at = cut(arena, at, HEADS)
    assert at <= core.left
    score_banks = ((bank[2], bank[3]), (bank[4], bank[5]))
    with stage_semaphores(nc, "att") as sem, ExitStack() as ctx:
        weights_in = [sem(f"w{k}_in") for k in range(2)]
        x_loaded = [sem("x_loaded0"), sem("x_loaded1")]
        again_loaded = [sem("again_loaded0"), sem("again_loaded1")]
        experts_in = sem("experts_in")
        chains = [sem("chain_first"), sem("chain_loop"), sem("chain_last")]
        cleared = sem("cleared")
        var_ready, rstd_ready, xn_ready = sem("var_ready"), sem("rstd_ready"), sem("xn_ready")
        x_turned, xnT_ready = sem("x_turned"), sem("xnT_ready")
        q_made, k_made, v_made = sem("q_made"), sem("k_made"), sem("v_made")
        q_ready, k_ready, v_ready = sem("q_ready"), sem("k_ready"), sem("v_ready")
        scores_made, max_ready, probs_ready = sem("scores_made"), sem("max_ready"), sem("probs_ready")
        probs_turned, probsT_ready, pv_made = sem("probs_turned"), sem("probsT_ready"), sem("pv_made")
        o_ready, o_turned, oT_ready = sem("o_ready"), sem("o_turned"), sem("oT_ready")
        out_made, added, stored = sem("out_made"), sem("added"), sem("stored")
        block = ctx.enter_context(nc.Block())

        @block.sync
        def _(sp):
            for par in range(2):
                sp.dma_start(x[:, par], x_in[par]).then_inc(x_loaded[par], 16)
            sp.dma_start(wqkv, w_qkv).then_inc(weights_in[0], 16)
            sp.dma_start(wo, w_out).then_inc(weights_in[1], 16)
            for e in range(core.kept_experts):
                sp.dma_start(core.w1[:, e * W1E:(e + 1) * W1E], w1_dram[:, e]).then_inc(experts_in, 16)
            for par in range(2):
                sp.dma_start(xres[:, par], x_in[par]).then_inc(again_loaded[par], 16)

            def one(t):
                return slice(t, t + 1) if isinstance(t, int) else bass.ds(t, 1)

            def store(t, par):
                sp.wait_ge(added, t + 1)
                sp.dma_start(x_out[one(t)].rearrange("a p d -> p a d"), xo.unsqueeze(1)).then_inc(stored, 16)

            def load(t, par):
                sp.wait_ge(xn_ready, t - 1)
                sp.dma_start(x[:, par:par + 1], x_in[one(t)].rearrange("a p d -> p a d")).then_inc(x_loaded[par], 16)

            def load_again(t, par):
                sp.dma_start(xres[:, par:par + 1], x_in[one(t)].rearrange("a p d -> p a d"))                    .then_inc(again_loaded[par], 16)

            load(2, 0)
            load(3, 1)
            with sp.Fori(0, TURNS - 2) as i:
                for par in range(2):
                    t = 2 * i + par
                    store(t, par)
                    load_again(t + 2, par)
                    load(t + 4, par)
            for t in range(TILES - 4, TILES):
                store(t, t % 2)
                if t < TILES - 2:
                    load_again(t + 2, t % 2)
            sp.wait_ge(stored, 16 * TILES)
            sp.wait_ge(experts_in, 16 * core.kept_experts)

        @block.gpsimd
        def _(pool):
            nc.gpsimd.memset(qz[0], 0.0).then_inc(cleared, 1)
            nc.gpsimd.memset(qz[1], 0.0).then_inc(cleared, 1)
            nc.gpsimd.memset(kT, 0.0).then_inc(cleared, 1)
            nc.gpsimd.memset(v, 0.0).then_inc(cleared, 1)
            with pool.Fori(0, TILES) as t:
                pool.wait_ge(var_ready, t + 1)
                nc.gpsimd.tensor_tensor(rstd, var_eps, core.mhalf[:], ALU.pow).then_inc(rstd_ready, 1)

        @block.vector
        def _(dve):
            def statistics(link, n, par, turn):
                dve.wait_ge(x_loaded[par], 16 * turn + 16)
                link(nc.vector.bn_stats(st, x[:, par]))
                nc.vector.nop(nofuse=True)
                after(dve, xn_ready, n)
                nc.vector.nop(nofuse=True)
                link(nc.vector.bn_aggr(mv, st))
                nc.vector.tensor_scalar(var_eps, mv[:, 1:2], EPS, None, ALU.add).then_inc(var_ready, 1)

            def normalise(n, par):
                dve.wait_ge(rstd_ready, n + 1)
                after(dve, x_turned, n)
                nc.vector.tensor_scalar(xn, x[:, par], mv[:, 0:1], rstd, ALU.subtract, ALU.mult).then_inc(xn_ready, 1)

            def keys_out(n, par):
                dve.wait_ge(k_made, n + 1)
                after(dve, scores_made, 4 * n)
                nc.vector.tensor_copy(kT[:, :, par], bank[0][:].rearrange("p (a b) -> p a b", b=P)).then_inc(k_ready, 1)

            def row_max(t, g):
                dve.wait_ge(scores_made, 4 * t + g + 1)
                if g == 0:
                    after(dve, probs_ready, 4 * t)
                for pair in range(2):
                    last = nc.vector.tensor_reduce(
                        nmax[:, HG * g + 2 * pair:HG * g + 2 * pair + 2],
                        score_banks[g % 2][pair][:].rearrange("p (h j) -> p h j", h=2),
                        AX.X, ALU.max, negate=True)
                last.then_inc(max_ready, 1)

            def probs_out(t, g):
                for half, b in ((0, 6), (1, 1)):
                    dve.wait_ge(probs_turned, 8 * t + 2 * g + half + 1)
                    after(dve, pv_made, 4 * t + g)
                    nc.vector.tensor_copy(probsT[:, half], bank[b][:].rearrange("p (a b) -> p a b", b=P))\
                        .then_inc(probsT_ready, 1)

            def values_out(link, t):
                link(nc.vector.reciprocal(rinv, psum_p))
                dve.wait_ge(pv_made, 4 * t + 4)
                after(dve, o_turned, t)
                nc.vector.tensor_tensor(o.rearrange("p (h d) -> p h d", d=HD),
                                        bank[7][:].rearrange("p (h d) -> p h d", d=HD),
                                        spread(rinv, 2, HD), ALU.mult).then_inc(o_ready, 1)

            def add_input(t, par, turn):
                dve.wait_ge(again_loaded[par], 16 * turn + 16)
                dve.wait_ge(out_made, t + 1)
                after(dve, stored, 16 * t)
                nc.vector.tensor_tensor(xo, bank[1][:], xres[:, par], ALU.add).then_inc(added, 1)

            def step(link, t, par, turn, first=False, front=True, load=True):
                row_max(t, 0)
                row_max(t, 1)
                probs_out(t, 0)
                row_max(t, 2)
                if not first:
                    add_input(t - 1, 1 - par, turn if par else turn - 1)
                probs_out(t, 1)
                row_max(t, 3)
                if load:
                    statistics(link, t + 2, par, turn + 1)
                probs_out(t, 2)
                if front:
                    keys_out(t + 1, 1 - par)
                if load:
                    normalise(t + 2, par)
                probs_out(t, 3)
                values_out(link, t)

            dve.wait_ge(cleared, 4)
            link = Chain(dve, chains[0])
            statistics(link, 0, 0, 0)
            normalise(0, 0)
            keys_out(0, 0)
            statistics(link, 1, 1, 0)
            normalise(1, 1)
            link = Chain(dve, chains[1], 0, 6)
            for par in range(2):
                step(link, par, par, 0, first=(par == 0))
            link.end()
            with dve.Fori(1, TURNS - 1) as i:
                link = Chain(dve, chains[1], i, 6)
                for par in range(2):
                    step(link, 2 * i + par, par, i)
                link.end()
            link = Chain(dve, chains[2])
            step(link, TILES - 2, 0, TURNS - 1, load=False)
            step(link, TILES - 1, 1, TURNS - 1, front=False, load=False)
            add_input(TILES - 1, 1, TURNS - 1)

        @block.scalar
        def _(act):
            def by_chunk(v):
                return v.rearrange("p (a b) -> p a b", b=P)

            def rows_out(n):
                act.wait_ge(x_turned, n + 1)
                after(act, v_made, n)
                nc.scalar.activation(xnT, by_chunk(bank[0][:]), ACT.Copy).then_inc(xnT_ready, 1)

            def queries_out(n, par):
                act.wait_ge(q_made, n + 1)
                after(act, scores_made, 4 * (n - 1))
                for r in range(HG):
                    rows = slice(HD * r, HD * r + HD)
                    last = nc.scalar.activation(qz[par][rows, r], by_chunk(bank[0][rows, :]), ACT.Copy,
                                                scale=float(HD) ** -0.5)
                last.then_inc(q_ready, 1)

            def new_values_out(n, par):
                act.wait_ge(v_made, n + 1)
                after(act, pv_made, 4 * n)
                nc.scalar.activation(v[:, par], bank[0][:], ACT.Copy).then_inc(v_ready, 1)

            def exponentials(t, g):
                act.wait_ge(max_ready, 4 * t + g + 1)
                if g == 0:
                    after(act, o_ready, t)
                after(act, probs_turned, 8 * t + 2 * (g - 1))
                for r in range(HG):
                    h = HG * g + r
                    last = nc.scalar.activation(
                        probs[:, g % 2, r], score_banks[g % 2][r // 2][:, (r % 2) * 2 * P:(r % 2 + 1) * 2 * P],
                        ACT.Exp, bias=nmax[:, h:h + 1], accum_out=psum_p[:, h:h + 1])
                last.then_inc(probs_ready, 1)

            def o_out(t):
                act.wait_ge(o_turned, t + 1)
                after(act, out_made, t)
                nc.scalar.activation(oT, by_chunk(bank[6][:]), ACT.Copy).then_inc(oT_ready, 1)

            def step(t, par, first=False, front=True):
                exponentials(t, 0)
                if front:
                    rows_out(t + 1)
                exponentials(t, 1)
                if not first:
                    o_out(t - 1)
                if front:
                    queries_out(t + 1, 1 - par)
                exponentials(t, 2)
                exponentials(t, 3)
                if front:
                    new_values_out(t + 1, 1 - par)

            act.wait_ge(cleared, 4)
            rows_out(0)
            queries_out(0, 0)
            new_values_out(0, 0)
            for par in range(2):
                step(par, par, first=(par == 0))
            with act.Fori(1, TURNS - 1) as i:
                for par in range(2):
                    step(2 * i + par, par)
            step(TILES - 2, 0)
            step(TILES - 1, 1, front=False)
            o_out(TILES - 1)

        @block.tensor
        def _(pe):
            def turn_rows(n):
                pe.wait_ge(xn_ready, n + 1)
                after(pe, v_ready, n)
                for k in range(KD):
                    last = nc.tensor.transpose(bank[0][:, k * P:k * P + P], xn[:, k * P:k * P + P], core.ident[:])
                last.then_inc(x_turned, 1)

            def channels(n, first, free, done):
                pe.wait_ge(free, n + 1)
                for c in range(KD):
                    for k in range(KD):
                        last = nc.tensor.matmul(bank[0][:, c * P:c * P + P],
                                                wqkv[:, k, first + c * P:first + c * P + P], xnT[:, k],
                                                start=(k == 0), stop=(k == KD - 1))
                last.then_inc(done, 1)

            def queries(n):
                channels(n, 0, xnT_ready, q_made)

            def keys(n):
                channels(n, D, q_ready, k_made)

            def new_values(n):
                pe.wait_ge(k_ready, n + 1)
                for k in range(KD):
                    last = nc.tensor.matmul(bank[0][:], xnT[:, k], wqkv[:, k, 2 * D:3 * D],
                                            start=(k == 0), stop=(k == KD - 1))
                last.then_inc(v_made, 1)

            def scores(t, par, turn, g):
                if g == 0:
                    pe.wait_ge(q_ready, t + 1)
                    pe.wait_ge(k_ready, t + 1)
                after(pe, probs_ready, 4 * t + g - 1)
                for r in range(HG):
                    out = score_banks[g % 2][r // 2][:, (r % 2) * 2 * P:(r % 2 + 1) * 2 * P]
                    if par == 0:
                        which = 1 - (TURNS_PER_BATCH - turn % TURNS_PER_BATCH) // TURNS_PER_BATCH
                        mask = core.att_mask[:, bass.ds(which, 1)].rearrange("p a j -> p (a j)")
                    else:
                        mask = core.att_mask[:, 2]
                    nc.tensor.matmul(out, core.identb[:], mask, start=True, stop=False)
                    last = nc.tensor.matmul(out, qz[par][:, r, g], kT[:, g].rearrange("p a j -> p (a j)"),
                                            start=False, stop=True)
                last.then_inc(scores_made, 1)

            def values(t, g):
                pe.wait_ge(probs_ready, 4 * t + g + 1)
                if g == 0:
                    pe.wait_ge(v_ready, t + 1)
                for half, b in ((0, 6), (1, 1)):
                    if g == 1:
                        after(pe, added if half else oT_ready, t)
                    for j in range(4):
                        last = nc.tensor.transpose(bank[b][:, j * P:j * P + P],
                                                   probs[:, g % 2, 2 * half + j // 2, (j % 2) * P:(j % 2 + 1) * P],
                                                   core.ident[:])
                    last.then_inc(probs_turned, 1)
                if g == 0:
                    after(pe, o_ready, t)
                for half in range(2):
                    pe.wait_ge(probsT_ready, 8 * t + 2 * g + half + 1)
                    for r in range(2):
                        h = HG * g + 2 * half + r
                        for s in range(2):
                            last = nc.tensor.matmul(bank[7][:, h * HD:h * HD + HD], probsT[:, half, 2 * r + s],
                                                    v[:, s, h * HD:h * HD + HD], start=(s == 0), stop=(s == 1))
                last.then_inc(pv_made, 1)

            def turn_o(t):
                pe.wait_ge(o_ready, t + 1)
                for k in range(KD):
                    last = nc.tensor.transpose(bank[6][:, k * P:k * P + P], o[:, k * P:k * P + P], core.ident[:])
                last.then_inc(o_turned, 1)

            def output(t):
                pe.wait_ge(oT_ready, t + 1)
                for k in range(KD):
                    last = nc.tensor.matmul(bank[1][:], oT[:, k], wo[:, k], start=(k == 0), stop=(k == KD - 1))
                last.then_inc(out_made, 1)

            def step(t, par, turn, first=False, front=True):
                scores(t, par, turn, 0)
                scores(t, par, turn, 1)
                if front:
                    turn_rows(t + 1)
                values(t, 0)
                if not first:
                    turn_o(t - 1)
                if front:
                    queries(t + 1)
                scores(t, par, turn, 2)
                if not first:
                    output(t - 1)
                values(t, 1)
                scores(t, par, turn, 3)
                if front:
                    keys(t + 1)
                values(t, 2)
                if front:
                    new_values(t + 1)
                values(t, 3)

            pe.wait_ge(weights_in[0], 16)
            pe.wait_ge(weights_in[1], 16)
            turn_rows(0)
            queries(0)
            keys(0)
            new_values(0)
            for par in range(2):
                step(par, par, 0, first=(par == 0))
            with pe.Fori(1, TURNS - 1) as i:
                for par in range(2):
                    step(2 * i + par, par, i)
            step(TILES - 2, 0, TURNS - 1)
            step(TILES - 1, 1, TURNS - 1, front=False)
            turn_o(TILES - 1)
            output(TILES - 1)


def experts(core, tag, x_rows, xn_rows, gate, w1_dram, w2_dram, w2_tail):
    nc, bank, arena = core.nc, core.bank, core.arena
    gate_sb, at = cut(arena, core.work_at, KD, EXPERTS)
    index, at = cut(arena, at, SLOTS)
    weight, at = cut(arena, at, SLOTS)
    owner, at = cut(arena, at, SLOTS)
    index, owner = index.bitcast(U32), owner.bitcast(I32)
    stage_at = at
    with stage_semaphores(nc, tag) as sem:
        gate_in, rest_in, tail_in = sem("gate_in"), sem("rest_in"), sem("w2_in")
        score_rows(core, sem, x_rows, xn_rows, gate_sb, gate, w1_dram, w2_dram, w2_tail, gate_in, rest_in, tail_in,
                   stage_at)
        sort_rows(core, sem, index, weight, owner, stage_at)
        run_slots(core, tag, sem, x_rows, xn_rows, index, weight, owner, rest_in, tail_in, stage_at)


def score_rows(core, sem, x_rows, xn_rows, gate_sb, gate, w1_dram, w2_dram, w2_tail, gate_in, rest_in, tail_in, at):
    nc, bank, arena = core.nc, core.bank, core.arena
    x_in = x_rows.rearrange("(t p) d -> t p d", p=P)
    xn_out = xn_rows.rearrange("(t p) d -> t p d", p=P)
    x, at = cut(arena, at, 2, D)
    xn, at = cut(arena, at, 2, D)
    xnT, at = cut(arena, at, KD, P)
    st, at = cut(arena, at, 6)
    mv, at = cut(arena, at, 2)
    var_eps, at = cut(arena, at, 1)
    rstd, at = cut(arena, at, 1)
    assert at <= core.left
    x_loaded = [sem("x_loaded0"), sem("x_loaded1")]
    xn_stored = [sem("xn_stored0"), sem("xn_stored1")]
    chain = sem("norm_chain")
    var_ready, rstd_ready, xn_ready = sem("var_ready"), sem("rstd_ready"), sem("xn_ready")
    x_turned, xnT_ready, logits_made = sem("x_turned"), sem("xnT_ready"), sem("logits_made")
    with nc.Block() as block:
        @block.sync
        def _(sp):
            for par in range(2):
                sp.dma_start(x[:, par], x_in[par]).then_inc(x_loaded[par], 16)
            sp.dma_start(gate_sb, gate).then_inc(gate_in, 16)
            with sp.Fori(0, TURNS) as i:
                for par in range(2):
                    sp.wait_ge(xn_ready, 2 * i + par + 1)
                    sp.dma_start(xn_out[bass.ds(2 * i + par, 1)].rearrange("a p d -> p a d"),
                                 xn[:, par:par + 1]).then_inc(xn_stored[par], 16)
                    sp.dma_start(x[:, par:par + 1], x_in[bass.ds((2 * i + 2 + par) % (TILES + 1), 1)]
                                 .rearrange("a p d -> p a d")).then_inc(x_loaded[par], 16)
            for par in range(2):
                sp.wait_ge(xn_stored[par], 16 * TURNS)
                sp.wait_ge(x_loaded[par], 16 * (TURNS + 1))

        @block.gpsimd
        def _(pool):
            with pool.Fori(0, TURNS) as i:
                for par in range(2):
                    pool.wait_ge(var_ready, 2 * i + par + 1)
                    nc.gpsimd.tensor_tensor(rstd, var_eps, core.mhalf[:], ALU.pow).then_inc(rstd_ready, 1)

        @block.vector
        def _(dve):
            with dve.Fori(0, TURNS) as i:
                link = Chain(dve, chain, i, 4)
                for par in range(2):
                    t = 2 * i + par
                    dve.wait_ge(x_loaded[par], 16 * i + 16)
                    link(nc.vector.bn_stats(st, x[:, par]))
                    nc.vector.nop(nofuse=True)
                    link(nc.vector.bn_aggr(mv, st))
                    nc.vector.tensor_scalar(var_eps, mv[:, 1:2], EPS, None, ALU.add).then_inc(var_ready, 1)
                    dve.wait_ge(rstd_ready, t + 1)
                    after(dve, x_turned, t)
                    after(dve, xn_stored[par], 16 * i)
                    nc.vector.tensor_scalar(xn[:, par], x[:, par], mv[:, 0:1], rstd, ALU.subtract, ALU.mult)\
                        .then_inc(xn_ready, 1)
                link.end()

        @block.scalar
        def _(act):
            for e in range(core.kept_experts, EXPERTS):
                act.dma_start(core.w1[:, e * W1E:(e + 1) * W1E], w1_dram[:, e]).then_inc(rest_in, 16)
            w2 = core.w2.rearrange("p (e k d) -> p e k d", e=EXPERTS, k=KI)
            act.dma_start(w2[:, :, 0:KI - 1], w2_dram).then_inc(tail_in, 16)
            act.dma_start(w2[0:LAST_I, :, KI - 1], w2_tail).then_inc(tail_in, 16)
            with act.Fori(0, TURNS) as i:
                for par in range(2):
                    t = 2 * i + par
                    act.wait_ge(x_turned, t + 1)
                    act.wait_ge(logits_made, t)
                    nc.scalar.activation(xnT, bank[par][:].rearrange("p (a b) -> p a b", b=P), ACT.Copy)\
                        .then_inc(xnT_ready, 1)

        @block.tensor
        def _(pe):
            pe.wait_ge(gate_in, 16)
            with pe.Fori(0, TURNS) as i:
                for par in range(2):
                    t = 2 * i + par
                    pe.wait_ge(xn_ready, t + 1)
                    pe.wait_ge(xnT_ready, t)
                    for k in range(KD):
                        last = nc.tensor.transpose(bank[par][:, k * P:k * P + P], xn[:, par, k * P:k * P + P],
                                                   core.ident[:])
                    last.then_inc(x_turned, 1)
                    pe.wait_ge(xnT_ready, t + 1)
                    for k in range(KD):
                        last = nc.tensor.matmul(bank[7][:, bass.ds(EXPERTS * t, EXPERTS)], xnT[:, k], gate_sb[:, k],
                                                start=(k == 0), stop=(k == KD - 1))
                    last.then_inc(logits_made, 1)


def sort_rows(core, sem, index, weight, owner, at):
    nc, bank, arena = core.nc, core.bank, core.arena
    E, T, K = EXPERTS, TILES, TOPK
    logits, at = cut(arena, at, T, E)
    best, at = cut(arena, at, T, 8)
    which, at = cut(arena, at, T, 8)
    which_f, at = cut(arena, at, T, K)
    chosen, at = cut(arena, at, K, T * E)
    both, at = cut(arena, at, (T + 1) * E)
    both = both.bitcast(BF16)[:, 0:(T + 1) * E].rearrange("p (t e) -> p t e", e=E)
    gap, at = cut(arena, at, T)
    gap_exp, at = cut(arena, at, T)
    den, at = cut(arena, at, T)
    w, at = cut(arena, at, K, T)
    need, at = cut(arena, at, E)
    need_i, at = cut(arena, at, E)
    slots_i, at = cut(arena, at, E)
    slots, at = cut(arena, at, E)
    end, at = cut(arena, at, E)
    start, at = cut(arena, at, E)
    place, at = cut(arena, at, T * E)
    picked, at = cut(arena, at, K, T * E)
    entry, at = cut(arena, at, K * T)
    entry_i, at = cut(arena, at, K * T)
    slot_i, at = cut(arena, at, K * T)
    spot_i, at = cut(arena, at, K * T)
    slot, at = cut(arena, at, K * T)
    spot, at = cut(arena, at, K * T)
    at_spot, at = cut(arena, at, K * T, P)
    by_slot, at = cut(arena, at, 3, K * T, SLOTS)
    empty, at = cut(arena, at, SLOTS)
    index_f, at = cut(arena, at, SLOTS)
    past, at = cut(arena, at, SLOTS, E)
    owner_f, at = cut(arena, at, SLOTS)
    assert at <= core.left
    chain = sem("sort_chain")
    both_ready, ranks_made, gap_ready, exp_ready = sem("both"), sem("ranks"), sem("gap"), sem("exp")
    tables_ready, lists_made, done = sem("tables"), sem("lists"), sem("sorted")
    with nc.Block() as block:
        @block.vector
        def _(dve):
            link = Chain(dve, chain)
            link(nc.vector.tensor_copy(logits.rearrange("p t e -> p (t e)"), bank[7][:, 0:T * E]))
            for t in range(T):
                last = nc.vector.max(best[:, t], logits[:, t])
            link(last)
            for t in range(T):
                last = nc.vector.max_index(which.bitcast(U32)[:, t], best[:, t], logits[:, t])
            link(last)
            nc.vector.tensor_tensor(gap, best[:, :, 1], best[:, :, 0], ALU.subtract).then_inc(gap_ready, 1)
            link(nc.vector.tensor_copy(which_f, which.bitcast(U32)[:, :, 0:K]))
            for k in range(K):
                last = nc.vector.tensor_tensor(chosen[:, k].rearrange("p (t e) -> p t e", e=E),
                                               spread(core.count[:, 0:E], 1, T), spread(which_f[:, :, k], 2, E),
                                               ALU.is_equal)
            link(last)
            link(nc.vector.memset(both[:, T], 0.0))
            nc.vector.tensor_tensor(both[:, 0:T].rearrange("p t e -> p (t e)"), chosen[:, 0], chosen[:, 1], ALU.add)\
                .then_inc(both_ready, 1)
            dve.wait_ge(exp_ready, 1)
            link(nc.vector.tensor_scalar(den, gap_exp, 1.0, None, ALU.add))
            link(nc.vector.reciprocal(w[:, 0], den))
            link(nc.vector.tensor_tensor(w[:, 1], gap_exp, w[:, 0], ALU.mult))
            dve.wait_ge(ranks_made, 1)
            link(nc.vector.tensor_scalar(need, bank[0][:, T * E:(T + 1) * E], float(P - 1), None, ALU.add))
            link(nc.vector.tensor_copy(need_i.bitcast(I32), need))
            link(nc.vector.tensor_scalar(slots_i.bitcast(I32), need_i.bitcast(I32), 7, None, ALU.logical_shift_right))
            link(nc.vector.tensor_copy(slots, slots_i.bitcast(I32)))
            link(nc.vector.tensor_tensor_scan(end, slots, core.zero[:, 0:E], 0.0, ALU.add, ALU.add))
            link(nc.vector.tensor_tensor(start, end, slots, ALU.subtract))
            link(nc.vector.tensor_scalar(start, start, float(P), None, ALU.mult))
            link(nc.vector.tensor_tensor(place.rearrange("p (t e) -> p t e", e=E),
                                         bank[0][:, 0:T * E].rearrange("p (t e) -> p t e", e=E),
                                         spread(start, 1, T), ALU.add))
            link(nc.vector.tensor_tensor(picked, chosen, spread(place, 1, K), ALU.mult))
            link(nc.vector.tensor_reduce(entry, picked.rearrange("p k (t e) -> p (k t) e", e=E), AX.X, ALU.add))
            link(nc.vector.tensor_copy(entry_i.bitcast(I32), entry))
            link(nc.vector.tensor_scalar(slot_i.bitcast(I32), entry_i.bitcast(I32), 7, None, ALU.logical_shift_right))
            link(nc.vector.tensor_scalar(spot_i.bitcast(I32), entry_i.bitcast(I32), P - 1, None, ALU.bitwise_and))
            link(nc.vector.tensor_copy(slot, slot_i.bitcast(I32)))
            link(nc.vector.tensor_copy(spot, spot_i.bitcast(I32)))
            link(nc.vector.tensor_tensor(at_spot, spread(core.count[:], 1, K * T), spread(spot, 2, P), ALU.is_equal))
            link(nc.vector.tensor_tensor(by_slot[:, 2], spread(core.count[:, 0:SLOTS], 1, K * T),
                                         spread(slot, 2, SLOTS), ALU.is_equal))
            for k in range(K):
                part = slice(k * T, (k + 1) * T)
                link(nc.vector.tensor_tensor(by_slot[:, 0, part], by_slot[:, 2, part],
                                             spread(core.rowid[:], 2, SLOTS), ALU.mult))
            for k in range(K):
                part = slice(k * T, (k + 1) * T)
                last = nc.vector.tensor_tensor(by_slot[:, 1, part], by_slot[:, 2, part],
                                               spread(w[:, k], 2, SLOTS), ALU.mult)
            last.then_inc(tables_ready, 1)
            link(nc.vector.tensor_tensor(past, spread(core.count[:, 0:SLOTS], 2, E), spread(end, 1, SLOTS), ALU.is_ge))
            link(nc.vector.tensor_reduce(owner_f, past, AX.X, ALU.add))
            link(nc.vector.tensor_scalar(owner_f, owner_f, float(E - 1), None, ALU.min))
            link(nc.vector.tensor_copy(owner, owner_f))
            dve.wait_ge(lists_made, 1)
            link(nc.vector.tensor_scalar(empty, bank[1][:, 2 * SLOTS:3 * SLOTS], -1.0, 1.0, ALU.mult, ALU.add))
            link(nc.vector.scalar_tensor_tensor(out=index_f, in0=empty, scalar=core.spareid[:], in1=bank[1][:, 0:SLOTS],
                                                op0=ALU.mult, op1=ALU.add))
            link(nc.vector.tensor_copy(index, index_f))
            link(nc.vector.tensor_copy(weight, bank[1][:, SLOTS:2 * SLOTS]))

        @block.scalar
        def _(act):
            act.wait_ge(gap_ready, 1)
            nc.scalar.activation(gap_exp, gap, ACT.Exp).then_inc(exp_ready, 1)

        @block.tensor
        def _(pe):
            pe.wait_ge(both_ready, 1)
            nc.tensor.matmul(bank[0][:, 0:(T + 1) * E], core.before[:], both.rearrange("p t e -> p (t e)"),
                             start=True, stop=False)
            for t in range(T):
                last = nc.tensor.matmul(bank[0][:, (t + 1) * E:(T + 1) * E].rearrange("p (t e) -> p t e", e=E),
                                        core.onesb[:], spread(both[:, t], 1, T - t), start=False, stop=(t == T - 1))
            last.then_inc(ranks_made, 1)
            pe.wait_ge(tables_ready, 1)
            for j in range(K * T):
                last = nc.tensor.matmul(bank[1][:, 0:3 * SLOTS].rearrange("p (c s) -> p c s", c=3), at_spot[:, j],
                                        by_slot[:, :, j], start=(j == 0), stop=(j == K * T - 1))
            last.then_inc(lists_made, 1)


def run_slots(core, tag, sem, x_rows, xn_rows, index, weight, owner, rest_in, tail_in, at):
    nc, bank, arena = core.nc, core.bank, core.arena
    rows, at = cut(arena, at, 2, D)
    rowsT, at = cut(arena, at, 2, KD * P)
    silu, at = cut(arena, at, 2, INTER)
    act_sb, at = cut(arena, at, INTER)
    actT, at = cut(arena, at, KI, P)
    y, at = cut(arena, at, 2, D)
    from_rows, at = cut(arena, at, 2)
    to_rows, at = cut(arena, at, 1)
    from_rows, to_rows = from_rows.bitcast(U32), to_rows.bitcast(U32)
    assert at <= core.left
    w1 = core.w1.rearrange("p (e n) -> p e n", e=EXPERTS)
    w2 = core.w2.rearrange("p (e n) -> p e n", e=EXPERTS)
    picked, placed = sem("index_read"), sem("index_to")
    *gathered, added = core.pool_dma[tag]
    rows_turned, rowsT_ready, up_made, silu_ready = sem("rows_turned"), sem("rowsT_ready"), sem("up"), sem("silu")
    act_ready, act_turned, actT_ready = sem("act_ready"), sem("act_turned"), sem("actT_ready")
    y_made, y_ready = sem("y_made"), sem("y_ready")
    turns = SLOTS // 2
    with nc.Block() as block:
        @block.gpsimd
        def _(pool):
            def gather(s, par, turn):
                if turn is not None:
                    pool.wait_ge(rows_turned, s - 1)
                    nc.gpsimd.nop(nofuse=True)
                nc.gpsimd.tensor_copy(from_rows[:, par:par + 1], index[:, bass.ds(s, 1)]).then_inc(picked, 1)
                pool.wait_ge(picked, s + 1)
                nc.gpsimd.nop(nofuse=True)
                nc.gpsimd.indirect_dma_start(
                    out=rows[:, par], out_offset=None, in_=xn_rows,
                    in_offset=bass.IndirectOffsetOnAxis(ap=from_rows[:, par:par + 1], axis=0))\
                    .then_inc(gathered[par], 16)

            def add(s, par):
                pool.wait_ge(added, 16 * s)
                nc.gpsimd.nop(nofuse=True)
                nc.gpsimd.tensor_copy(to_rows, index[:, bass.ds(s, 1)]).then_inc(placed, 1)
                pool.wait_ge(placed, s + 1)
                pool.wait_ge(y_ready, s + 1)
                nc.gpsimd.nop(nofuse=True)
                nc.gpsimd.indirect_dma_start(
                    out=x_rows, out_offset=bass.IndirectOffsetOnAxis(ap=to_rows, axis=0),
                    in_=y[:, par], in_offset=None, compute_op=ALU.add).then_inc(added, 16)

            for par in range(2):
                gather(par, par, None)
            with pool.Fori(0, turns - 1) as i:
                for par in range(2):
                    gather(2 * i + 2 + par, par, i + 1)
                    add(2 * i + par, par)
            for par in range(2):
                add(SLOTS - 2 + par, par)
            pool.wait_ge(added, 16 * SLOTS)

        def turned(act, s, par):
            act.wait_ge(rows_turned, s + 1)
            if not isinstance(s, int) or s >= 2:
                act.wait_ge(up_made, s - 1)
            nc.scalar.activation(rowsT[:, par], bank[0][:], ACT.Copy).then_inc(rowsT_ready, 1)

        def gated(act, s, par):
            act.wait_ge(up_made, s + 1)
            act.wait_ge(act_ready, s)
            nc.scalar.activation(silu[:, par], bank[1 + 2 * par][:, 0:INTER], ACT.Silu).then_inc(silu_ready, 1)

        def result(act, s, par):
            act.wait_ge(y_made, s + 1)
            act.wait_ge(added, 16 * s)
            nc.scalar.activation(y[:, par], bank[6][:], ACT.Copy).then_inc(y_ready, 1)

        @block.scalar
        def _(act):
            turned(act, 0, 0)
            turned(act, 1, 1)
            gated(act, 0, 0)
            with act.Fori(0, turns - 1) as i:
                for par in range(2):
                    s = 2 * i + par
                    gated(act, s + 1, 1 - par)
                    turned(act, s + 2, par)
                    result(act, s, par)
            gated(act, SLOTS - 1, 1)
            result(act, SLOTS - 2, 0)
            result(act, SLOTS - 1, 1)

        def product(dve, s, par):
            dve.wait_ge(silu_ready, s + 1)
            dve.wait_ge(act_turned, s)
            nc.vector.scalar_tensor_tensor(out=act_sb, in0=silu[:, par], scalar=weight[:, bass.ds(s, 1)],
                                           in1=bank[2 + 2 * par][:, 0:INTER], op0=ALU.mult, op1=ALU.mult)\
                .then_inc(act_ready, 1)

        def act_out(dve, s):
            dve.wait_ge(act_turned, s + 1)
            dve.wait_ge(y_made, s)
            nc.vector.tensor_copy(actT[:, 0:KI - 1], bank[5][:, 0:(KI - 1) * P].rearrange("p (a b) -> p a b", b=P))
            nc.vector.tensor_copy(actT[0:LAST_I, KI - 1], bank[5][0:LAST_I, (KI - 1) * P:KI * P])\
                .then_inc(actT_ready, 1)

        @block.vector
        def _(dve):
            product(dve, 0, 0)
            with dve.Fori(0, turns - 1) as i:
                for par in range(2):
                    s = 2 * i + par
                    act_out(dve, s)
                    product(dve, s + 1, 1 - par)
            act_out(dve, SLOTS - 2)
            product(dve, SLOTS - 1, 1)
            act_out(dve, SLOTS - 1)

        @block.tensor
        def _(pe):
            def turn(s, par, i):
                pe.wait_ge(gathered[par], 16 * i + 16)
                pe.wait_ge(rowsT_ready, s)
                for k in range(KD):
                    last = nc.tensor.transpose(bank[0][:, k * P:k * P + P], rows[:, par, k * P:k * P + P],
                                               core.ident[:])
                last.then_inc(rows_turned, 1)

            def up(s, par):
                e = pe.value_load(owner[0:1, bass.ds(s, 1)], min_val=0, max_val=EXPERTS - 1)
                pe.wait_ge(rowsT_ready, s + 1)
                if not isinstance(s, int) or s >= 1:
                    pe.wait_ge(act_ready, s - 1)
                for part in range(2):
                    for k in range(KD):
                        at = (2 * k + part) * INTER
                        last = nc.tensor.matmul(bank[1 + 2 * par + part][:, 0:INTER], rowsT[:, par, k * P:k * P + P],
                                                w1[:, bass.ds(e, 1), at:at + INTER].rearrange("p a n -> p (a n)"),
                                                start=(k == 0), stop=(k == KD - 1))
                last.then_inc(up_made, 1)

            def turn_act(s):
                pe.wait_ge(act_ready, s + 1)
                pe.wait_ge(actT_ready, s)
                for k in range(KI):
                    n = P if k < KI - 1 else LAST_I
                    last = nc.tensor.transpose(bank[5][0:n, k * P:k * P + P], act_sb[:, k * P:k * P + n], core.ident[:])
                last.then_inc(act_turned, 1)

            def down(s):
                e = pe.value_load(owner[0:1, bass.ds(s, 1)], min_val=0, max_val=EXPERTS - 1)
                pe.wait_ge(actT_ready, s + 1)
                pe.wait_ge(y_ready, s)
                for k in range(KI):
                    n = P if k < KI - 1 else LAST_I
                    last = nc.tensor.matmul(bank[6][:], actT[0:n, k],
                                            w2[0:n, bass.ds(e, 1), k * D:k * D + D].rearrange("p a n -> p (a n)"),
                                            start=(k == 0), stop=(k == KI - 1))
                last.then_inc(y_made, 1)

            turn(0, 0, 0)
            pe.wait_ge(rest_in, 16 * (EXPERTS - core.kept_experts))
            pe.wait_ge(tail_in, 32)
            up(0, 0)
            turn(1, 1, 0)
            with pe.Fori(0, turns - 1) as i:
                for par in range(2):
                    s = 2 * i + par
                    up(s + 1, 1 - par)
                    turn_act(s)
                    turn(s + 2, par, i + 1)
                    down(s)
            up(SLOTS - 1, 1)
            turn_act(SLOTS - 2)
            down(SLOTS - 2)
            turn_act(SLOTS - 1)
            down(SLOTS - 1)


def mamba(core, x_in, x_out, in_w, out_w, conv_w, conv_b, a_log, d_skip, dt_bias, norm_w):
    nc, bank, arena = core.nc, core.bank, core.arena
    H = MHEADS
    halo = TAPS - 1
    at = core.other_at
    w_in, at = cut(arena, at, KD, WIN_COLS)
    w_out, at = cut(arena, at, KY, D)
    taps, at = cut(arena, at, CB, TAPS)
    tap_bias, at = cut(arena, at, CB)
    norm, at = cut(arena, at, KY)
    a_row, at = cut(arena, at, H)
    d_row, at = cut(arena, at, H)
    dtb_row, at = cut(arena, at, H)
    x, at = cut(arena, at, 2, D)
    xres, at = cut(arena, at, 2, D)
    xn, at = cut(arena, at, D)
    xnT, at = cut(arena, at, KD, P)
    cin = []
    for par in range(2):
        c, at = cut(arena, at, CB, halo + P)
        cin.append(c)
    conv, at = cut(arena, at, CB, P)
    xc, at = cut(arena, at, 2, CB, P)
    zs, at = cut(arena, at, 2, INNER)
    decays, at = cut(arena, at, 2, H // 2, BLK)
    mixed, at = cut(arena, at, H, P)
    steps = core.halves
    xs, at = cut(arena, at, INNER)
    xskip, at = cut(arena, at, INNER)
    xdt, at = cut(arena, at, INNER)
    xlast, at = cut(arena, at, INNER)
    state, at = cut(arena, at, INNER)
    ysum, at = cut(arena, at, INNER)
    y, at = cut(arena, at, INNER)
    state_mid = y
    yT, at = cut(arena, at, KY, P)
    xo, at = cut(arena, at, D)
    b_rows, at = cut(arena, at, 2, STATE)
    st, at = cut(arena, at, 6)
    mv, at = cut(arena, at, 2)
    var_eps, at = cut(arena, at, 1)
    rstd, at = cut(arena, at, 1)
    u, at = cut(arena, at, H)
    mag, at = cut(arena, at, H)
    e_mag, at = cut(arena, at, H)
    ratio, at = cut(arena, at, H)
    ratio2, at = cut(arena, at, H)
    series, at = cut(arena, at, H)
    dt, at = cut(arena, at, 2, H)
    da, at = cut(arena, at, 2, H)
    da_parts, at = cut(arena, at, 2, H)
    sums, at = cut(arena, at, 4 * H)
    ncs, at = cut(arena, at, H)
    gap, at = cut(arena, at, H)
    to_end, at = cut(arena, at, H)
    exps, at = cut(arena, at, 3 * H)
    carried, at = cut(arena, at, H)
    squares, at = cut(arena, at, 1)
    mean_eps, at = cut(arena, at, 1)
    rinv, at = cut(arena, at, 1)
    assert at <= core.left, at - core.left
    small = bank[2]
    state_banks = ((7, 3), (4, 7))
    CS, BC, BROWS, DT = 0, P, 2 * P, 2 * P
    blocks = [slice(b * BLK, (b + 1) * BLK) for b in range(2)]
    parts = (slice(KY, CB), slice(0, KY // 2), slice(KY // 2, KY))
    part_banks = (bank[1], bank[0], bank[1])
    with stage_semaphores(nc, "mam") as sem, ExitStack() as ctx:
        w_in_here, w_out_here, rows_here = sem("w_in"), sem("w_out"), sem("rows_here")
        x_loaded = [sem("x_loaded0"), sem("x_loaded1")]
        again_loaded = [sem("again_loaded0"), sem("again_loaded1")]
        chains = [sem("chain_first"), sem("chain_loop"), sem("chain_last")]
        cleared, a_exp, a_ready = sem("cleared"), sem("a_exp"), sem("a_ready")
        var_ready, rstd_ready, xn_ready = sem("var_ready"), sem("rstd_ready"), sem("xn_ready")
        x_turned, xnT_ready = sem("x_turned"), sem("xnT_ready")
        front_made, cin_ready, tap_ready, conv_ready, xc_ready, z_ready = (
            sem("front_made"), sem("cin_ready"), sem("tap_ready"), sem("conv_ready"), sem("xc_ready"), sem("z_ready"))
        mag_ready, e_mag_ready, da_ready = sem("mag"), sem("e_mag"), sem("da_ready")
        parts_ready, steps_ready = sem("da_parts"), sem("steps")
        xs_turned, xs_ready, small_made, b_ready = sem("xs_turned"), sem("xs_ready"), sem("small"), sem("b_ready")
        sums_ready = sem("sums_ready")
        gap_ready, exps_ready, to_end_ready, carried_ready = sem("gap"), sem("exps"), sem("to_end"), sem("carried")
        xdt_ready, xskip_ready, xlast_ready = sem("xdt"), sem("xskip"), sem("xlast")
        sums_made, decays_ready, mixed_ready, yd_made = sem("sums"), sem("decays"), sem("mixed"), sem("yd_made")
        yo_made, yo_read, ysum_ready, y_ready = sem("yo_made"), sem("yo_read"), sem("ysum"), sem("y_ready")
        st_made, mid_ready, decayed, state_ready = sem("st_made"), sem("mid_ready"), sem("decayed"), sem("state_ready")
        y_turned, yT_ready, squares_ready = sem("y_turned"), sem("yT_ready"), sem("squares")
        mean_ready, rinv_ready = sem("mean"), sem("rinv")
        out_made, added, stored = sem("out_made"), sem("added"), sem("stored")
        block = ctx.enter_context(nc.Block())

        def by_head(v):
            return v.rearrange("p (h d) -> p h d", h=v.shape[1] // MHD)

        def by_chunk(v):
            return v.rearrange("p (a b) -> p a b", b=P)

        @block.sync
        def _(sp):
            def one(t):
                return slice(t, t + 1) if isinstance(t, int) else bass.ds(t, 1)

            def store(t):
                sp.wait_ge(added, t + 1)
                sp.dma_start(x_out[one(t)].rearrange("a p d -> p a d"), xo.unsqueeze(1)).then_inc(stored, 16)

            def load(t, par):
                sp.wait_ge(xn_ready, t - 1)
                sp.dma_start(x[:, par:par + 1], x_in[one(t)].rearrange("a p d -> p a d")).then_inc(x_loaded[par], 16)

            def load_again(t, par):
                sp.dma_start(xres[:, par:par + 1], x_in[one(t)].rearrange("a p d -> p a d"))\
                    .then_inc(again_loaded[par], 16)

            for par in range(2):
                sp.dma_start(x[:, par], x_in[par]).then_inc(x_loaded[par], 16)
            for k in range(KD):
                sp.dma_start(w_in[:, k], in_w[:, k]).then_inc(w_in_here, 16)
            for dst, src in ((taps, conv_w), (tap_bias, conv_b), (norm, norm_w)):
                sp.dma_start(dst, src).then_inc(rows_here, 16)
            for dst, src in ((a_row, a_log), (d_row, d_skip), (dtb_row, dt_bias)):
                sp.dma_start(dst, src.partition_broadcast(P)).then_inc(rows_here, 16)
            sp.dma_start(w_out, out_w).then_inc(w_out_here, 16)
            load_again(0, 0)
            load_again(1, 1)
            load(2, 0)
            load(3, 1)
            with sp.Fori(0, TURNS - 2) as i:
                for par in range(2):
                    t = 2 * i + par
                    store(t)
                    load_again(t + 2, par)
                    load(t + 4, par)
            for t in range(TILES - 4, TILES):
                store(t)
                if t < TILES - 2:
                    load_again(t + 2, t % 2)
            sp.wait_ge(stored, 16 * TILES)

        @block.gpsimd
        def _(pool):
            for zeros in (state, mixed, b_rows, cin[0], cin[1]):
                nc.gpsimd.memset(zeros, 0.0).then_inc(cleared, 1)
            pool.wait_ge(rows_here, 96)
            pool.wait_ge(cleared, 5)

            def norm_power(n):
                pool.wait_ge(var_ready, n + 1)
                nc.gpsimd.tensor_tensor(rstd, var_eps, core.mhalf[:], ALU.pow).then_inc(rstd_ready, 1)

            def spread_steps(n):
                pool.wait_ge(parts_ready, 2 * n + 2)
                after(pool, sums_made, 2 * n)
                for part in range(2):
                    nc.gpsimd.tensor_tensor(steps[:, part].rearrange("p (h l) -> p h l", h=H),
                                            spread(da_parts[:, part], 2, BLK), spread(core.upto[:], 1, H), ALU.mult)\
                        .then_inc(steps_ready, 1)

            def mean_power(t):
                pool.wait_ge(mean_ready, t + 1)
                nc.gpsimd.tensor_tensor(rinv, mean_eps, core.mhalf[:], ALU.pow).then_inc(rinv_ready, 1)

            def step(t, before, front):
                pool.wait_ge(xs_ready, 2 * t + 2)
                after(pool, squares_ready, t)
                after(pool, ysum_ready, t)
                nc.gpsimd.tensor_tensor(by_head(xskip), by_head(xs), spread(d_row, 2, MHD), ALU.mult)\
                    .then_inc(xskip_ready, 1)
                if before:
                    mean_power(t - 1)
                pool.wait_ge(to_end_ready, t + 1)
                pool.wait_ge(xdt_ready, t + 1)
                after(pool, st_made, 4 * t)
                nc.gpsimd.tensor_tensor(by_head(xlast), by_head(xdt), spread(to_end, 2, MHD), ALU.mult)\
                    .then_inc(xlast_ready, 1)
                pool.wait_ge(carried_ready, t + 1)
                after(pool, yo_made, 2 * t)
                nc.gpsimd.tensor_tensor(by_head(state), by_head(state), spread(carried, 2, MHD), ALU.mult)\
                    .then_inc(decayed, 1)
                if front:
                    spread_steps(t + 1)

            norm_power(0)
            spread_steps(0)
            norm_power(1)
            step(0, False, True)
            norm_power(2)
            step(1, True, True)
            norm_power(3)
            with pool.Fori(2, TILES - 2) as t:
                step(t, True, True)
                norm_power(t + 2)
            step(TILES - 2, True, True)
            step(TILES - 1, True, False)
            mean_power(TILES - 1)

        @block.vector
        def _(dve):
            def layer_norm(link, n, par, turn):
                dve.wait_ge(x_loaded[par], 16 * turn + 16)
                link(nc.vector.bn_stats(st, x[:, par]))
                nc.vector.nop(nofuse=True)
                link(nc.vector.bn_aggr(mv, st))
                nc.vector.tensor_scalar(var_eps, mv[:, 1:2], EPS, None, ALU.add).then_inc(var_ready, 1)
                dve.wait_ge(rstd_ready, n + 1)
                after(dve, x_turned, n)
                nc.vector.tensor_scalar(xn, x[:, par], mv[:, 0:1], rstd, ALU.subtract, ALU.mult).then_inc(xn_ready, 1)

            def time_steps(link, n, par):
                dve.wait_ge(front_made, 5 * n + 1)
                link(nc.vector.tensor_tensor(u, bank[1][:, DT:DT + H], dtb_row, ALU.add))
                nc.vector.scalar_tensor_tensor(out=mag, in0=u, scalar=-1.0, in1=u, op0=ALU.mult, op1=ALU.max)\
                    .then_inc(mag_ready, 1)
                dve.wait_ge(e_mag_ready, n + 1)
                link(nc.vector.tensor_scalar(ratio, e_mag, 2.0, None, ALU.add))
                link(nc.vector.reciprocal(ratio, ratio))
                link(nc.vector.tensor_tensor(ratio, e_mag, ratio, ALU.mult))
                link(nc.vector.tensor_tensor(ratio2, ratio, ratio, ALU.mult))
                link(nc.vector.tensor_scalar(series, ratio2, 1.0 / 15, None, ALU.mult))
                for odd in (13, 11, 9, 7, 5, 3):
                    link(nc.vector.scalar_tensor_tensor(out=series, in0=series, scalar=1.0 / odd, in1=ratio2,
                                                        op0=ALU.add, op1=ALU.mult))
                link(nc.vector.scalar_tensor_tensor(out=series, in0=series, scalar=1.0, in1=ratio,
                                                    op0=ALU.add, op1=ALU.mult))
                link(nc.vector.tensor_scalar(u, u, 0.0, None, ALU.max))
                link(nc.vector.scalar_tensor_tensor(out=dt[:, par], in0=series, scalar=2.0, in1=u,
                                                    op0=ALU.mult, op1=ALU.add))
                nc.vector.tensor_tensor(da[:, par], dt[:, par], a_row, ALU.mult).then_inc(da_ready, 1)
                dve.wait_ge(da_ready, n + 1)
                after(dve, steps_ready, 2 * n)
                nc.vector.tensor_copy(da_parts[:, 0].bitcast(F32R), da[:, par]).then_inc(parts_ready, 1)
                dve.wait_ge(parts_ready, 2 * n + 1)
                nc.vector.tensor_tensor(da_parts[:, 1], da[:, par], da_parts[:, 0], ALU.subtract)\
                    .then_inc(parts_ready, 1)

            def halo_in(link, n, par, keep):
                after(dve, cin_ready, 3 * n)
                link(nc.vector.tensor_scalar(cin[par][:, :, 0:halo], cin[1 - par][:, :, P:P + halo], keep, None,
                                             ALU.mult))

            def convolve(link, n, par, part):
                dve.wait_ge(cin_ready, 3 * n + part + 1)
                dve.wait_ge(tap_ready, 3 * n + part + 1)
                for k in range(halo):
                    for c in range(parts[part].start, parts[part].stop):
                        last = nc.vector.scalar_tensor_tensor(out=conv[:, c], in0=cin[par][:, c, k:k + P],
                                                              scalar=taps[:, c, k:k + 1], in1=conv[:, c],
                                                              op0=ALU.mult, op1=ALU.add)
                    if k < halo - 1:
                        link(last)
                last.then_inc(conv_ready, 1)

            def first_factor(turn):
                return core.keep[:, bass.ds(turn % TURNS_PER_BATCH, 1)]

            def turned_out(t):
                dve.wait_ge(y_turned, t + 1)
                after(dve, out_made, t)
                for half in range(2):
                    part = slice(4 * half, 4 * half + 4)
                    last = nc.vector.tensor_tensor(yT[:, part], by_chunk(bank[5 + half][:]),
                                                   spread(norm[:, part], 2, P), ALU.mult)
                last.then_inc(yT_ready, 1)
                dve.wait_ge(squares_ready, t + 1)
                nc.vector.tensor_scalar(mean_eps, squares, 1.0 / INNER, EPS, ALU.mult, ALU.add).then_inc(mean_ready, 1)

            def put_out(t, par, turn):
                dve.wait_ge(out_made, t + 1)
                dve.wait_ge(rinv_ready, t + 1)
                dve.wait_ge(again_loaded[par], 16 * turn + 16)
                after(dve, stored, 16 * t)
                nc.vector.scalar_tensor_tensor(out=xo, in0=bank[7][:], scalar=rinv, in1=xres[:, par],
                                               op0=ALU.mult, op1=ALU.add).then_inc(added, 1)

            def step(link, t, turn, par, before, front):
                keep = first_factor(turn) if par == 0 else core.ones[:, 0:1]
                dve.wait_ge(sums_ready, t + 1)
                after(dve, decays_ready, 2 * t)
                link(nc.vector.tensor_scalar(ncs, sums[:, CS:CS + H], -1.0, None, ALU.mult))
                after(dve, to_end_ready, t)
                nc.vector.tensor_tensor(gap, sums[:, 3 * H:4 * H], ncs, ALU.add).then_inc(gap_ready, 1)
                if before:
                    turned_out(t - 1)
                dve.wait_ge(xs_ready, 2 * t + 2)
                after(dve, yd_made, 2 * t)
                after(dve, xlast_ready, t)
                nc.vector.tensor_tensor(by_head(xdt), by_head(xs), spread(dt[:, par], 2, MHD), ALU.mult)\
                    .then_inc(xdt_ready, 1)
                dve.wait_ge(exps_ready, t + 1)
                after(dve, decayed, t)
                nc.vector.tensor_scalar(carried, exps[:, H:2 * H], keep, None, ALU.mult).then_inc(carried_ready, 1)
                if front:
                    halo_in(link, t + 1, 1 - par, first_factor(turn + 1) if par else core.ones[:, 0:1])
                    time_steps(link, t + 1, 1 - par)
                    convolve(link, t + 1, 1 - par, 0)
                if before:
                    put_out(t - 1, 1 - par, turn if par else turn - 1)
                after(dve, yd_made, 2 * t)
                for g in range(2):
                    dve.wait_ge(decays_ready, 2 * t + g + 1)
                    heads = slice(g * H // 2, (g + 1) * H // 2)
                    for rows in blocks:
                        nc.vector.tensor_tensor(mixed[rows, heads, rows], decays[rows, g],
                                                spread(small[rows, BC:BC + BLK], 1, H // 2), ALU.mult)\
                            .then_inc(mixed_ready, 1)
                dve.wait_ge(decayed, t + 1)
                after(dve, y_turned, t)
                after(dve, squares_ready, t)
                for half in range(2):
                    part = slice(half * 512, half * 512 + 512)
                    heads = slice(half * H // 2, (half + 1) * H // 2)
                    first, second = state_banks[half]
                    dve.wait_ge(st_made, 4 * t + 2 * half + 1)
                    nc.vector.tensor_tensor(state_mid[:, part], state[:, part], bank[first][:], ALU.add)\
                        .then_inc(mid_ready, 1)
                    dve.wait_ge(mid_ready, 2 * t + half + 1)
                    link(nc.vector.tensor_tensor(by_head(state[:, part]), by_head(state_mid[:, part]),
                                                 spread(exps[:, 2 * H:3 * H][:, heads], 2, MHD), ALU.mult))
                    dve.wait_ge(st_made, 4 * t + 2 * half + 2)
                    nc.vector.tensor_tensor(state[:, part], state[:, part], bank[second][:], ALU.add)\
                        .then_inc(state_ready, 1)
                if front:
                    convolve(link, t + 1, 1 - par, 1)
                    convolve(link, t + 1, 1 - par, 2)
                for half, b in ((0, 3), (1, 4)):
                    part = slice(half * 512, half * 512 + 512)
                    heads = slice(half * H // 2, (half + 1) * H // 2)
                    dve.wait_ge(yo_made, 2 * t + half + 1)
                    nc.vector.tensor_tensor(by_head(ysum[:, part]), by_head(bank[b][:]),
                                            spread(exps[:, heads], 2, MHD), ALU.mult).then_inc(yo_read, 1)
                dve.wait_ge(yd_made, 2 * t + 2)
                dve.wait_ge(yo_read, 2 * t + 2)
                for half in range(2):
                    part = slice(half * 512, half * 512 + 512)
                    last = nc.vector.tensor_tensor(ysum[:, part], ysum[:, part], bank[5 + half][:], ALU.add)
                link(last)
                dve.wait_ge(xskip_ready, t + 1)
                nc.vector.tensor_tensor(ysum, ysum, xskip, ALU.add).then_inc(ysum_ready, 1)
                dve.wait_ge(ysum_ready, t + 1)
                dve.wait_ge(z_ready, 2 * t + 2)
                nc.vector.tensor_tensor(y, ysum, zs[:, par], ALU.mult).then_inc(y_ready, 1)

            dve.wait_ge(cleared, 5)
            dve.wait_ge(rows_here, 96)
            dve.wait_ge(a_exp, 1)
            nc.vector.tensor_scalar(a_row, a_row, -1.0, None, ALU.mult).then_inc(a_ready, 1)
            dve.wait_ge(a_ready, 1)
            link = Chain(dve, chains[0])
            layer_norm(link, 0, 0, 0)
            halo_in(link, 0, 0, core.keep[:, 0:1])
            time_steps(link, 0, 0)
            layer_norm(link, 1, 1, 0)
            for part in range(3):
                convolve(link, 0, 0, part)
            per_turn = 56
            link = Chain(dve, chains[1], 0, per_turn)
            for par in range(2):
                step(link, par, 0, par, par > 0, True)
                layer_norm(link, par + 2, par, 1)
            link.end()
            with dve.Fori(1, TURNS - 1) as i:
                link = Chain(dve, chains[1], i, per_turn)
                for par in range(2):
                    step(link, 2 * i + par, i, par, True, True)
                    layer_norm(link, 2 * i + par + 2, par, i + 1)
                link.end()
            link = Chain(dve, chains[2])
            step(link, TILES - 2, TURNS - 1, 0, True, True)
            step(link, TILES - 1, TURNS - 1, 1, True, False)
            turned_out(TILES - 1)
            put_out(TILES - 1, 1, TURNS - 1)

        @block.scalar
        def _(act):
            def rows_out(n):
                act.wait_ge(x_turned, n + 1)
                after(act, front_made, 5 * n)
                nc.scalar.activation(xnT, by_chunk(bank[0][:]), ACT.Copy).then_inc(xnT_ready, 1)

            def conv_in(n, par, part):
                act.wait_ge(front_made, 5 * n + part + 1)
                after(act, conv_ready, 3 * n)
                after(act, xc_ready, 3 * n)
                c = parts[part]
                nc.scalar.activation(cin[par][:, c, halo:halo + P],
                                     by_chunk(part_banks[part][:, 0:(c.stop - c.start) * P]), ACT.Copy)\
                    .then_inc(cin_ready, 1)
                act.wait_ge(cin_ready, 3 * n + part + 1)
                for c in range(parts[part].start, parts[part].stop):
                    last = nc.scalar.activation(conv[:, c], cin[par][:, c, halo:halo + P], ACT.Copy,
                                                scale=taps[:, c, halo:halo + 1])
                last.then_inc(tap_ready, 1)

            def gate(n, par):
                for half in range(2):
                    act.wait_ge(front_made, 5 * n + 4 + half)
                    after(act, y_ready, n - 1)
                    nc.scalar.activation(zs[:, par, half * 512:half * 512 + 512], bank[half][:], ACT.Silu)\
                        .then_inc(z_ready, 1)

            def conv_out(n, par, part):
                act.wait_ge(conv_ready, 3 * n + part + 1)
                after(act, yo_made, 2 * n - 2)
                for c in range(parts[part].start, parts[part].stop):
                    last = nc.scalar.activation(xc[:, par, c], conv[:, c], ACT.Silu, bias=tap_bias[:, c:c + 1])
                last.then_inc(xc_ready, 1)

            def e_mags(n):
                act.wait_ge(mag_ready, n + 1)
                after(act, da_ready, n)
                nc.scalar.activation(e_mag, mag, ACT.Exp, scale=-1.0).then_inc(e_mag_ready, 1)

            def decay(t, g):
                act.wait_ge(sums_made, 2 * t + g + 1)
                if g == 0:
                    after(act, mixed_ready, 4 * t)
                for r in range(H // 2):
                    h = H // 2 * g + r
                    last = nc.scalar.activation(decays[:, g, r], bank[3 + g][:, r * BLK:(r + 1) * BLK], ACT.Exp,
                                                bias=ncs[:, h:h + 1])
                last.then_inc(decays_ready, 1)

            def squares_of(t):
                act.wait_ge(y_ready, t + 1)
                after(act, mean_ready, t)
                nc.scalar.activation(xskip, y, ACT.Square, accum_out=squares).then_inc(squares_ready, 1)

            def step(t, par, before, front):
                act.wait_ge(small_made, t + 1)
                after(act, gap_ready, t)
                nc.scalar.activation(sums, small[:, CS:CS + 4 * H], ACT.Copy).then_inc(sums_ready, 1)
                after(act, yo_read, 2 * t)
                nc.scalar.activation(exps, small[:, CS:CS + 3 * H], ACT.Exp).then_inc(exps_ready, 1)
                act.wait_ge(xs_turned, t + 1)
                after(act, xdt_ready, t)
                after(act, xskip_ready, t)
                for half in range(2):
                    nc.scalar.activation(xs[:, half * 512:half * 512 + 512], bank[3 + half][:], ACT.Copy)\
                        .then_inc(xs_ready, 1)
                after(act, st_made, 4 * t)
                for b, rows in enumerate(blocks):
                    nc.scalar.activation(b_rows[rows, b], small[rows, BROWS:BROWS + P], ACT.Copy).then_inc(b_ready, 1)
                act.wait_ge(gap_ready, t + 1)
                after(act, xlast_ready, t)
                nc.scalar.activation(to_end, gap, ACT.Exp).then_inc(to_end_ready, 1)
                if front:
                    rows_out(t + 1)
                if before:
                    squares_of(t - 1)
                if front:
                    e_mags(t + 1)
                    conv_in(t + 1, 1 - par, 0)
                decay(t, 0)
                decay(t, 1)
                if front:
                    conv_in(t + 1, 1 - par, 1)
                    conv_in(t + 1, 1 - par, 2)
                    for part in range(3):
                        conv_out(t + 1, 1 - par, part)
                    gate(t + 1, 1 - par)

            act.wait_ge(rows_here, 96)
            act.wait_ge(cleared, 5)
            nc.scalar.activation(a_row, a_row, ACT.Exp).then_inc(a_exp, 1)
            rows_out(0)
            e_mags(0)
            for part in range(3):
                conv_in(0, 0, part)
            for part in range(3):
                conv_out(0, 0, part)
            gate(0, 0)
            for par in range(2):
                step(par, par, par > 0, True)
            with act.Fori(1, TURNS - 1) as i:
                for par in range(2):
                    step(2 * i + par, par, True, True)
            step(TILES - 2, 0, True, True)
            step(TILES - 1, 1, True, False)
            squares_of(TILES - 1)

        @block.tensor
        def _(pe):
            def turn_rows(n):
                pe.wait_ge(xn_ready, n + 1)
                after(pe, z_ready, 2 * n)
                for k in range(KD):
                    last = nc.tensor.transpose(bank[0][:, k * P:k * P + P], xn[:, k * P:k * P + P], core.ident[:])
                last.then_inc(x_turned, 1)

            def channels(n, part):
                if part == 0:
                    pe.wait_ge(xnT_ready, n + 1)
                if part == 2:
                    pe.wait_ge(cin_ready, 3 * n + 1)
                    pe.wait_ge(mag_ready, n + 1)
                for j, c in enumerate(range(parts[part].start, parts[part].stop)):
                    at = INNER + c * P
                    for k in range(KD):
                        last = nc.tensor.matmul(part_banks[part][:, j * P:j * P + P],
                                                w_in[:, k, at:at + P], xnT[:, k], start=(k == 0), stop=(k == KD - 1))
                if part == 0:
                    for k in range(KD):
                        last = nc.tensor.matmul(bank[1][:, DT:DT + H], xnT[:, k], w_in[:, k, INNER + XBC:WIN_COLS],
                                                start=(k == 0), stop=(k == KD - 1))
                last.then_inc(front_made, 1)

            def gate_rows(n, half):
                pe.wait_ge(cin_ready, 3 * n + 2 + half)
                for k in range(KD):
                    last = nc.tensor.matmul(bank[half][:], xnT[:, k], w_in[:, k, half * 512:half * 512 + 512],
                                            start=(k == 0), stop=(k == KD - 1))
                last.then_inc(front_made, 1)

            def running_sums(g):
                b = bank[3 + g]
                nc.tensor.matmul(b[:], core.identb[:], core.ssd_mask[:].rearrange("p a b -> p (a b)"),
                                 start=True, stop=False)
                for part in range(2):
                    last = nc.tensor.matmul(b[:], core.own_r[:],
                                            steps[:, part, g * 512:g * 512 + 512],
                                            start=False, stop=(part == 1))
                last.then_inc(sums_made, 1)

            def scan_rows(t, par):
                B, C = xc[:, par, KY], xc[:, par, KY + 1]
                pe.wait_ge(xc_ready, 3 * t + 1)
                pe.wait_ge(da_ready, t + 1)
                after(pe, mixed_ready, 4 * t)
                after(pe, b_ready, 2 * t)
                nc.tensor.transpose(small[:, BROWS:BROWS + P], B, core.ident[:])
                for j, which in enumerate((core.upto_own[:], core.in_block[:, 0], core.in_block[:, 1], core.own[:])):
                    nc.tensor.matmul(small[:, CS + j * H:CS + (j + 1) * H], which, da[:, par], start=True, stop=True)
                for rows in blocks:
                    last = nc.tensor.matmul(small[rows, BC:BC + BLK], B[:, rows], C[:, rows], start=True, stop=True)
                last.then_inc(small_made, 1)
                pe.wait_ge(xc_ready, 3 * t + 3)
                after(pe, yo_read, 2 * t)
                for k in range(KY):
                    last = nc.tensor.transpose(bank[3 + k // 4][:, (k % 4) * P:(k % 4 + 1) * P], xc[:, par, k],
                                               core.ident[:])
                last.then_inc(xs_turned, 1)

            def turn_y(t):
                pe.wait_ge(y_ready, t + 1)
                for k in range(KY):
                    last = nc.tensor.transpose(bank[5 + k // 4][:, (k % 4) * P:(k % 4 + 1) * P],
                                               y[:, k * P:k * P + P], core.ident[:])
                last.then_inc(y_turned, 1)

            def project_out(t):
                pe.wait_ge(yT_ready, t + 1)
                for k in range(KY):
                    last = nc.tensor.matmul(bank[7][:], yT[:, k], w_out[:, k], start=(k == 0), stop=(k == KY - 1))
                last.then_inc(out_made, 1)

            def block_states(t):
                pe.wait_ge(xlast_ready, t + 1)
                pe.wait_ge(b_ready, 2 * t + 2)
                for half in range(2):
                    for b in range(2):
                        if (half, b) == (0, 0):
                            after(pe, added, t)
                        if (half, b) == (0, 1):
                            pe.wait_ge(decays_ready, 2 * t + 1)
                        if (half, b) == (1, 0):
                            pe.wait_ge(decays_ready, 2 * t + 2)
                        if (half, b) == (1, 1):
                            pe.wait_ge(mid_ready, 2 * t + 1)
                        nc.tensor.matmul(bank[state_banks[half][b]][:], b_rows[:, b],
                                         xlast[:, half * 512:half * 512 + 512], start=True, stop=True)\
                            .then_inc(st_made, 1)

            def own_rows(t, g):
                pe.wait_ge(mixed_ready, 4 * t + 2 * g + 2)
                if g == 0:
                    pe.wait_ge(xdt_ready, t + 1)
                for r in range(H // 2):
                    h = H // 2 * g + r
                    last = nc.tensor.matmul(bank[5 + g][:, r * MHD:(r + 1) * MHD], mixed[:, h],
                                            xdt[:, h * MHD:h * MHD + MHD], start=True, stop=True)
                last.then_inc(yd_made, 1)

            def from_states(t, par):
                C = xc[:, par, KY + 1]
                for half, b in ((0, 3), (1, 4)):
                    pe.wait_ge(state_ready, 2 * t + half + 1)
                    for rows, held in zip(blocks, (state_mid, state)):
                        last = nc.tensor.matmul(bank[b][rows, :], C[:, rows], held[:, half * 512:half * 512 + 512],
                                                start=True, stop=True)
                    last.then_inc(yo_made, 1)

            def step(t, par, before, front):
                scan_rows(t, par)
                if front:
                    turn_rows(t + 1)
                if before:
                    turn_y(t - 1)
                if front:
                    channels(t + 1, 0)
                if before:
                    project_out(t - 1)
                pe.wait_ge(xs_ready, 2 * t + 2)
                pe.wait_ge(steps_ready, 2 * t + 2)
                running_sums(0)
                running_sums(1)
                if front:
                    channels(t + 1, 1)
                block_states(t)
                if front:
                    channels(t + 1, 2)
                own_rows(t, 0)
                own_rows(t, 1)
                from_states(t, par)
                if front:
                    gate_rows(t + 1, 0)
                    gate_rows(t + 1, 1)

            pe.wait_ge(w_in_here, 16 * KD)
            turn_rows(0)
            for part in range(3):
                channels(0, part)
            gate_rows(0, 0)
            gate_rows(0, 1)
            pe.wait_ge(w_out_here, 16)
            pe.wait_ge(cleared, 5)
            for par in range(2):
                step(par, par, par > 0, True)
            with pe.Fori(1, TURNS - 1) as i:
                for par in range(2):
                    step(2 * i + par, par, True, True)
            step(TILES - 2, 0, True, True)
            step(TILES - 1, 1, True, False)
            turn_y(TILES - 1)
            project_out(TILES - 1)


def hybrid_block(nc, x, w_qkv, w_out, in_w, conv_w, conv_b, a_log, d_skip, dt_bias, norm_w, out_w, gate, w1, w2, w2_tail, out):
    def tiles(rows):
        return rows[0:ROWS].rearrange("(t p) d -> t p d", p=P)

    with ExitStack() as ctx:
        core = Core(nc, ctx)
        mid = nc.dram_tensor("mid_rows", (ROWS + SPARE, D), F32).ap()
        xn_rows = nc.dram_tensor("normalised_rows", (ROWS + SPARE, D), F32).ap()
        make_constants(core, [rows[ROWS:ROWS + SPARE] for rows in (mid, xn_rows, out)])
        attention(core, tiles(x), tiles(mid), w_qkv, w_out, w1)
        experts(core, "moe_a", mid, xn_rows, gate, w1, w2, w2_tail)
        mamba(core, tiles(mid), tiles(out), in_w, out_w, conv_w, conv_b, a_log, d_skip, dt_bias, norm_w)
        experts(core, "moe_b", out, xn_rows, gate, w1, w2, w2_tail)


def _by_partition(w):
    import numpy as _np
    return _np.ascontiguousarray(w.T.reshape(-1, 128, w.shape[0]).transpose(1, 0, 2))


def kernel(**inputs):
    import numpy as _np
    import concourse.bacc as _bacc
    from concourse import mybir as _mybir
    from concourse.bass_utils import run_bass_kernel_spmd as _run

    a = {name: _np.asarray(v) for name, v in inputs.items()}
    w1, w2 = a["L0_ffn_w1"], a["L0_ffn_w2"]
    n_e, two_i, d = w1.shape
    inner = w2.shape[2]
    whole = inner // 128 * 128
    w1 = w1.transpose(2, 0, 1).reshape(d // 128, 128, n_e, two_i).transpose(1, 2, 0, 3).reshape(128, n_e, -1)
    w2 = w2.transpose(2, 0, 1)
    taps = a["L0_attn_b_conv_w"].shape[2]
    laid = {
        "x": a["L0_attn_a_x"].reshape(-1, d),
        "w_qkv": _by_partition(a["L0_attn_a_w_qkv"]),
        "w_out": _by_partition(a["L0_attn_a_w_out"]),
        "in_w": _by_partition(a["L0_attn_b_in_proj_w"]),
        "conv_w": a["L0_attn_b_conv_w"].reshape(-1, 128, taps).transpose(1, 0, 2),
        "conv_b": a["L0_attn_b_conv_b"].reshape(-1, 128).T,
        "a_log": a["L0_attn_b_A_log"],
        "d_skip": a["L0_attn_b_D"],
        "dt_bias": a["L0_attn_b_dt_bias"],
        "norm_w": a["L0_attn_b_norm_w"].reshape(-1, 128).T,
        "out_w": _by_partition(a["L0_attn_b_out_proj_w"]),
        "gate": _by_partition(a["L0_ffn_gate_w"]),
        "w1": w1,
        "w2": w2[:whole].reshape(whole // 128, 128, n_e, d).transpose(1, 2, 0, 3),
        "w2_tail": w2[whole:],
    }
    nc = _bacc.Bacc("TRN2", target_bir_lowering=False, num_devices=1)
    arrays, args = {}, []
    for name, v in laid.items():
        v = _np.ascontiguousarray(v)
        arrays[f"in_{name}_dram"] = v
        args.append(nc.dram_tensor(f"in_{name}_dram", v.shape, _mybir.dt.from_np(v.dtype), kind="ExternalInput").ap())
    rows = laid["x"].shape[0]
    args.append(nc.dram_tensor("out_dram", (rows + 128, d), _mybir.dt.float32, kind="ExternalOutput").ap())
    hybrid_block(nc, *args)
    r = _run(nc, [arrays], core_ids=[0])
    return r.results[0]["out_dram"][:rows].reshape(a["L0_attn_a_x"].shape)
```

```python
from contextlib import ExitStack, contextmanager

import concourse.bass as bass
from concourse import mybir

F32 = mybir.dt.float32
BF16 = mybir.dt.bfloat16
F32R = mybir.dt.float32r
I32 = mybir.dt.int32
U32 = mybir.dt.uint32
ALU = mybir.AluOpType
ACT = mybir.ActivationFunctionType
AX = mybir.AxisListType

P = 128
BATCH, SEQ, D = 2, 1024, 512
ROWS = BATCH * SEQ
TILES = ROWS // P
TURNS = TILES // 2
TURNS_PER_BATCH = TURNS // BATCH
KD = D // P
EPS = 1e-5
NEG = -1e30

HEADS, HD = 16, 32
HG = P // HD
WIN = P

EXPERTS, TOPK, INTER = 8, 2, 352
KI = -(-INTER // P)
LAST_I = INTER - (KI - 1) * P
SLOTS = -(-(TOPK * ROWS + EXPERTS * (P - 1)) // (2 * P)) * 2
SPARE = P
W1E = KD * 2 * INTER
W2E = KI * D

INNER, STATE, MHEADS, MHD, TAPS = 1024, 128, 16, 64, 4
BLK = 64
XBC = INNER + 2 * STATE
CB = XBC // P
KY = INNER // P
WIN_COLS = 2 * INNER + 2 * STATE + MHEADS


class Chain:

    def __init__(self, eng, sem, turn=0, per_turn=0):
        self.eng, self.sem, self.turn, self.per_turn, self.n = eng, sem, turn, per_turn, 0

    def __call__(self, ins):
        self.n += 1
        ins.then_inc(self.sem, 1)
        self.eng.wait_ge(self.sem, self.turn * self.per_turn + self.n)

    def end(self):
        assert self.n == self.per_turn, self.n


def after(eng, sem, n):
    if not isinstance(n, int) or n > 0:
        eng.wait_ge(sem, n)


def cut(arena, at, *shape):
    n = 1
    for s in shape:
        n *= s
    v = arena[:, at:at + n]
    if len(shape) == 2:
        v = v.rearrange("p (a b) -> p a b", b=shape[1])
    if len(shape) == 3:
        v = v.rearrange("p (a b c) -> p a b c", b=shape[1], c=shape[2])
    return v, at + n


def spread(ap, axis, n):
    v = ap.unsqueeze(axis)
    shape = list(v.shape)
    shape[axis] = n
    return v.broadcast_to(shape)


@contextmanager
def stage_semaphores(nc, tag):
    taken = []

    def sem(name):
        taken.append(nc.alloc_semaphore(name=f"{tag}_{name}"))
        return taken[-1]

    yield sem
    nc.clear_and_free_semaphores(taken)
    nc.all_engine_barrier()


class Core:

    def __init__(self, nc, ctx):
        self.nc, self.ctx = nc, ctx
        self.bank = [ctx.enter_context(nc.psum_tensor(f"bank{i}", [P, 512], F32)) for i in range(8)]

        def sb(name, shape, dt=F32):
            return ctx.enter_context(nc.sbuf_tensor(name, shape, dt))

        self.pool_dma = {tag: [ctx.enter_context(nc.semaphore(f"{tag}_{name}"))
                               for name in ("gathered0", "gathered1", "added")] for tag in ("moe_a", "moe_b")}
        self.ident = sb("ident", [P, P])
        self.identb = sb("identb", [P, P], BF16)
        self.zero = sb("zero", [P, 8])
        self.att_mask = sb("att_mask", [P, 3, 2 * P], BF16)
        self.ssd_mask = sb("ssd_mask", [P, MHEADS // 2, BLK], BF16)
        self.upto = sb("upto", [P, BLK])
        self.upto_own = sb("upto_own", [P, P])
        self.own = sb("own", [P, P])
        self.own_r = sb("own_r", [P, P], F32R)
        self.halves = sb("halves", [P, 2, INNER], F32R)
        self.in_block = sb("in_block", [P, 2, P])
        self.before = sb("before", [P, P], BF16)
        self.ones = sb("ones", [P, P])
        self.onesb = sb("onesb", [P, P], BF16)
        self.count = sb("count", [P, P])
        self.rowid = sb("rowid", [P, TILES])
        self.spareid = sb("spareid", [P, 1])
        self.mhalf = sb("mhalf", [P, 1])
        self.gate = sb("gate", [P, KD, EXPERTS])
        self.logits = sb("logits", [P, TILES, EXPERTS])
        self.keep = sb("keep", [P, TURNS_PER_BATCH])
        left = (nc.sbuf_bytes_remaining - 64) // 4 // 8 * 8
        self.arena = sb("arena", [P, left])
        self.left = left
        self.w1_at, self.w2_at = 0, EXPERTS * W1E
        self.work_at = self.w2_at + EXPERTS * W2E
        self.mamba_experts = 4
        self.mamba_at = self.mamba_experts * W1E
        self.att_experts = 2
        self.att_at = self.w2_at + self.att_experts * W2E
        self.w_in_at = left - KD * WIN_COLS
        self.w1 = self.arena[:, 0:EXPERTS * W1E]
        self.w2 = self.arena[:, self.w2_at:self.work_at]


class Scoring:

    def __init__(self, core, sem, xn_rows, rows_at, at):
        self.core, self.nc = core, core.nc
        self.xn_out = xn_rows[0:ROWS].rearrange("(t p) d -> t p d", p=P)
        self.xn, rows_at = cut(core.arena, rows_at, D)
        self.xnT, _ = cut(core.arena, rows_at, KD, P)
        self.st, at = cut(core.arena, at, 6)
        self.mv, at = cut(core.arena, at, 2)
        self.var_eps, at = cut(core.arena, at, 1)
        self.rstd, at = cut(core.arena, at, 1)
        self.end = at
        self.var_ready, self.rstd_ready, self.xn_ready = sem("out_var"), sem("out_rstd"), sem("out_xn")
        self.turned, self.xnT_ready = sem("out_turned"), sem("out_xnT")
        self.made, self.ready, self.stored = sem("logits_made"), sem("logits_ready"), sem("out_xn_stored")

    def statistics(self, dve, link, x):
        link(self.nc.vector.bn_stats(self.st, x))
        self.nc.vector.nop(nofuse=True)
        link(self.nc.vector.bn_aggr(self.mv, self.st))
        self.nc.vector.tensor_scalar(self.var_eps, self.mv[:, 1:2], EPS, None, ALU.add).then_inc(self.var_ready, 1)

    def power(self, pool, n):
        pool.wait_ge(self.var_ready, n + 1)
        self.nc.gpsimd.tensor_tensor(self.rstd, self.var_eps, self.core.mhalf[:], ALU.pow)\
            .then_inc(self.rstd_ready, 1)

    def normalise(self, dve, n, x):
        dve.wait_ge(self.rstd_ready, n + 1)
        after(dve, self.turned, n)
        after(dve, self.stored, 16 * n)
        self.nc.vector.tensor_scalar(self.xn, x, self.mv[:, 0:1], self.rstd, ALU.subtract, ALU.mult)\
            .then_inc(self.xn_ready, 1)

    def store(self, sp, n):
        sp.wait_ge(self.xn_ready, n + 1)
        where = slice(n, n + 1) if isinstance(n, int) else bass.ds(n, 1)
        sp.dma_start(self.xn_out[where].rearrange("a p d -> p a d"), self.xn.unsqueeze(1)).then_inc(self.stored, 16)

    def turn(self, pe, n, bank):
        pe.wait_ge(self.xn_ready, n + 1)
        for k in range(KD):
            last = self.nc.tensor.transpose(bank[:, k * P:k * P + P], self.xn[:, k * P:k * P + P], self.core.ident[:])
        last.then_inc(self.turned, 1)

    def turned_out(self, act, n, bank):
        act.wait_ge(self.turned, n + 1)
        after(act, self.made, n)
        self.nc.scalar.activation(self.xnT, bank[:].rearrange("p (a b) -> p a b", b=P), ACT.Copy)\
            .then_inc(self.xnT_ready, 1)

    def product(self, pe, n, bank):
        pe.wait_ge(self.xnT_ready, n + 1)
        for k in range(KD):
            last = self.nc.tensor.matmul(bank[:, 0:EXPERTS], self.xnT[:, k], self.core.gate[:, k],
                                         start=(k == 0), stop=(k == KD - 1))
        last.then_inc(self.made, 1)

    def logits_out(self, dve, n, bank):
        dve.wait_ge(self.made, n + 1)
        self.nc.vector.nop(nofuse=True)
        where = slice(n, n + 1) if isinstance(n, int) else bass.ds(n, 1)
        self.nc.vector.tensor_copy(self.core.logits[:, where].rearrange("p t e -> p (t e)"), bank[:, 0:EXPERTS])\
            .then_inc(self.ready, 1)


def make_constants(core, spare_rows):
    nc = core.nc
    with stage_semaphores(nc, "const") as sem, ExitStack() as ctx:
        made, base_made, zeroed = sem("made"), sem("base_made"), sem("spare_zeroed")
        zero_rows = core.arena[:, core.att_at:core.att_at + D]
        block = ctx.enter_context(nc.Block())

        @block.vector
        def _(dve):
            for ap, value in ((core.zero, 0.0), (core.ident, 0.0), (core.identb, 0.0), (core.ones, 1.0),
                              (core.onesb, 1.0), (core.att_mask, 0.0), (core.ssd_mask, 0.0), (core.in_block, 1.0),
                              (core.mhalf, -0.5), (core.keep, 1.0)):
                nc.vector.memset(ap[:], value)
            nc.vector.memset(zero_rows, 0.0).then_inc(base_made, 1)

        @block.gpsimd
        def _(pool):
            g = Chain(pool, made)
            pool.wait_ge(base_made, 1)
            for m in (core.ident, core.identb):
                g(nc.gpsimd.affine_select(out=m[:], in_=m[:], compare_op=ALU.not_equal, fill=1.0, base=0,
                                          pattern=[[-1, P]], channel_multiplier=1))
            g(nc.gpsimd.affine_select(out=core.before[:], in_=core.onesb[:], compare_op=ALU.is_gt, fill=0.0,
                                      base=0, pattern=[[1, P]], channel_multiplier=-1))
            for b in range(2):
                rows = slice(b * BLK, (b + 1) * BLK)
                m = core.ssd_mask[rows]
                g(nc.gpsimd.affine_select(out=m, in_=m, compare_op=ALU.is_ge, fill=NEG, base=0,
                                          pattern=[[0, MHEADS // 2], [1, BLK]], channel_multiplier=-1))
                g(nc.gpsimd.affine_select(out=core.upto[rows], in_=core.ones[rows, 0:BLK], compare_op=ALU.is_ge,
                                          fill=0.0, base=0, pattern=[[1, BLK]], channel_multiplier=-1))
                m = core.in_block[:, b]
                g(nc.gpsimd.affine_select(out=m, in_=m, compare_op=ALU.is_ge, fill=0.0, base=-b * BLK,
                                          pattern=[[0, P]], channel_multiplier=1))
                g(nc.gpsimd.affine_select(out=m, in_=m, compare_op=ALU.is_ge, fill=0.0, base=b * BLK + BLK - 1,
                                          pattern=[[0, P]], channel_multiplier=-1))
                g(nc.gpsimd.tensor_copy(core.own[:, b * BLK:(b + 1) * BLK], m[:, 0:BLK]))
                g(nc.gpsimd.tensor_copy(core.own_r[:, b * BLK:(b + 1) * BLK], m[:, 0:BLK]))
            g(nc.gpsimd.affine_select(out=core.upto_own[:], in_=core.own[:], compare_op=ALU.is_ge, fill=0.0,
                                      base=0, pattern=[[1, P]], channel_multiplier=-1))
            for which, own, prev in ((0, 0, None), (1, 0, 1), (2, 1, 0)):
                m = core.att_mask[:, which, own * P:own * P + P]
                g(nc.gpsimd.affine_select(out=m, in_=m, compare_op=ALU.is_ge, fill=NEG, base=0,
                                          pattern=[[-1, P]], channel_multiplier=1))
                if prev is not None:
                    m = core.att_mask[:, which, prev * P:prev * P + P]
                    g(nc.gpsimd.affine_select(out=m, in_=m, compare_op=ALU.is_ge, fill=NEG, base=0,
                                              pattern=[[1, P]], channel_multiplier=-1))
            g(nc.gpsimd.memset(core.att_mask[:, 0, P:2 * P], NEG))
            g(nc.gpsimd.memset(core.keep[:, 0:1], 0.0))
            g(nc.gpsimd.iota(core.count[:], [[1, P]], 0, 0, allow_small_or_imprecise_dtypes=True))
            g(nc.gpsimd.iota(core.rowid[:], [[P, TILES]], 0, 1, allow_small_or_imprecise_dtypes=True))
            g(nc.gpsimd.iota(core.spareid[:], [[0, 1]], ROWS, 1, allow_small_or_imprecise_dtypes=True))

        @block.sync
        def _(sp):
            sp.wait_ge(base_made, 1)
            for rows in spare_rows:
                sp.dma_start(rows, zero_rows).then_inc(zeroed, 16)
            sp.wait_ge(zeroed, 16 * len(spare_rows))


def attention(core, x_in, x_out, xn_rows, w_qkv, w_out, gate, w1_dram, w2_dram, w2_tail):
    nc, bank = core.nc, core.bank
    arena, at = core.arena, core.att_at
    wqkv, at = cut(arena, at, KD, 3 * D)
    wo, at = cut(arena, at, KD, D)
    x, at = cut(arena, at, 2, D)
    xn, at = cut(arena, at, D)
    xnT, at = cut(arena, at, KD, P)
    qz = []
    for par in range(2):
        q, at = cut(arena, at, HG, KD, P)
        qz.append(q)
    kT, at = cut(arena, at, KD, 2, P)
    v, at = cut(arena, at, 2, D)
    probs, at = cut(arena, at, 2, HG, 2 * P)
    probsT, at = cut(arena, at, 2, 4, P)
    oT, at = cut(arena, at, KD, P)
    xo, at = cut(arena, at, D)
    xres, at = cut(arena, at, 2, D)
    st, at = cut(arena, at, 6)
    mv, at = cut(arena, at, 2)
    var_eps, at = cut(arena, at, 1)
    rstd, at = cut(arena, at, 1)
    nmax, at = cut(arena, at, HEADS)
    psum_p, at = cut(arena, at, HEADS)
    rinv, at = cut(arena, at, HEADS)
    scored_at = at
    score_banks = ((bank[2], bank[3]), (bank[4], bank[5]))
    with stage_semaphores(nc, "att") as sem, ExitStack() as ctx:
        weights_in = [sem(f"w{k}_in") for k in range(2)]
        x_loaded = [sem("x_loaded0"), sem("x_loaded1")]
        again_loaded = [sem("again_loaded0"), sem("again_loaded1")]
        experts_in, gate_in = sem("experts_in"), sem("gate_in")
        chains = [sem("chain_first"), sem("chain_loop"), sem("chain_last")]
        cleared = sem("cleared")
        var_ready, rstd_ready, xn_ready = sem("var_ready"), sem("rstd_ready"), sem("xn_ready")
        x_turned, xnT_ready = sem("x_turned"), sem("xnT_ready")
        q_made, k_made, v_made = sem("q_made"), sem("k_made"), sem("v_made")
        q_ready, k_ready, v_ready = sem("q_ready"), sem("k_ready"), sem("v_ready")
        scores_made, max_ready, probs_ready = sem("scores_made"), sem("max_ready"), sem("probs_ready")
        probs_turned, probsT_ready, pv_made = sem("probs_turned"), sem("probsT_ready"), sem("pv_made")
        oT_ready = sem("oT_ready")
        sums_read, weights_ready = sem("sums_read"), sem("weights_ready")
        out_made, added, stored = sem("out_made"), sem("added"), sem("stored")
        scored = Scoring(core, sem, xn_rows, scored_at, scored_at + 2 * D)
        assert scored.end <= core.left, scored.end - core.left
        block = ctx.enter_context(nc.Block())

        @block.sync
        def _(sp):
            for par in range(2):
                sp.dma_start(x[:, par], x_in[par]).then_inc(x_loaded[par], 16)
            sp.dma_start(wqkv, w_qkv).then_inc(weights_in[0], 16)
            sp.dma_start(wo, w_out).then_inc(weights_in[1], 16)
            for par in range(2):
                sp.dma_start(xres[:, par], x_in[par]).then_inc(again_loaded[par], 16)
            sp.dma_start(core.gate[:], gate).then_inc(gate_in, 16)
            load_experts(core, sp, w1_dram, w2_dram, w2_tail, range(EXPERTS), range(core.att_experts), experts_in)

            def one(t):
                return slice(t, t + 1) if isinstance(t, int) else bass.ds(t, 1)

            def store(t, par):
                sp.wait_ge(added, t + 1)
                sp.dma_start(x_out[one(t)].rearrange("a p d -> p a d"), xo.unsqueeze(1)).then_inc(stored, 16)

            def load(t, par):
                sp.wait_ge(xn_ready, t - 1)
                sp.dma_start(x[:, par:par + 1], x_in[one(t)].rearrange("a p d -> p a d")).then_inc(x_loaded[par], 16)

            def load_again(t, par):
                sp.dma_start(xres[:, par:par + 1], x_in[one(t)].rearrange("a p d -> p a d"))\
                    .then_inc(again_loaded[par], 16)

            load(2, 0)
            load(3, 1)
            with sp.Fori(0, TURNS - 2) as i:
                for par in range(2):
                    t = 2 * i + par
                    store(t, par)
                    load_again(t + 2, par)
                    scored.store(sp, t)
                    load(t + 4, par)
            for t in range(TILES - 4, TILES):
                store(t, t % 2)
                if t < TILES - 2:
                    load_again(t + 2, t % 2)
                scored.store(sp, t)
            sp.wait_ge(stored, 16 * TILES)
            sp.wait_ge(scored.stored, 16 * TILES)
            sp.wait_ge(experts_in, 16 * (EXPERTS + 2))

        @block.gpsimd
        def _(pool):
            nc.gpsimd.memset(qz[0], 0.0).then_inc(cleared, 1)
            nc.gpsimd.memset(qz[1], 0.0).then_inc(cleared, 1)
            nc.gpsimd.memset(kT, 0.0).then_inc(cleared, 1)
            nc.gpsimd.memset(v, 0.0).then_inc(cleared, 1)

            def norm_power(n):
                pool.wait_ge(var_ready, n + 1)
                nc.gpsimd.tensor_tensor(rstd, var_eps, core.mhalf[:], ALU.pow).then_inc(rstd_ready, 1)

            norm_power(0)
            norm_power(1)
            norm_power(2)
            with pool.Fori(0, TILES - 3) as t:
                scored.power(pool, t)
                norm_power(t + 3)
            for t in range(TILES - 3, TILES):
                scored.power(pool, t)

        @block.vector
        def _(dve):
            def statistics(link, n, par, turn):
                dve.wait_ge(x_loaded[par], 16 * turn + 16)
                link(nc.vector.bn_stats(st, x[:, par]))
                nc.vector.nop(nofuse=True)
                after(dve, xn_ready, n)
                nc.vector.nop(nofuse=True)
                link(nc.vector.bn_aggr(mv, st))
                nc.vector.tensor_scalar(var_eps, mv[:, 1:2], EPS, None, ALU.add).then_inc(var_ready, 1)

            def normalise(n, par):
                dve.wait_ge(rstd_ready, n + 1)
                after(dve, x_turned, n)
                nc.vector.tensor_scalar(xn, x[:, par], mv[:, 0:1], rstd, ALU.subtract, ALU.mult).then_inc(xn_ready, 1)

            def keys_out(n, par):
                dve.wait_ge(k_made, n + 1)
                after(dve, scores_made, 4 * n)
                nc.vector.tensor_copy(kT[:, :, par], bank[0][:].rearrange("p (a b) -> p a b", b=P)).then_inc(k_ready, 1)

            def row_max(t, g):
                dve.wait_ge(scores_made, 4 * t + g + 1)
                if g == 0:
                    after(dve, probs_ready, 4 * t)
                for pair in range(2):
                    last = nc.vector.tensor_reduce(
                        nmax[:, HG * g + 2 * pair:HG * g + 2 * pair + 2],
                        score_banks[g % 2][pair][:].rearrange("p (h j) -> p h j", h=2),
                        AX.X, ALU.max, negate=True)
                last.then_inc(max_ready, 1)

            def probs_out(t, g):
                for half, b in ((0, 6), (1, 1)):
                    dve.wait_ge(probs_turned, 8 * t + 2 * g + half + 1)
                    after(dve, pv_made, 4 * t + g)
                    nc.vector.tensor_copy(probsT[:, half], bank[b][:].rearrange("p (a b) -> p a b", b=P))\
                        .then_inc(probsT_ready, 1)

            def weights_out(t, g):
                heads = slice(HG * g, HG * g + HG)
                dve.wait_ge(probs_ready, 4 * t + g + 1)
                nc.vector.reciprocal(rinv[:, heads], psum_p[:, heads]).then_inc(sums_read, 1)
                dve.wait_ge(sums_read, 4 * t + g + 1)
                nc.vector.tensor_tensor(probs[:, g % 2], probs[:, g % 2], spread(rinv[:, heads], 2, 2 * P), ALU.mult)\
                    .then_inc(weights_ready, 1)

            def add_input(t, par, turn):
                dve.wait_ge(again_loaded[par], 16 * turn + 16)
                dve.wait_ge(out_made, t + 1)
                after(dve, stored, 16 * t)
                nc.vector.tensor_tensor(xo, bank[1][:], xres[:, par], ALU.add).then_inc(added, 1)

            def step(link, t, par, turn, first=False, front=True, load=True):
                weights_out(t, 0)
                probs_out(t, 0)
                row_max(t, 2)
                weights_out(t, 1)
                if not first:
                    add_input(t - 1, 1 - par, turn if par else turn - 1)
                if not first:
                    dve.wait_ge(added, t)
                    scored.statistics(dve, link, xo)
                probs_out(t, 1)
                if not first:
                    scored.normalise(dve, t - 1, xo)
                row_max(t, 3)
                weights_out(t, 2)
                if load:
                    statistics(link, t + 2, par, turn + 1)
                if front:
                    keys_out(t + 1, 1 - par)
                if not first:
                    scored.logits_out(dve, t - 1, bank[1])
                probs_out(t, 2)
                weights_out(t, 3)
                if front:
                    row_max(t + 1, 0)
                probs_out(t, 3)
                if front:
                    row_max(t + 1, 1)
                if load:
                    normalise(t + 2, par)

            dve.wait_ge(cleared, 4)
            link = Chain(dve, chains[0])
            statistics(link, 0, 0, 0)
            normalise(0, 0)
            keys_out(0, 0)
            statistics(link, 1, 1, 0)
            normalise(1, 1)
            row_max(0, 0)
            row_max(0, 1)
            step(link, 0, 0, 0, first=True)
            link = Chain(dve, chains[1], 0, 4)
            step(link, 1, 1, 0)
            link.end()
            with dve.Fori(1, TURNS - 1) as i:
                link = Chain(dve, chains[1], 2 * i - 1, 4)
                step(link, 2 * i, 0, i)
                link.end()
                link = Chain(dve, chains[1], 2 * i, 4)
                step(link, 2 * i + 1, 1, i)
                link.end()
            link = Chain(dve, chains[2])
            step(link, TILES - 2, 0, TURNS - 1, load=False)
            step(link, TILES - 1, 1, TURNS - 1, front=False, load=False)
            add_input(TILES - 1, 1, TURNS - 1)
            dve.wait_ge(added, TILES)
            scored.statistics(dve, link, xo)
            scored.normalise(dve, TILES - 1, xo)
            scored.logits_out(dve, TILES - 1, bank[1])

        @block.scalar
        def _(act):
            def by_chunk(v):
                return v.rearrange("p (a b) -> p a b", b=P)

            def rows_out(n):
                act.wait_ge(x_turned, n + 1)
                after(act, v_made, n)
                nc.scalar.activation(xnT, by_chunk(bank[0][:]), ACT.Copy).then_inc(xnT_ready, 1)

            def queries_out(n, par):
                act.wait_ge(q_made, n + 1)
                after(act, scores_made, 4 * (n - 1))
                for r in range(HG):
                    rows = slice(HD * r, HD * r + HD)
                    last = nc.scalar.activation(qz[par][rows, r], by_chunk(bank[0][rows, :]), ACT.Copy,
                                                scale=float(HD) ** -0.5)
                last.then_inc(q_ready, 1)

            def new_values_out(n, par):
                act.wait_ge(v_made, n + 1)
                after(act, pv_made, 4 * n)
                nc.scalar.activation(v[:, par], bank[0][:], ACT.Copy).then_inc(v_ready, 1)

            def exponentials(t, g):
                act.wait_ge(max_ready, 4 * t + g + 1)
                after(act, sums_read, 4 * (t - 1) + g + 1)
                after(act, probs_turned, 8 * t + 2 * (g - 1))
                for r in range(HG):
                    h = HG * g + r
                    last = nc.scalar.activation(
                        probs[:, g % 2, r], score_banks[g % 2][r // 2][:, (r % 2) * 2 * P:(r % 2 + 1) * 2 * P],
                        ACT.Exp, bias=nmax[:, h:h + 1], accum_out=psum_p[:, h:h + 1])
                last.then_inc(probs_ready, 1)

            def o_out(t):
                act.wait_ge(pv_made, 4 * t + 4)
                after(act, out_made, t)
                nc.scalar.activation(oT, by_chunk(bank[7][:]), ACT.Copy).then_inc(oT_ready, 1)

            def step(t, par, first=False, front=True):
                exponentials(t, 0)
                if not first:
                    o_out(t - 1)
                new_values_out(t, par)
                exponentials(t, 1)
                if front:
                    rows_out(t + 1)
                exponentials(t, 2)
                if front:
                    queries_out(t + 1, 1 - par)
                exponentials(t, 3)
                if not first:
                    scored.turned_out(act, t - 1, bank[6])

            act.wait_ge(cleared, 4)
            rows_out(0)
            queries_out(0, 0)
            for par in range(2):
                step(par, par, first=(par == 0))
            with act.Fori(1, TURNS - 1) as i:
                for par in range(2):
                    step(2 * i + par, par)
            step(TILES - 2, 0)
            step(TILES - 1, 1, front=False)
            o_out(TILES - 1)
            scored.turned_out(act, TILES - 1, bank[6])

        @block.tensor
        def _(pe):
            def turn_rows(n):
                pe.wait_ge(xn_ready, n + 1)
                after(pe, v_ready, n)
                for k in range(KD):
                    last = nc.tensor.transpose(bank[0][:, k * P:k * P + P], xn[:, k * P:k * P + P], core.ident[:])
                last.then_inc(x_turned, 1)

            def channels(n, first, free, done):
                pe.wait_ge(free, n + 1)
                for c in range(KD):
                    for k in range(KD):
                        last = nc.tensor.matmul(bank[0][:, c * P:c * P + P],
                                                wqkv[:, k, first + c * P:first + c * P + P], xnT[:, k],
                                                start=(k == 0), stop=(k == KD - 1))
                last.then_inc(done, 1)

            def queries(n):
                channels(n, 0, xnT_ready, q_made)

            def keys(n):
                channels(n, D, q_ready, k_made)

            def new_values(n):
                pe.wait_ge(k_ready, n + 1)
                for k in range(KD):
                    last = nc.tensor.matmul(bank[0][:], xnT[:, k], wqkv[:, k, 2 * D:3 * D],
                                            start=(k == 0), stop=(k == KD - 1))
                last.then_inc(v_made, 1)

            def scores(t, par, turn, g):
                if g == 0:
                    pe.wait_ge(q_ready, t + 1)
                    pe.wait_ge(k_ready, t + 1)
                after(pe, probs_ready, 4 * t + g - 1)
                for r in range(HG):
                    out = score_banks[g % 2][r // 2][:, (r % 2) * 2 * P:(r % 2 + 1) * 2 * P]
                    if par == 0:
                        which = 1 - (TURNS_PER_BATCH - turn % TURNS_PER_BATCH) // TURNS_PER_BATCH
                        mask = core.att_mask[:, bass.ds(which, 1)].rearrange("p a j -> p (a j)")
                    else:
                        mask = core.att_mask[:, 2]
                    nc.tensor.matmul(out, core.identb[:], mask, start=True, stop=False)
                    last = nc.tensor.matmul(out, qz[par][:, r, g], kT[:, g].rearrange("p a j -> p (a j)"),
                                            start=False, stop=True)
                last.then_inc(scores_made, 1)

            def turn_probs(t, g):
                pe.wait_ge(weights_ready, 4 * t + g + 1)
                for half, b in ((0, 6), (1, 1)):
                    if g == 1 and half == 1:
                        after(pe, added, t)
                    if g == 2:
                        after(pe, scored.ready if half else scored.xnT_ready, t)
                    for j in range(4):
                        last = nc.tensor.transpose(bank[b][:, j * P:j * P + P],
                                                   probs[:, g % 2, 2 * half + j // 2, (j % 2) * P:(j % 2 + 1) * P],
                                                   core.ident[:])
                    last.then_inc(probs_turned, 1)

            def values(t, g):
                if g == 0:
                    pe.wait_ge(v_ready, t + 1)
                    after(pe, oT_ready, t)
                pe.wait_ge(probsT_ready, 8 * t + 2 * g + 2)
                for s in range(2):
                    for r in range(HG):
                        h = HG * g + r
                        last = nc.tensor.matmul(bank[7][HD * r:HD * r + HD, g * P:g * P + P],
                                                v[:, s, h * HD:h * HD + HD], probsT[:, r // 2, 2 * (r % 2) + s],
                                                start=(s == 0), stop=(s == 1))
                last.then_inc(pv_made, 1)

            def output(t):
                pe.wait_ge(oT_ready, t + 1)
                for k in range(KD):
                    last = nc.tensor.matmul(bank[1][:], oT[:, k], wo[:, k], start=(k == 0), stop=(k == KD - 1))
                last.then_inc(out_made, 1)

            def step(t, par, turn, first=False, front=True):
                turn_probs(t, 0)
                scores(t, par, turn, 2)
                if front:
                    turn_rows(t + 1)
                values(t, 0)
                if not first:
                    output(t - 1)
                if front:
                    queries(t + 1)
                turn_probs(t, 1)
                scores(t, par, turn, 3)
                values(t, 1)
                if not first:
                    scored.turn(pe, t - 1, bank[6])
                if front:
                    keys(t + 1)
                if not first:
                    scored.product(pe, t - 1, bank[1])
                turn_probs(t, 2)
                turn_next = turn + 1 if par else turn
                if front:
                    scores(t + 1, 1 - par, turn_next, 0)
                values(t, 2)
                turn_probs(t, 3)
                if front:
                    scores(t + 1, 1 - par, turn_next, 1)
                values(t, 3)
                if front:
                    new_values(t + 1)

            pe.wait_ge(weights_in[0], 16)
            pe.wait_ge(weights_in[1], 16)
            pe.wait_ge(gate_in, 16)
            turn_rows(0)
            queries(0)
            keys(0)
            new_values(0)
            scores(0, 0, 0, 0)
            scores(0, 0, 0, 1)
            for par in range(2):
                step(par, par, 0, first=(par == 0))
            with pe.Fori(1, TURNS - 1) as i:
                for par in range(2):
                    step(2 * i + par, par, i)
            step(TILES - 2, 0, TURNS - 1)
            step(TILES - 1, 1, TURNS - 1, front=False)
            output(TILES - 1)
            scored.turn(pe, TILES - 1, bank[6])
            pe.wait_ge(added, TILES)
            scored.product(pe, TILES - 1, bank[1])


def load_experts(core, eng, w1_dram, w2_dram, w2_tail, w1_of, w2_of, done):
    for e in w1_of:
        eng.dma_start(core.w1[:, e * W1E:(e + 1) * W1E], w1_dram[:, e]).then_inc(done, 16)
    w2 = core.w2.rearrange("p (e k d) -> p e k d", e=EXPERTS, k=KI)
    some = slice(w2_of.start, w2_of.stop)
    eng.dma_start(w2[:, some, 0:KI - 1], w2_dram[:, some]).then_inc(done, 16)
    eng.dma_start(w2[0:LAST_I, some, KI - 1], w2_tail[:, some]).then_inc(done, 16)


def experts(core, tag, x_rows, xn_rows, w1_dram, w2_dram, w2_tail, w1_of, w2_of, in_w):
    arena, at = core.arena, core.work_at
    index, at = cut(arena, at, SLOTS)
    weight, at = cut(arena, at, SLOTS)
    owner, at = cut(arena, at, SLOTS)
    index, owner = index.bitcast(U32), owner.bitcast(I32)
    with stage_semaphores(core.nc, tag) as sem:
        weights_in = sem("weights_in")
        sort_rows(core, sem, index, weight, owner, at,
                  lambda sp: load_experts(core, sp, w1_dram, w2_dram, w2_tail, w1_of, w2_of, weights_in))
        run_slots(core, tag, sem, x_rows, xn_rows, index, weight, owner, weights_in, 16 * (len(w1_of) + 2), in_w, at)


def sort_rows(core, sem, index, weight, owner, at, start_loads):
    nc, bank, arena = core.nc, core.bank, core.arena
    E, T, K = EXPERTS, TILES, TOPK
    logits = core.logits
    best, at = cut(arena, at, T, 8)
    which, at = cut(arena, at, T, 8)
    which_f, at = cut(arena, at, T, K)
    chosen, at = cut(arena, at, K, T * E)
    both, at = cut(arena, at, (T + 1) * E)
    both = both.bitcast(BF16)[:, 0:(T + 1) * E].rearrange("p (t e) -> p t e", e=E)
    gap, at = cut(arena, at, T)
    gap_exp, at = cut(arena, at, T)
    den, at = cut(arena, at, T)
    w, at = cut(arena, at, K, T)
    need, at = cut(arena, at, E)
    need_i, at = cut(arena, at, E)
    slots_i, at = cut(arena, at, E)
    slots, at = cut(arena, at, E)
    end, at = cut(arena, at, E)
    start, at = cut(arena, at, E)
    place, at = cut(arena, at, T * E)
    picked, at = cut(arena, at, K, T * E)
    entry, at = cut(arena, at, K * T)
    entry_i, at = cut(arena, at, K * T)
    slot_i, at = cut(arena, at, K * T)
    spot_i, at = cut(arena, at, K * T)
    slot, at = cut(arena, at, K * T)
    spot, at = cut(arena, at, K * T)
    at_spot, at = cut(arena, at, K * T, P)
    by_slot, at = cut(arena, at, 3, K * T, SLOTS)
    empty, at = cut(arena, at, SLOTS)
    index_f, at = cut(arena, at, SLOTS)
    past, at = cut(arena, at, SLOTS, E)
    owner_f, at = cut(arena, at, SLOTS)
    assert at <= core.left
    chain = sem("sort_chain")
    both_ready, ranks_made, gap_ready, exp_ready = sem("both"), sem("ranks"), sem("gap"), sem("exp")
    tables_ready, lists_made = sem("tables"), sem("lists")
    with nc.Block() as block:
        @block.sync
        def _(sp):
            start_loads(sp)

        @block.vector
        def _(dve):
            link = Chain(dve, chain)
            for t in range(T):
                last = nc.vector.max(best[:, t], logits[:, t])
            link(last)
            for t in range(T):
                last = nc.vector.max_index(which.bitcast(U32)[:, t], best[:, t], logits[:, t])
            link(last)
            nc.vector.tensor_tensor(gap, best[:, :, 1], best[:, :, 0], ALU.subtract).then_inc(gap_ready, 1)
            link(nc.vector.tensor_copy(which_f, which.bitcast(U32)[:, :, 0:K]))
            for k in range(K):
                last = nc.vector.tensor_tensor(chosen[:, k].rearrange("p (t e) -> p t e", e=E),
                                               spread(core.count[:, 0:E], 1, T), spread(which_f[:, :, k], 2, E),
                                               ALU.is_equal)
            link(last)
            link(nc.vector.memset(both[:, T], 0.0))
            nc.vector.tensor_tensor(both[:, 0:T].rearrange("p t e -> p (t e)"), chosen[:, 0], chosen[:, 1], ALU.add)\
                .then_inc(both_ready, 1)
            dve.wait_ge(exp_ready, 1)
            link(nc.vector.tensor_scalar(den, gap_exp, 1.0, None, ALU.add))
            link(nc.vector.reciprocal(w[:, 0], den))
            link(nc.vector.tensor_tensor(w[:, 1], gap_exp, w[:, 0], ALU.mult))
            dve.wait_ge(ranks_made, 1)
            link(nc.vector.tensor_scalar(need, bank[0][:, T * E:(T + 1) * E], float(P - 1), None, ALU.add))
            link(nc.vector.tensor_copy(need_i.bitcast(I32), need))
            link(nc.vector.tensor_scalar(slots_i.bitcast(I32), need_i.bitcast(I32), 7, None, ALU.logical_shift_right))
            link(nc.vector.tensor_copy(slots, slots_i.bitcast(I32)))
            link(nc.vector.tensor_tensor_scan(end, slots, core.zero[:, 0:E], 0.0, ALU.add, ALU.add))
            link(nc.vector.tensor_tensor(start, end, slots, ALU.subtract))
            link(nc.vector.tensor_scalar(start, start, float(P), None, ALU.mult))
            link(nc.vector.tensor_tensor(place.rearrange("p (t e) -> p t e", e=E),
                                         bank[0][:, 0:T * E].rearrange("p (t e) -> p t e", e=E),
                                         spread(start, 1, T), ALU.add))
            link(nc.vector.tensor_tensor(picked, chosen, spread(place, 1, K), ALU.mult))
            link(nc.vector.tensor_reduce(entry, picked.rearrange("p k (t e) -> p (k t) e", e=E), AX.X, ALU.add))
            link(nc.vector.tensor_copy(entry_i.bitcast(I32), entry))
            link(nc.vector.tensor_scalar(slot_i.bitcast(I32), entry_i.bitcast(I32), 7, None, ALU.logical_shift_right))
            link(nc.vector.tensor_scalar(spot_i.bitcast(I32), entry_i.bitcast(I32), P - 1, None, ALU.bitwise_and))
            link(nc.vector.tensor_copy(slot, slot_i.bitcast(I32)))
            link(nc.vector.tensor_copy(spot, spot_i.bitcast(I32)))
            link(nc.vector.tensor_tensor(at_spot, spread(core.count[:], 1, K * T), spread(spot, 2, P), ALU.is_equal))
            link(nc.vector.tensor_tensor(by_slot[:, 2], spread(core.count[:, 0:SLOTS], 1, K * T),
                                         spread(slot, 2, SLOTS), ALU.is_equal))
            for k in range(K):
                part = slice(k * T, (k + 1) * T)
                link(nc.vector.tensor_tensor(by_slot[:, 0, part], by_slot[:, 2, part],
                                             spread(core.rowid[:], 2, SLOTS), ALU.mult))
            for k in range(K):
                part = slice(k * T, (k + 1) * T)
                last = nc.vector.tensor_tensor(by_slot[:, 1, part], by_slot[:, 2, part],
                                               spread(w[:, k], 2, SLOTS), ALU.mult)
            last.then_inc(tables_ready, 1)
            link(nc.vector.tensor_tensor(past, spread(core.count[:, 0:SLOTS], 2, E), spread(end, 1, SLOTS), ALU.is_ge))
            link(nc.vector.tensor_reduce(owner_f, past, AX.X, ALU.add))
            link(nc.vector.tensor_scalar(owner_f, owner_f, float(E - 1), None, ALU.min))
            link(nc.vector.tensor_copy(owner, owner_f))
            dve.wait_ge(lists_made, 1)
            link(nc.vector.tensor_scalar(empty, bank[1][:, 2 * SLOTS:3 * SLOTS], -1.0, 1.0, ALU.mult, ALU.add))
            link(nc.vector.scalar_tensor_tensor(out=index_f, in0=empty, scalar=core.spareid[:], in1=bank[1][:, 0:SLOTS],
                                                op0=ALU.mult, op1=ALU.add))
            link(nc.vector.tensor_copy(index, index_f))
            link(nc.vector.tensor_copy(weight, bank[1][:, SLOTS:2 * SLOTS]))

        @block.scalar
        def _(act):
            act.wait_ge(gap_ready, 1)
            nc.scalar.activation(gap_exp, gap, ACT.Exp).then_inc(exp_ready, 1)

        @block.tensor
        def _(pe):
            pe.wait_ge(both_ready, 1)
            nc.tensor.matmul(bank[0][:, 0:(T + 1) * E], core.before[:], both.rearrange("p t e -> p (t e)"),
                             start=True, stop=False)
            for t in range(T):
                last = nc.tensor.matmul(bank[0][:, (t + 1) * E:(T + 1) * E].rearrange("p (t e) -> p t e", e=E),
                                        core.onesb[:], spread(both[:, t], 1, T - t), start=False, stop=(t == T - 1))
            last.then_inc(ranks_made, 1)
            pe.wait_ge(tables_ready, 1)
            for j in range(K * T):
                last = nc.tensor.matmul(bank[1][:, 0:3 * SLOTS].rearrange("p (c s) -> p c s", c=3), at_spot[:, j],
                                        by_slot[:, :, j], start=(j == 0), stop=(j == K * T - 1))
            last.then_inc(lists_made, 1)


def run_slots(core, tag, sem, x_rows, xn_rows, index, weight, owner, weights_in, weights_count, in_w, at):
    nc, bank, arena = core.nc, core.bank, core.arena
    rows, at = cut(arena, at, 2, D)
    rowsT, at = cut(arena, at, 2, KD * P)
    silu, at = cut(arena, at, 2, INTER)
    actT, at = cut(arena, at, 2, KI, P)
    y, at = cut(arena, at, 2, D)
    from_rows, at = cut(arena, at, 2)
    to_rows, at = cut(arena, at, 2)
    from_rows, to_rows = from_rows.bitcast(U32), to_rows.bitcast(U32)
    assert at <= core.w_in_at
    w1 = core.w1.rearrange("p (e n) -> p e n", e=EXPERTS)
    w2 = core.w2.rearrange("p (e n) -> p e n", e=EXPERTS)
    picked, placed = sem("index_read"), sem("index_to")
    *gathered, added = core.pool_dma[tag]
    rows_turned, rowsT_ready, up_made, silu_ready = sem("rows_turned"), sem("rowsT_ready"), sem("up"), sem("silu")
    act_ready, act_turned, actT_ready = sem("act_ready"), sem("act_turned"), sem("actT_ready")
    y_made, y_ready = sem("y_made"), sem("y_ready")
    turns = SLOTS // 2
    gate_made, mixer_in = sem("gate_made"), sem("mixer_in")
    with nc.Block() as block:
        @block.sync
        def _(sp):
            if in_w is not None:
                sp.wait_ge(rows_turned, 2)
                sp.dma_start(core.arena[:, core.w_in_at:core.left], in_w.rearrange("p k n -> p (k n)"))\
                    .then_inc(mixer_in, 16)
                sp.wait_ge(mixer_in, 16)

        @block.gpsimd
        def _(pool):
            def gather(s, par):
                after(pool, rows_turned, s - 1)
                nc.gpsimd.nop(nofuse=True)
                nc.gpsimd.tensor_copy(from_rows[:, par:par + 1], index[:, bass.ds(s, 1)]).then_inc(picked, 1)
                pool.wait_ge(picked, s + 1)
                nc.gpsimd.nop(nofuse=True)
                nc.gpsimd.indirect_dma_start(
                    out=rows[:, par], out_offset=None, in_=xn_rows,
                    in_offset=bass.IndirectOffsetOnAxis(ap=from_rows[:, par:par + 1], axis=0))\
                    .then_inc(gathered[par], 16)

            def add(s, par):
                nc.gpsimd.tensor_copy(to_rows[:, par:par + 1], index[:, bass.ds(s, 1)]).then_inc(placed, 1)
                pool.wait_ge(placed, s + 1)
                pool.wait_ge(y_ready, s + 1)
                after(pool, added, 16 * s)
                nc.gpsimd.nop(nofuse=True)
                nc.gpsimd.indirect_dma_start(
                    out=x_rows, out_offset=bass.IndirectOffsetOnAxis(ap=to_rows[:, par:par + 1], axis=0),
                    in_=y[:, par], in_offset=None, compute_op=ALU.add).then_inc(added, 16)

            for s in range(4):
                gather(s, s % 2)
            for par in range(2):
                gather(4 + par, par)
                add(par, par)
            with pool.Fori(1, turns - 2) as i:
                for par in range(2):
                    gather(2 * i + 4 + par, par)
                    add(2 * i + par, par)
            for s in range(SLOTS - 4, SLOTS):
                add(s, s % 2)
            pool.wait_ge(added, 16 * SLOTS)

        @block.scalar
        def _(act):
            def turned(s, par):
                act.wait_ge(rows_turned, s + 1)
                after(act, up_made, s - 1)
                nc.scalar.activation(rowsT[:, par], bank[0][:], ACT.Copy).then_inc(rowsT_ready, 1)

            def gated(s, par):
                act.wait_ge(gate_made, s + 1)
                after(act, act_turned, s - 1)
                nc.scalar.activation(silu[:, par], bank[1 + 2 * par][:, 0:INTER], ACT.Silu).then_inc(silu_ready, 1)

            def result(s, par):
                act.wait_ge(y_made, s + 1)
                after(act, added, 16 * (s - 1))
                nc.scalar.activation(y[:, par], bank[6 + par][:], ACT.Copy).then_inc(y_ready, 1)

            def step(s, par):
                gated(s + 1, 1 - par)
                turned(s + 2, par)
                result(s, par)

            turned(0, 0)
            turned(1, 1)
            gated(0, 0)
            for par in range(2):
                step(par, par)
            with act.Fori(1, turns - 1) as i:
                for par in range(2):
                    step(2 * i + par, par)
            gated(SLOTS - 1, 1)
            result(SLOTS - 2, 0)
            result(SLOTS - 1, 1)

        @block.vector
        def _(dve):
            def product(s, par):
                dve.wait_ge(silu_ready, s + 1)
                dve.wait_ge(up_made, s + 1)
                nc.vector.nop(nofuse=True)
                nc.vector.scalar_tensor_tensor(out=silu[:, par], in0=silu[:, par], scalar=weight[:, bass.ds(s, 1)],
                                               in1=bank[2 + 2 * par][:, 0:INTER], op0=ALU.mult, op1=ALU.mult)\
                    .then_inc(act_ready, 1)

            def act_out(s, par):
                dve.wait_ge(act_turned, s + 1)
                after(dve, y_made, s - 1)
                nc.vector.tensor_copy(actT[:, par, 0:KI - 1],
                                      bank[5][:, 0:(KI - 1) * P].rearrange("p (a b) -> p a b", b=P))
                nc.vector.tensor_copy(actT[0:LAST_I, par, KI - 1], bank[5][0:LAST_I, (KI - 1) * P:KI * P])\
                    .then_inc(actT_ready, 1)

            def step(s, par):
                act_out(s, par)
                product(s + 1, 1 - par)

            product(0, 0)
            for par in range(2):
                step(par, par)
            with dve.Fori(1, turns - 1) as i:
                for par in range(2):
                    step(2 * i + par, par)
            step(SLOTS - 2, 0)
            act_out(SLOTS - 1, 1)

        @block.tensor
        def _(pe):
            def turn(s, par, turn):
                pe.wait_ge(gathered[par], 16 * turn + 16)
                after(pe, rowsT_ready, s)
                for k in range(KD):
                    last = nc.tensor.transpose(bank[0][:, k * P:k * P + P], rows[:, par, k * P:k * P + P],
                                               core.ident[:])
                last.then_inc(rows_turned, 1)

            def up(s, par, part, e):
                if part == 0:
                    pe.wait_ge(rowsT_ready, s + 1)
                    after(pe, act_ready, s - 1)
                for k in range(KD):
                    at = (2 * k + part) * INTER
                    last = nc.tensor.matmul(bank[1 + 2 * par + part][:, 0:INTER], rowsT[:, par, k * P:k * P + P],
                                            w1[:, bass.ds(e, 1), at:at + INTER].rearrange("p a n -> p (a n)"),
                                            start=(k == 0), stop=(k == KD - 1))
                last.then_inc(up_made if part else gate_made, 1)

            def turn_act(s, par):
                pe.wait_ge(act_ready, s + 1)
                after(pe, actT_ready, s)
                for k in range(KI):
                    n = P if k < KI - 1 else LAST_I
                    last = nc.tensor.transpose(bank[5][0:n, k * P:k * P + P], silu[:, par, k * P:k * P + n],
                                               core.ident[:])
                last.then_inc(act_turned, 1)

            def expert_of(s):
                return pe.value_load(owner[0:1, bass.ds(s, 1)], min_val=0, max_val=EXPERTS - 1)

            def down(s, par, e):
                pe.wait_ge(actT_ready, s + 1)
                after(pe, y_ready, s - 1)
                for k in range(KI):
                    n = P if k < KI - 1 else LAST_I
                    last = nc.tensor.matmul(bank[6 + par][:], actT[0:n, par, k],
                                            w2[0:n, bass.ds(e, 1), k * D:k * D + D].rearrange("p a n -> p (a n)"),
                                            start=(k == 0), stop=(k == KI - 1))
                last.then_inc(y_made, 1)

            def step(s, par, turn_after):
                mine, following = expert_of(s), expert_of(s + 1)
                up(s + 1, 1 - par, 0, following)
                turn_act(s, par)
                up(s + 1, 1 - par, 1, following)
                turn(s + 2, par, turn_after)
                down(s, par, mine)

            turn(0, 0, 0)
            pe.wait_ge(weights_in, weights_count)
            first = expert_of(0)
            up(0, 0, 0, first)
            up(0, 0, 1, first)
            turn(1, 1, 0)
            for par in range(2):
                step(par, par, 1)
            with pe.Fori(1, turns - 1) as i:
                for par in range(2):
                    step(2 * i + par, par, i + 1)
            before_last, last_one = expert_of(SLOTS - 2), expert_of(SLOTS - 1)
            up(SLOTS - 1, 1, 0, last_one)
            turn_act(SLOTS - 2, 0)
            up(SLOTS - 1, 1, 1, last_one)
            down(SLOTS - 2, 0, before_last)
            turn_act(SLOTS - 1, 1)
            down(SLOTS - 1, 1, last_one)


def mamba(core, x_in, x_out, xn_rows, out_w, conv_w, conv_b, a_log, d_skip, dt_bias, norm_w):
    nc, bank, arena = core.nc, core.bank, core.arena
    H = MHEADS
    halo = TAPS - 1
    at = core.mamba_at
    w_in, _ = cut(arena, core.w_in_at, KD, WIN_COLS)
    w_out, at = cut(arena, at, KY, D)
    taps, at = cut(arena, at, CB, TAPS)
    tap_bias, at = cut(arena, at, CB)
    norm, at = cut(arena, at, KY)
    a_row, at = cut(arena, at, H)
    d_row, at = cut(arena, at, H)
    dtb_row, at = cut(arena, at, H)
    x, at = cut(arena, at, 2, D)
    xres, at = cut(arena, at, 2, D)
    xn, at = cut(arena, at, D)
    xnT, at = cut(arena, at, KD, P)
    cin = []
    for par in range(2):
        c, at = cut(arena, at, CB, halo + P)
        cin.append(c)
    conv, at = cut(arena, at, CB, P)
    xc, at = cut(arena, at, 2, CB, P)
    zs, at = cut(arena, at, 2, INNER)
    decays, at = cut(arena, at, 2, H // 2, BLK)
    mixed, at = cut(arena, at, H, P)
    steps = core.halves
    xs_at = at
    xs, at = cut(arena, at, INNER)
    xskip, at = cut(arena, at, INNER)
    xdt, at = cut(arena, at, INNER)
    xlast, at = cut(arena, at, INNER)
    state, at = cut(arena, at, INNER)
    ysum, at = cut(arena, at, INNER)
    y, at = cut(arena, at, INNER)
    state_mid = y
    yT, at = cut(arena, at, KY, P)
    xo, at = cut(arena, at, D)
    b_rows, at = cut(arena, at, 2, STATE)
    st, at = cut(arena, at, 6)
    mv, at = cut(arena, at, 2)
    var_eps, at = cut(arena, at, 1)
    rstd, at = cut(arena, at, 1)
    u, at = cut(arena, at, H)
    mag, at = cut(arena, at, H)
    e_mag, at = cut(arena, at, H)
    ratio, at = cut(arena, at, H)
    ratio2, at = cut(arena, at, H)
    series, at = cut(arena, at, H)
    dt, at = cut(arena, at, 2, H)
    da, at = cut(arena, at, 2, H)
    da_parts, at = cut(arena, at, 2, H)
    sums, at = cut(arena, at, 4 * H)
    ncs, at = cut(arena, at, H)
    gap, at = cut(arena, at, H)
    to_end, at = cut(arena, at, H)
    exps, at = cut(arena, at, 3 * H)
    carried, at = cut(arena, at, H)
    squares, at = cut(arena, at, 1)
    mean_eps, at = cut(arena, at, 1)
    rinv, at = cut(arena, at, 1)
    scored_at = at
    small = bank[2]
    state_banks = ((7, 3), (4, 7))
    CS, BC, BROWS, DT = 0, P, 2 * P, 2 * P
    blocks = [slice(b * BLK, (b + 1) * BLK) for b in range(2)]
    parts = (slice(KY, CB), slice(0, KY // 2), slice(KY // 2, KY))
    part_banks = (bank[1], bank[0], bank[1])
    with stage_semaphores(nc, "mam") as sem, ExitStack() as ctx:
        w_out_here, rows_here = sem("w_out"), sem("rows_here")
        x_loaded = [sem("x_loaded0"), sem("x_loaded1")]
        again_loaded = [sem("again_loaded0"), sem("again_loaded1")]
        chains = [sem("chain_first"), sem("chain_loop"), sem("chain_last")]
        cleared, a_exp, a_ready = sem("cleared"), sem("a_exp"), sem("a_ready")
        var_ready, rstd_ready, xn_ready = sem("var_ready"), sem("rstd_ready"), sem("xn_ready")
        x_turned, xnT_ready = sem("x_turned"), sem("xnT_ready")
        front_made, cin_ready, tap_ready, conv_ready, xc_ready, z_ready = (
            sem("front_made"), sem("cin_ready"), sem("tap_ready"), sem("conv_ready"), sem("xc_ready"), sem("z_ready"))
        mag_ready, e_mag_ready, da_ready = sem("mag"), sem("e_mag"), sem("da_ready")
        parts_ready, steps_ready = sem("da_parts"), sem("steps")
        xs_turned, xs_ready, small_made, b_ready = sem("xs_turned"), sem("xs_ready"), sem("small"), sem("b_ready")
        sums_ready = sem("sums_ready")
        gap_ready, exps_ready, to_end_ready, carried_ready = sem("gap"), sem("exps"), sem("to_end"), sem("carried")
        xdt_ready, xskip_ready, xlast_ready = sem("xdt"), sem("xskip"), sem("xlast")
        sums_made, decays_ready, mixed_ready, yd_made = sem("sums"), sem("decays"), sem("mixed"), sem("yd_made")
        yo_made, yo_read, ysum_ready, y_ready = sem("yo_made"), sem("yo_read"), sem("ysum"), sem("y_ready")
        st_made, mid_ready, decayed, state_ready = sem("st_made"), sem("mid_ready"), sem("decayed"), sem("state_ready")
        y_turned, yT_ready, squares_ready = sem("y_turned"), sem("yT_ready"), sem("squares")
        mean_ready, rinv_ready = sem("mean"), sem("rinv")
        out_made, added, stored = sem("out_made"), sem("added"), sem("stored")
        scored = Scoring(core, sem, xn_rows, xs_at, scored_at)
        assert scored.end <= core.w_in_at, scored.end - core.w_in_at
        block = ctx.enter_context(nc.Block())

        def by_head(v):
            return v.rearrange("p (h d) -> p h d", h=v.shape[1] // MHD)

        def by_chunk(v):
            return v.rearrange("p (a b) -> p a b", b=P)

        @block.sync
        def _(sp):
            def one(t):
                return slice(t, t + 1) if isinstance(t, int) else bass.ds(t, 1)

            def store(t):
                sp.wait_ge(added, t + 1)
                sp.dma_start(x_out[one(t)].rearrange("a p d -> p a d"), xo.unsqueeze(1)).then_inc(stored, 16)

            def load(t, par):
                sp.wait_ge(xn_ready, t - 1)
                sp.dma_start(x[:, par:par + 1], x_in[one(t)].rearrange("a p d -> p a d")).then_inc(x_loaded[par], 16)

            def load_again(t, par):
                sp.dma_start(xres[:, par:par + 1], x_in[one(t)].rearrange("a p d -> p a d"))\
                    .then_inc(again_loaded[par], 16)

            for par in range(2):
                sp.dma_start(x[:, par], x_in[par]).then_inc(x_loaded[par], 16)
            for dst, src in ((taps, conv_w), (tap_bias, conv_b), (norm, norm_w)):
                sp.dma_start(dst, src).then_inc(rows_here, 16)
            for dst, src in ((a_row, a_log), (d_row, d_skip), (dtb_row, dt_bias)):
                sp.dma_start(dst, src.partition_broadcast(P)).then_inc(rows_here, 16)
            sp.dma_start(w_out, out_w).then_inc(w_out_here, 16)
            load_again(0, 0)
            load_again(1, 1)
            load(2, 0)
            load(3, 1)
            with sp.Fori(0, TURNS - 2) as i:
                for par in range(2):
                    t = 2 * i + par
                    store(t)
                    load_again(t + 2, par)
                    scored.store(sp, t)
                    load(t + 4, par)
            for t in range(TILES - 4, TILES):
                store(t)
                if t < TILES - 2:
                    load_again(t + 2, t % 2)
                scored.store(sp, t)
            sp.wait_ge(stored, 16 * TILES)
            sp.wait_ge(scored.stored, 16 * TILES)

        @block.gpsimd
        def _(pool):
            for zeros in (state, mixed, b_rows, cin[0], cin[1]):
                nc.gpsimd.memset(zeros, 0.0).then_inc(cleared, 1)
            pool.wait_ge(rows_here, 96)
            pool.wait_ge(cleared, 5)

            def norm_power(n):
                pool.wait_ge(var_ready, n + 1)
                nc.gpsimd.tensor_tensor(rstd, var_eps, core.mhalf[:], ALU.pow).then_inc(rstd_ready, 1)

            def spread_steps(n):
                pool.wait_ge(parts_ready, 2 * n + 2)
                after(pool, sums_made, 2 * n)
                for part in range(2):
                    nc.gpsimd.tensor_tensor(steps[:, part].rearrange("p (h l) -> p h l", h=H),
                                            spread(da_parts[:, part], 2, BLK), spread(core.upto[:], 1, H), ALU.mult)\
                        .then_inc(steps_ready, 1)

            def mean_power(t):
                pool.wait_ge(mean_ready, t + 1)
                nc.gpsimd.tensor_tensor(rinv, mean_eps, core.mhalf[:], ALU.pow).then_inc(rinv_ready, 1)

            def step(t, before, front):
                pool.wait_ge(xs_ready, 2 * t + 2)
                after(pool, squares_ready, t)
                after(pool, ysum_ready, t)
                nc.gpsimd.tensor_tensor(by_head(xskip), by_head(xs), spread(d_row, 2, MHD), ALU.mult)\
                    .then_inc(xskip_ready, 1)
                if before:
                    mean_power(t - 1)
                pool.wait_ge(to_end_ready, t + 1)
                pool.wait_ge(xdt_ready, t + 1)
                after(pool, st_made, 4 * t)
                nc.gpsimd.tensor_tensor(by_head(xlast), by_head(xdt), spread(to_end, 2, MHD), ALU.mult)\
                    .then_inc(xlast_ready, 1)
                pool.wait_ge(carried_ready, t + 1)
                after(pool, yo_made, 2 * t)
                nc.gpsimd.tensor_tensor(by_head(state), by_head(state), spread(carried, 2, MHD), ALU.mult)\
                    .then_inc(decayed, 1)
                if front:
                    spread_steps(t + 1)
                if before:
                    scored.power(pool, t - 1)

            norm_power(0)
            spread_steps(0)
            norm_power(1)
            step(0, False, True)
            norm_power(2)
            step(1, True, True)
            norm_power(3)
            with pool.Fori(2, TILES - 2) as t:
                step(t, True, True)
                norm_power(t + 2)
            step(TILES - 2, True, True)
            step(TILES - 1, True, False)
            mean_power(TILES - 1)
            scored.power(pool, TILES - 1)

        @block.vector
        def _(dve):
            def layer_norm(link, n, par, turn):
                dve.wait_ge(x_loaded[par], 16 * turn + 16)
                link(nc.vector.bn_stats(st, x[:, par]))
                nc.vector.nop(nofuse=True)
                link(nc.vector.bn_aggr(mv, st))
                nc.vector.tensor_scalar(var_eps, mv[:, 1:2], EPS, None, ALU.add).then_inc(var_ready, 1)
                dve.wait_ge(rstd_ready, n + 1)
                after(dve, x_turned, n)
                nc.vector.tensor_scalar(xn, x[:, par], mv[:, 0:1], rstd, ALU.subtract, ALU.mult).then_inc(xn_ready, 1)

            def time_steps(link, n, par):
                dve.wait_ge(front_made, 5 * n + 1)
                link(nc.vector.tensor_tensor(u, bank[1][:, DT:DT + H], dtb_row, ALU.add))
                nc.vector.scalar_tensor_tensor(out=mag, in0=u, scalar=-1.0, in1=u, op0=ALU.mult, op1=ALU.max)\
                    .then_inc(mag_ready, 1)
                dve.wait_ge(e_mag_ready, n + 1)
                link(nc.vector.tensor_scalar(ratio, e_mag, 2.0, None, ALU.add))
                link(nc.vector.reciprocal(ratio, ratio))
                link(nc.vector.tensor_tensor(ratio, e_mag, ratio, ALU.mult))
                link(nc.vector.tensor_tensor(ratio2, ratio, ratio, ALU.mult))
                link(nc.vector.tensor_scalar(series, ratio2, 1.0 / 15, None, ALU.mult))
                for odd in (13, 11, 9, 7, 5, 3):
                    link(nc.vector.scalar_tensor_tensor(out=series, in0=series, scalar=1.0 / odd, in1=ratio2,
                                                        op0=ALU.add, op1=ALU.mult))
                link(nc.vector.scalar_tensor_tensor(out=series, in0=series, scalar=1.0, in1=ratio,
                                                    op0=ALU.add, op1=ALU.mult))
                link(nc.vector.tensor_scalar(u, u, 0.0, None, ALU.max))
                link(nc.vector.scalar_tensor_tensor(out=dt[:, par], in0=series, scalar=2.0, in1=u,
                                                    op0=ALU.mult, op1=ALU.add))
                nc.vector.tensor_tensor(da[:, par], dt[:, par], a_row, ALU.mult).then_inc(da_ready, 1)
                dve.wait_ge(da_ready, n + 1)
                after(dve, steps_ready, 2 * n)
                nc.vector.tensor_copy(da_parts[:, 0].bitcast(F32R), da[:, par]).then_inc(parts_ready, 1)
                dve.wait_ge(parts_ready, 2 * n + 1)
                nc.vector.tensor_tensor(da_parts[:, 1], da[:, par], da_parts[:, 0], ALU.subtract)\
                    .then_inc(parts_ready, 1)

            def halo_in(link, n, par, keep):
                after(dve, cin_ready, 3 * n)
                link(nc.vector.tensor_scalar(cin[par][:, :, 0:halo], cin[1 - par][:, :, P:P + halo], keep, None,
                                             ALU.mult))

            def convolve(link, n, par, part):
                dve.wait_ge(cin_ready, 3 * n + part + 1)
                dve.wait_ge(tap_ready, 3 * n + part + 1)
                for k in range(halo):
                    for c in range(parts[part].start, parts[part].stop):
                        last = nc.vector.scalar_tensor_tensor(out=conv[:, c], in0=cin[par][:, c, k:k + P],
                                                              scalar=taps[:, c, k:k + 1], in1=conv[:, c],
                                                              op0=ALU.mult, op1=ALU.add)
                    if k < halo - 1:
                        link(last)
                last.then_inc(conv_ready, 1)

            def first_factor(turn):
                return core.keep[:, bass.ds(turn % TURNS_PER_BATCH, 1)]

            def turned_out(t):
                dve.wait_ge(y_turned, t + 1)
                after(dve, out_made, t)
                for half in range(2):
                    part = slice(4 * half, 4 * half + 4)
                    last = nc.vector.tensor_tensor(yT[:, part], by_chunk(bank[5 + half][:]),
                                                   spread(norm[:, part], 2, P), ALU.mult)
                last.then_inc(yT_ready, 1)
                dve.wait_ge(squares_ready, t + 1)
                nc.vector.tensor_scalar(mean_eps, squares, 1.0 / INNER, EPS, ALU.mult, ALU.add).then_inc(mean_ready, 1)

            def put_out(t, par, turn):
                dve.wait_ge(out_made, t + 1)
                dve.wait_ge(rinv_ready, t + 1)
                dve.wait_ge(again_loaded[par], 16 * turn + 16)
                after(dve, stored, 16 * t)
                nc.vector.scalar_tensor_tensor(out=xo, in0=bank[7][:], scalar=rinv, in1=xres[:, par],
                                               op0=ALU.mult, op1=ALU.add).then_inc(added, 1)

            def step(link, t, turn, par, before, front):
                keep = first_factor(turn) if par == 0 else core.ones[:, 0:1]
                dve.wait_ge(sums_ready, t + 1)
                after(dve, decays_ready, 2 * t)
                link(nc.vector.tensor_scalar(ncs, sums[:, CS:CS + H], -1.0, None, ALU.mult))
                after(dve, to_end_ready, t)
                nc.vector.tensor_tensor(gap, sums[:, 3 * H:4 * H], ncs, ALU.add).then_inc(gap_ready, 1)
                if before:
                    turned_out(t - 1)
                dve.wait_ge(xs_ready, 2 * t + 2)
                after(dve, yd_made, 2 * t)
                after(dve, xlast_ready, t)
                nc.vector.tensor_tensor(by_head(xdt), by_head(xs), spread(dt[:, par], 2, MHD), ALU.mult)\
                    .then_inc(xdt_ready, 1)
                dve.wait_ge(exps_ready, t + 1)
                after(dve, decayed, t)
                nc.vector.tensor_scalar(carried, exps[:, H:2 * H], keep, None, ALU.mult).then_inc(carried_ready, 1)
                if front:
                    halo_in(link, t + 1, 1 - par, first_factor(turn + 1) if par else core.ones[:, 0:1])
                    time_steps(link, t + 1, 1 - par)
                    convolve(link, t + 1, 1 - par, 0)
                if before:
                    put_out(t - 1, 1 - par, turn if par else turn - 1)
                    dve.wait_ge(added, t)
                    scored.statistics(dve, link, xo)
                after(dve, yd_made, 2 * t)
                for g in range(2):
                    dve.wait_ge(decays_ready, 2 * t + g + 1)
                    heads = slice(g * H // 2, (g + 1) * H // 2)
                    for rows in blocks:
                        nc.vector.tensor_tensor(mixed[rows, heads, rows], decays[rows, g],
                                                spread(small[rows, BC:BC + BLK], 1, H // 2), ALU.mult)\
                            .then_inc(mixed_ready, 1)
                if before:
                    dve.wait_ge(xskip_ready, t + 1)
                    scored.normalise(dve, t - 1, xo)
                dve.wait_ge(decayed, t + 1)
                after(dve, y_turned, t)
                after(dve, squares_ready, t)
                for half in range(2):
                    part = slice(half * 512, half * 512 + 512)
                    heads = slice(half * H // 2, (half + 1) * H // 2)
                    first, second = state_banks[half]
                    dve.wait_ge(st_made, 4 * t + 2 * half + 1)
                    nc.vector.tensor_tensor(state_mid[:, part], state[:, part], bank[first][:], ALU.add)\
                        .then_inc(mid_ready, 1)
                    dve.wait_ge(mid_ready, 2 * t + half + 1)
                    link(nc.vector.tensor_tensor(by_head(state[:, part]), by_head(state_mid[:, part]),
                                                 spread(exps[:, 2 * H:3 * H][:, heads], 2, MHD), ALU.mult))
                    dve.wait_ge(st_made, 4 * t + 2 * half + 2)
                    nc.vector.tensor_tensor(state[:, part], state[:, part], bank[second][:], ALU.add)\
                        .then_inc(state_ready, 1)
                if front:
                    convolve(link, t + 1, 1 - par, 1)
                    convolve(link, t + 1, 1 - par, 2)
                for half, b in ((0, 3), (1, 4)):
                    part = slice(half * 512, half * 512 + 512)
                    heads = slice(half * H // 2, (half + 1) * H // 2)
                    dve.wait_ge(yo_made, 2 * t + half + 1)
                    nc.vector.tensor_tensor(by_head(ysum[:, part]), by_head(bank[b][:]),
                                            spread(exps[:, heads], 2, MHD), ALU.mult).then_inc(yo_read, 1)
                dve.wait_ge(yd_made, 2 * t + 2)
                dve.wait_ge(yo_read, 2 * t + 2)
                for half in range(2):
                    part = slice(half * 512, half * 512 + 512)
                    last = nc.vector.tensor_tensor(ysum[:, part], ysum[:, part], bank[5 + half][:], ALU.add)
                link(last)
                dve.wait_ge(xskip_ready, t + 1)
                nc.vector.tensor_tensor(ysum, ysum, xskip, ALU.add).then_inc(ysum_ready, 1)
                dve.wait_ge(ysum_ready, t + 1)
                dve.wait_ge(z_ready, 2 * t + 2)
                nc.vector.tensor_tensor(y, ysum, zs[:, par], ALU.mult).then_inc(y_ready, 1)
                if before:
                    scored.logits_out(dve, t - 1, small)

            dve.wait_ge(cleared, 5)
            dve.wait_ge(rows_here, 96)
            dve.wait_ge(a_exp, 1)
            nc.vector.tensor_scalar(a_row, a_row, -1.0, None, ALU.mult).then_inc(a_ready, 1)
            dve.wait_ge(a_ready, 1)
            link = Chain(dve, chains[0])
            layer_norm(link, 0, 0, 0)
            halo_in(link, 0, 0, core.keep[:, 0:1])
            time_steps(link, 0, 0)
            layer_norm(link, 1, 1, 0)
            for part in range(3):
                convolve(link, 0, 0, part)
            step(link, 0, 0, 0, False, True)
            layer_norm(link, 2, 0, 1)
            per_step = 30
            link = Chain(dve, chains[1], 0, per_step)
            step(link, 1, 0, 1, True, True)
            layer_norm(link, 3, 1, 1)
            link.end()
            with dve.Fori(1, TURNS - 1) as i:
                for par in range(2):
                    link = Chain(dve, chains[1], 2 * i + par - 1, per_step)
                    step(link, 2 * i + par, i, par, True, True)
                    layer_norm(link, 2 * i + par + 2, par, i + 1)
                    link.end()
            link = Chain(dve, chains[2])
            step(link, TILES - 2, TURNS - 1, 0, True, True)
            step(link, TILES - 1, TURNS - 1, 1, True, False)
            turned_out(TILES - 1)
            put_out(TILES - 1, 1, TURNS - 1)
            dve.wait_ge(added, TILES)
            scored.statistics(dve, link, xo)
            scored.normalise(dve, TILES - 1, xo)
            scored.logits_out(dve, TILES - 1, small)

        @block.scalar
        def _(act):
            def rows_out(n):
                act.wait_ge(x_turned, n + 1)
                after(act, front_made, 5 * n)
                nc.scalar.activation(xnT, by_chunk(bank[0][:]), ACT.Copy).then_inc(xnT_ready, 1)

            def conv_in(n, par, part):
                act.wait_ge(front_made, 5 * n + part + 1)
                after(act, conv_ready, 3 * n)
                after(act, xc_ready, 3 * n)
                c = parts[part]
                nc.scalar.activation(cin[par][:, c, halo:halo + P],
                                     by_chunk(part_banks[part][:, 0:(c.stop - c.start) * P]), ACT.Copy)\
                    .then_inc(cin_ready, 1)
                act.wait_ge(cin_ready, 3 * n + part + 1)
                for c in range(parts[part].start, parts[part].stop):
                    last = nc.scalar.activation(conv[:, c], cin[par][:, c, halo:halo + P], ACT.Copy,
                                                scale=taps[:, c, halo:halo + 1])
                last.then_inc(tap_ready, 1)

            def gate(n, par):
                for half in range(2):
                    act.wait_ge(front_made, 5 * n + 4 + half)
                    after(act, y_ready, n - 1)
                    nc.scalar.activation(zs[:, par, half * 512:half * 512 + 512], bank[half][:], ACT.Silu)\
                        .then_inc(z_ready, 1)

            def conv_out(n, par, part):
                act.wait_ge(conv_ready, 3 * n + part + 1)
                after(act, yo_made, 2 * n - 2)
                for c in range(parts[part].start, parts[part].stop):
                    last = nc.scalar.activation(xc[:, par, c], conv[:, c], ACT.Silu, bias=tap_bias[:, c:c + 1])
                last.then_inc(xc_ready, 1)

            def e_mags(n):
                act.wait_ge(mag_ready, n + 1)
                after(act, da_ready, n)
                nc.scalar.activation(e_mag, mag, ACT.Exp, scale=-1.0).then_inc(e_mag_ready, 1)

            def decay(t, g):
                act.wait_ge(sums_made, 2 * t + g + 1)
                if g == 0:
                    after(act, mixed_ready, 4 * t)
                for r in range(H // 2):
                    h = H // 2 * g + r
                    last = nc.scalar.activation(decays[:, g, r], bank[3 + g][:, r * BLK:(r + 1) * BLK], ACT.Exp,
                                                bias=ncs[:, h:h + 1])
                last.then_inc(decays_ready, 1)

            def squares_of(t):
                act.wait_ge(y_ready, t + 1)
                after(act, mean_ready, t)
                nc.scalar.activation(xskip, y, ACT.Square, accum_out=squares).then_inc(squares_ready, 1)

            def step(t, par, before, front):
                if front:
                    rows_out(t + 1)
                act.wait_ge(small_made, t + 1)
                after(act, gap_ready, t)
                nc.scalar.activation(sums, small[:, CS:CS + 4 * H], ACT.Copy).then_inc(sums_ready, 1)
                after(act, yo_read, 2 * t)
                nc.scalar.activation(exps, small[:, CS:CS + 3 * H], ACT.Exp).then_inc(exps_ready, 1)
                act.wait_ge(xs_turned, t + 1)
                after(act, xdt_ready, t)
                after(act, xskip_ready, t)
                after(act, scored.turned, t - 1)
                after(act, scored.made, t - 1)
                after(act, scored.stored, 16 * (t - 1))
                for half in range(2):
                    nc.scalar.activation(xs[:, half * 512:half * 512 + 512], bank[3 + half][:], ACT.Copy)\
                        .then_inc(xs_ready, 1)
                after(act, st_made, 4 * t)
                for b, rows in enumerate(blocks):
                    nc.scalar.activation(b_rows[rows, b], small[rows, BROWS:BROWS + P], ACT.Copy).then_inc(b_ready, 1)
                act.wait_ge(gap_ready, t + 1)
                after(act, xlast_ready, t)
                nc.scalar.activation(to_end, gap, ACT.Exp).then_inc(to_end_ready, 1)
                if before:
                    squares_of(t - 1)
                if front:
                    e_mags(t + 1)
                    conv_in(t + 1, 1 - par, 0)
                decay(t, 0)
                decay(t, 1)
                if front:
                    conv_in(t + 1, 1 - par, 1)
                    conv_in(t + 1, 1 - par, 2)
                    conv_out(t + 1, 1 - par, 0)
                    conv_out(t + 1, 1 - par, 1)
                if before:
                    scored.turned_out(act, t - 1, small)
                if front:
                    conv_out(t + 1, 1 - par, 2)
                    gate(t + 1, 1 - par)

            act.wait_ge(rows_here, 96)
            act.wait_ge(cleared, 5)
            nc.scalar.activation(a_row, a_row, ACT.Exp).then_inc(a_exp, 1)
            rows_out(0)
            e_mags(0)
            for part in range(3):
                conv_in(0, 0, part)
            for part in range(3):
                conv_out(0, 0, part)
            gate(0, 0)
            for par in range(2):
                step(par, par, par > 0, True)
            with act.Fori(1, TURNS - 1) as i:
                for par in range(2):
                    step(2 * i + par, par, True, True)
            step(TILES - 2, 0, True, True)
            step(TILES - 1, 1, True, False)
            squares_of(TILES - 1)
            scored.turned_out(act, TILES - 1, small)

        @block.tensor
        def _(pe):
            def turn_rows(n):
                pe.wait_ge(xn_ready, n + 1)
                after(pe, z_ready, 2 * n)
                for k in range(KD):
                    last = nc.tensor.transpose(bank[0][:, k * P:k * P + P], xn[:, k * P:k * P + P], core.ident[:])
                last.then_inc(x_turned, 1)

            def channels(n, part):
                if part == 0:
                    pe.wait_ge(xnT_ready, n + 1)
                if part == 2:
                    pe.wait_ge(cin_ready, 3 * n + 1)
                    pe.wait_ge(mag_ready, n + 1)
                for j, c in enumerate(range(parts[part].start, parts[part].stop)):
                    at = INNER + c * P
                    for k in range(KD):
                        last = nc.tensor.matmul(part_banks[part][:, j * P:j * P + P],
                                                w_in[:, k, at:at + P], xnT[:, k], start=(k == 0), stop=(k == KD - 1))
                if part == 0:
                    for k in range(KD):
                        last = nc.tensor.matmul(bank[1][:, DT:DT + H], xnT[:, k], w_in[:, k, INNER + XBC:WIN_COLS],
                                                start=(k == 0), stop=(k == KD - 1))
                last.then_inc(front_made, 1)

            def gate_rows(n, half):
                pe.wait_ge(cin_ready, 3 * n + 2 + half)
                for k in range(KD):
                    last = nc.tensor.matmul(bank[half][:], xnT[:, k], w_in[:, k, half * 512:half * 512 + 512],
                                            start=(k == 0), stop=(k == KD - 1))
                last.then_inc(front_made, 1)

            def running_sums(g):
                b = bank[3 + g]
                nc.tensor.matmul(b[:], core.identb[:], core.ssd_mask[:].rearrange("p a b -> p (a b)"),
                                 start=True, stop=False)
                for part in range(2):
                    last = nc.tensor.matmul(b[:], core.own_r[:],
                                            steps[:, part, g * 512:g * 512 + 512],
                                            start=False, stop=(part == 1))
                last.then_inc(sums_made, 1)

            def scan_rows(t, par):
                B, C = xc[:, par, KY], xc[:, par, KY + 1]
                pe.wait_ge(xc_ready, 3 * t + 1)
                pe.wait_ge(da_ready, t + 1)
                after(pe, mixed_ready, 4 * t)
                after(pe, b_ready, 2 * t)
                after(pe, scored.ready, t - 1)
                nc.tensor.transpose(small[:, BROWS:BROWS + P], B, core.ident[:])
                for j, which in enumerate((core.upto_own[:], core.in_block[:, 0], core.in_block[:, 1], core.own[:])):
                    nc.tensor.matmul(small[:, CS + j * H:CS + (j + 1) * H], which, da[:, par], start=True, stop=True)
                for rows in blocks:
                    last = nc.tensor.matmul(small[rows, BC:BC + BLK], B[:, rows], C[:, rows], start=True, stop=True)
                last.then_inc(small_made, 1)
                pe.wait_ge(xc_ready, 3 * t + 3)
                after(pe, yo_read, 2 * t)
                for k in range(KY):
                    last = nc.tensor.transpose(bank[3 + k // 4][:, (k % 4) * P:(k % 4 + 1) * P], xc[:, par, k],
                                               core.ident[:])
                last.then_inc(xs_turned, 1)

            def turn_y(t):
                pe.wait_ge(y_ready, t + 1)
                for k in range(KY):
                    last = nc.tensor.transpose(bank[5 + k // 4][:, (k % 4) * P:(k % 4 + 1) * P],
                                               y[:, k * P:k * P + P], core.ident[:])
                last.then_inc(y_turned, 1)

            def project_out(t):
                pe.wait_ge(yT_ready, t + 1)
                for k in range(KY):
                    last = nc.tensor.matmul(bank[7][:], yT[:, k], w_out[:, k], start=(k == 0), stop=(k == KY - 1))
                last.then_inc(out_made, 1)

            def block_states(t):
                pe.wait_ge(xlast_ready, t + 1)
                pe.wait_ge(b_ready, 2 * t + 2)
                for half in range(2):
                    for b in range(2):
                        if (half, b) == (0, 0):
                            after(pe, added, t)
                        if (half, b) == (0, 1):
                            pe.wait_ge(decays_ready, 2 * t + 1)
                        if (half, b) == (1, 0):
                            pe.wait_ge(decays_ready, 2 * t + 2)
                        if (half, b) == (1, 1):
                            pe.wait_ge(mid_ready, 2 * t + 1)
                        nc.tensor.matmul(bank[state_banks[half][b]][:], b_rows[:, b],
                                         xlast[:, half * 512:half * 512 + 512], start=True, stop=True)\
                            .then_inc(st_made, 1)

            def own_rows(t, g):
                pe.wait_ge(mixed_ready, 4 * t + 2 * g + 2)
                if g == 0:
                    pe.wait_ge(xdt_ready, t + 1)
                for r in range(H // 2):
                    h = H // 2 * g + r
                    last = nc.tensor.matmul(bank[5 + g][:, r * MHD:(r + 1) * MHD], mixed[:, h],
                                            xdt[:, h * MHD:h * MHD + MHD], start=True, stop=True)
                last.then_inc(yd_made, 1)

            def from_states(t, par):
                C = xc[:, par, KY + 1]
                for half, b in ((0, 3), (1, 4)):
                    pe.wait_ge(state_ready, 2 * t + half + 1)
                    for rows, held in zip(blocks, (state_mid, state)):
                        last = nc.tensor.matmul(bank[b][rows, :], C[:, rows], held[:, half * 512:half * 512 + 512],
                                                start=True, stop=True)
                    last.then_inc(yo_made, 1)

            def step(t, par, before, front):
                if front:
                    turn_rows(t + 1)
                scan_rows(t, par)
                if before:
                    turn_y(t - 1)
                if front:
                    channels(t + 1, 0)
                if before:
                    project_out(t - 1)
                pe.wait_ge(xs_ready, 2 * t + 2)
                pe.wait_ge(steps_ready, 2 * t + 2)
                running_sums(0)
                running_sums(1)
                if front:
                    channels(t + 1, 1)
                block_states(t)
                if front:
                    channels(t + 1, 2)
                own_rows(t, 0)
                own_rows(t, 1)
                if before:
                    scored.turn(pe, t - 1, small)
                from_states(t, par)
                if front:
                    gate_rows(t + 1, 0)
                if before:
                    scored.product(pe, t - 1, small)
                if front:
                    gate_rows(t + 1, 1)

            turn_rows(0)
            for part in range(3):
                channels(0, part)
            gate_rows(0, 0)
            gate_rows(0, 1)
            pe.wait_ge(w_out_here, 16)
            pe.wait_ge(cleared, 5)
            for par in range(2):
                step(par, par, par > 0, True)
            with pe.Fori(1, TURNS - 1) as i:
                for par in range(2):
                    step(2 * i + par, par, True, True)
            step(TILES - 2, 0, True, True)
            step(TILES - 1, 1, True, False)
            turn_y(TILES - 1)
            project_out(TILES - 1)
            pe.wait_ge(scored.ready, TILES - 1)
            scored.turn(pe, TILES - 1, small)
            scored.product(pe, TILES - 1, small)


def hybrid_block(nc, x, w_qkv, w_out, in_w, conv_w, conv_b, a_log, d_skip, dt_bias, norm_w, out_w, gate, w1, w2, w2_tail, out):
    def tiles(rows):
        return rows[0:ROWS].rearrange("(t p) d -> t p d", p=P)

    with ExitStack() as ctx:
        core = Core(nc, ctx)
        mid = nc.dram_tensor("mid_rows", (ROWS + SPARE, D), F32).ap()
        xn_rows = nc.dram_tensor("normalised_rows", (ROWS + SPARE, D), F32).ap()
        weights = (w1, w2, w2_tail)
        make_constants(core, [rows[ROWS:ROWS + SPARE] for rows in (mid, xn_rows, out)])
        attention(core, tiles(x), tiles(mid), xn_rows, w_qkv, w_out, gate, *weights)
        experts(core, "moe_a", mid, xn_rows, *weights, range(0), range(core.att_experts, EXPERTS), in_w)
        mamba(core, tiles(mid), tiles(out), xn_rows, out_w, conv_w, conv_b, a_log, d_skip, dt_bias, norm_w)
        experts(core, "moe_b", out, xn_rows, *weights, range(core.mamba_experts, EXPERTS), range(EXPERTS), None)


def _by_partition(w):
    import numpy as _np
    return _np.ascontiguousarray(w.T.reshape(-1, 128, w.shape[0]).transpose(1, 0, 2))


def kernel(**inputs):
    import numpy as _np
    import concourse.bacc as _bacc
    from concourse import mybir as _mybir
    from concourse.bass_utils import run_bass_kernel_spmd as _run

    a = {name: _np.asarray(v) for name, v in inputs.items()}
    w1, w2 = a["L0_ffn_w1"], a["L0_ffn_w2"]
    n_e, two_i, d = w1.shape
    inner = w2.shape[2]
    whole = inner // 128 * 128
    w1 = w1.transpose(2, 0, 1).reshape(d // 128, 128, n_e, two_i).transpose(1, 2, 0, 3).reshape(128, n_e, -1)
    w2 = w2.transpose(2, 0, 1)
    taps = a["L0_attn_b_conv_w"].shape[2]
    laid = {
        "x": a["L0_attn_a_x"].reshape(-1, d),
        "w_qkv": _by_partition(a["L0_attn_a_w_qkv"]),
        "w_out": _by_partition(a["L0_attn_a_w_out"]),
        "in_w": _by_partition(a["L0_attn_b_in_proj_w"]),
        "conv_w": a["L0_attn_b_conv_w"].reshape(-1, 128, taps).transpose(1, 0, 2),
        "conv_b": a["L0_attn_b_conv_b"].reshape(-1, 128).T,
        "a_log": a["L0_attn_b_A_log"],
        "d_skip": a["L0_attn_b_D"],
        "dt_bias": a["L0_attn_b_dt_bias"],
        "norm_w": a["L0_attn_b_norm_w"].reshape(-1, 128).T,
        "out_w": _by_partition(a["L0_attn_b_out_proj_w"]),
        "gate": _by_partition(a["L0_ffn_gate_w"]),
        "w1": w1,
        "w2": w2[:whole].reshape(whole // 128, 128, n_e, d).transpose(1, 2, 0, 3),
        "w2_tail": w2[whole:],
    }
    nc = _bacc.Bacc("TRN2", target_bir_lowering=False, num_devices=1)
    arrays, args = {}, []
    for name, v in laid.items():
        v = _np.ascontiguousarray(v)
        arrays[f"in_{name}_dram"] = v
        args.append(nc.dram_tensor(f"in_{name}_dram", v.shape, _mybir.dt.from_np(v.dtype), kind="ExternalInput").ap())
    rows = laid["x"].shape[0]
    args.append(nc.dram_tensor("out_dram", (rows + 128, d), _mybir.dt.float32, kind="ExternalOutput").ap())
    hybrid_block(nc, *args)
    r = _run(nc, [arrays], core_ids=[0])
    return r.results[0]["out_dram"][:rows].reshape(a["L0_attn_a_x"].shape)
```
